# Optimizing a Trainium2 kernel written in Bass

```python
import numpy as np
import jax
import jax.numpy as jnp

def _softmax(x, axis=-1):
    return jax.nn.softmax(x, axis=axis)

def _gelu(x):
    return jax.nn.gelu(x, approximate=True)

def _silu(x):
    return jax.nn.silu(x)

def _sigmoid(x):
    return jax.nn.sigmoid(x)

def _layernorm(x, axis=-1, eps=1e-05):
    m = jnp.mean(x, axis=axis, keepdims=True)
    v = jnp.var(x, axis=axis, keepdims=True)
    return (x - m) / jnp.sqrt(v + eps)

def _scatter_add(tgt, idx, src, axis=0):
    return tgt.at[idx].add(src)

def _segment_sum(src, seg, n):
    return jax.ops.segment_sum(src, seg, n)
kernel_name = 'mk_flamingo_gated_d2_seqx_r8_e90938'

def setup_inputs(seed: int=0):
    np.random.seed(seed)
    _w = jnp.asarray

    def _rec_inputs():
        import jax
        import jax.numpy as jnp
        _rk = jax.random.key(seed)
        x = 7.22e-05 + 1 * jax.random.normal(jax.random.fold_in(_rk, 1), (32, 128, 128), jnp.float32)
        _lenS = 128 - jax.random.randint(jax.random.fold_in(_rk, 7), (32,), 0, max(1, 128 // 4) + 1, jnp.int32)
        _lenS2 = 128 - jax.random.randint(jax.random.fold_in(_rk, 8), (32,), 0, max(1, 128 // 4) + 1, jnp.int32)
        _ctx_1024P = jax.random.normal(jax.random.fold_in(_rk, 11), (32, 16, 128), jnp.float32)
        _ctx_1024c = jax.random.dirichlet(jax.random.fold_in(_rk, 511), 0.3 * jnp.ones((16,), jnp.float32), (32, 128))
        _ctx_1024t = jnp.einsum('bsk,bkd->bsd', _ctx_1024c, _ctx_1024P)
        _ctx_1024t = _ctx_1024t * jax.lax.rsqrt(jnp.mean(jnp.square(_ctx_1024t)) + 1e-12) * 0.953939
        ctx_1024 = -0.000514642 + 1.00011 * (_ctx_1024t + 0.3 * jax.random.normal(jax.random.fold_in(_rk, 611), (32, 128, 128), jnp.float32))
        _g = jax.random.normal(jax.random.fold_in(_rk, 9001), (2, 2), jnp.float32)
        _g = jnp.sign(_g) * jnp.maximum(jnp.abs(_g), 1.0) + (_g == 0) * 1.0
        g_xattn = _g[0]
        g_ffn = _g[1]
        return (x, ctx_1024, g_xattn, g_ffn)
    x, ctx_1024, g_xattn, g_ffn = _rec_inputs()

    def _L0_xattn_setup():
        import jax, jax.numpy as jnp
        import numpy as np
        B, L_ENC, L_DEC, D = (16, 64, 128, 128)
        key = jax.random.key(seed)
        k1, k2, k3, k4, k5, k6 = jax.random.split(key, 6)
        encoder_hc = jax.random.normal(k1, (B, L_ENC, D), dtype=jnp.float32)
        decoder_hq = jax.random.normal(k2, (B, L_DEC, D), dtype=jnp.float32)
        w_sim = jax.random.normal(k3, (3 * D,), dtype=jnp.float32) * 0.02
        b_sim = jax.random.normal(k4, (1,), dtype=jnp.float32) * 0.02
        W_qv = jax.random.normal(k5, (4 * D, D), dtype=jnp.float32) * 0.02
        b_qv = jax.random.normal(k6, (D,), dtype=jnp.float32) * 0.02
        return {'encoder_hc': encoder_hc, 'decoder_hq': decoder_hq, 'w_sim': w_sim, 'b_sim': b_sim, 'W_qv': W_qv, 'b_qv': b_qv}
    _L0_xattn_all = _L0_xattn_setup()
    _L0_xattn_in = {k: v for k, v in _L0_xattn_all.items() if k in ('w_sim', 'b_sim', 'W_qv', 'b_qv')}
    del _L0_xattn_all

    def _L0_ffn_setup():
        import jax, jax.numpy as jnp
        import numpy as np
        E, K, NG, TG = (64, 8, 8, 4)
        CAP = 128
        SCALE = 2.5

        def _route(x_flat, gate_weight, e_bias):
            T = x_flat.shape[0]
            logits = x_flat.astype(jnp.float32) @ gate_weight.astype(jnp.float32).T
            scores = jax.nn.sigmoid(logits)
            sfc = scores + e_bias[None, :]
            group_scores = jax.lax.top_k(sfc.reshape(T, NG, E // NG), 2)[0].sum(-1)
            _, gidx = jax.lax.top_k(group_scores, TG)
            gmask = jnp.zeros((T, NG), jnp.float32).at[jnp.arange(T)[:, None], gidx].set(1.0)
            smask = jnp.repeat(gmask, E // NG, axis=1)
            tmp = jnp.where(smask > 0, sfc, 0.0)
            _, topk_idx = jax.lax.top_k(tmp, K)
            topk_w = jnp.take_along_axis(scores, topk_idx, axis=1)
            topk_w = topk_w / (topk_w.sum(-1, keepdims=True) + 1e-20)
            return (topk_idx, topk_w * SCALE)

        def _moe_forward(hidden_states, gate_weight, e_bias, w1, w2, w3, shared_gate, shared_up, shared_down):
            B, S, H = hidden_states.shape
            T = B * S
            x = hidden_states.reshape(T, H)
            topk_idx, topk_w = _route(x, gate_weight, e_bias)
            Sk = T * K
            flat_e = topk_idx.reshape(-1)
            order = jnp.argsort(flat_e)
            sorted_e = flat_e[order]
            counts = jax.ops.segment_sum(jnp.ones((Sk,), jnp.int32), flat_e, num_segments=E)
            offsets = jnp.cumsum(counts) - counts
            pos = jnp.arange(Sk) - offsets[sorted_e]
            tok_sorted = x[order // K]
            xe = jnp.zeros((E, CAP, H), x.dtype).at[sorted_e, pos].set(tok_sorted, mode='drop')
            h = jax.nn.silu(jnp.einsum('ech,efh->ecf', xe, w1)) * jnp.einsum('ech,efh->ecf', xe, w3)
            ye = jnp.einsum('ecf,ehf->ech', h, w2)
            pos_c = jnp.minimum(pos, CAP - 1)
            vals = ye[sorted_e, pos_c]
            vals = jnp.where((pos < CAP)[:, None], vals, 0.0)
            flat_w = topk_w.reshape(-1)[order].astype(vals.dtype)
            flat_t = (jnp.arange(Sk) // K)[order]
            out = jax.ops.segment_sum(vals * flat_w[:, None], flat_t, num_segments=T)
            shared = jax.nn.silu(x @ shared_gate.T) * (x @ shared_up.T) @ shared_down.T
            return (out + shared).reshape(B, S, H)
        key = jax.random.key(seed)
        ks = jax.random.split(key, 9)
        B, S, H, F = (1, 256, 128, 64)
        bound = 1.0 / 32.0
        return {'hidden_states': jax.random.normal(ks[0], (B, S, H), jnp.float32), 'gate_weight': jax.random.uniform(ks[1], (E, H), jnp.float32, -bound, bound), 'e_bias': jnp.zeros((E,), jnp.float32), 'w1': jax.random.normal(ks[2], (E, F, H), jnp.float32) * 0.02, 'w2': jax.random.normal(ks[3], (E, H, F), jnp.float32) * 0.02, 'w3': jax.random.normal(ks[4], (E, F, H), jnp.float32) * 0.02, 'shared_gate': jax.random.normal(ks[5], (2 * F, H), jnp.float32) * 0.02, 'shared_up': jax.random.normal(ks[6], (2 * F, H), jnp.float32) * 0.02, 'shared_down': jax.random.normal(ks[7], (H, 2 * F), jnp.float32) * 0.02}
    _L0_ffn_all = _L0_ffn_setup()
    _L0_ffn_in = {k: v for k, v in _L0_ffn_all.items() if k in ('gate_weight', 'e_bias', 'w1', 'w2', 'w3', 'shared_gate', 'shared_up', 'shared_down')}
    del _L0_ffn_all

    def _L1_xattn_setup():
        import jax, jax.numpy as jnp
        import numpy as np
        D_MODEL = 128
        NHEAD = 16
        HEAD_DIM = D_MODEL // NHEAD
        key = jax.random.key(seed)
        ks = jax.random.split(key, 11)
        B, S, D = (4, 256, D_MODEL)
        scale = 1.0 / np.sqrt(D)
        inp = {'q': jax.random.normal(ks[0], (B, S, D), jnp.float32), 'k': jax.random.normal(ks[1], (B, S, D), jnp.float32), 'v': jax.random.normal(ks[2], (B, S, D), jnp.float32), 'Wq': jax.random.normal(ks[3], (D, D), jnp.float32) * scale, 'bq': jnp.zeros((D,), jnp.float32), 'Wk': jax.random.normal(ks[4], (D, D), jnp.float32) * scale, 'bk': jnp.zeros((D,), jnp.float32), 'Wv': jax.random.normal(ks[5], (D, D), jnp.float32) * scale, 'bv': jnp.zeros((D,), jnp.float32), 'Wo': jax.random.normal(ks[6], (D, D), jnp.float32) * scale, 'bo': jnp.zeros((D,), jnp.float32)}
        return inp
    _L1_xattn_all = _L1_xattn_setup()
    _L1_xattn_in = {k: v for k, v in _L1_xattn_all.items() if k in ('Wq', 'bq', 'Wk', 'bk', 'Wv', 'bv', 'Wo', 'bo')}
    del _L1_xattn_all

    def _L1_ffn_setup():
        import jax, jax.numpy as jnp
        import numpy as np
        D_MODEL = 128
        H_SHARED = 256
        H_ROUTED = 128
        N_EXPERTS = 8
        TOP_K = 2
        key = jax.random.key(seed)
        ks = jax.random.split(key, 8)
        B, T = (2, 256)
        sc_d = 1.0 / np.sqrt(D_MODEL)
        sc_hs = 1.0 / np.sqrt(H_SHARED)
        sc_hr = 1.0 / np.sqrt(H_ROUTED)
        return {'x': jax.random.normal(ks[0], (B, T, D_MODEL), dtype=jnp.float32), 'router_w': jax.random.normal(ks[1], (N_EXPERTS, D_MODEL), dtype=jnp.float32) * sc_d, 'router_bias': jnp.zeros((N_EXPERTS,), dtype=jnp.float32), 'sw1': jax.random.normal(ks[2], (D_MODEL, H_SHARED), dtype=jnp.float32) * sc_d, 'sw3': jax.random.normal(ks[3], (D_MODEL, H_SHARED), dtype=jnp.float32) * sc_d, 'sw2': jax.random.normal(ks[4], (H_SHARED, D_MODEL), dtype=jnp.float32) * sc_hs, 'ew1': jax.random.normal(ks[5], (N_EXPERTS, D_MODEL, H_ROUTED), dtype=jnp.float32) * sc_d, 'ew2': jax.random.normal(ks[6], (N_EXPERTS, H_ROUTED, D_MODEL), dtype=jnp.float32) * sc_hr}
    _L1_ffn_all = _L1_ffn_setup()
    _L1_ffn_in = {k: v for k, v in _L1_ffn_all.items() if k in ('router_w', 'router_bias', 'sw1', 'sw3', 'sw2', 'ew1', 'ew2')}
    del _L1_ffn_all
    return {'x': x, 'ctx_1024': ctx_1024, 'g_xattn': g_xattn, 'g_ffn': g_ffn, 'L0_xattn_w_sim': _L0_xattn_in['w_sim'], 'L0_xattn_b_sim': _L0_xattn_in['b_sim'], 'L0_xattn_W_qv': _L0_xattn_in['W_qv'], 'L0_xattn_b_qv': _L0_xattn_in['b_qv'], 'L0_ffn_gate_weight': _L0_ffn_in['gate_weight'], 'L0_ffn_e_bias': _L0_ffn_in['e_bias'], 'L0_ffn_w1': _L0_ffn_in['w1'], 'L0_ffn_w2': _L0_ffn_in['w2'], 'L0_ffn_w3': _L0_ffn_in['w3'], 'L0_ffn_shared_gate': _L0_ffn_in['shared_gate'], 'L0_ffn_shared_up': _L0_ffn_in['shared_up'], 'L0_ffn_shared_down': _L0_ffn_in['shared_down'], 'L1_xattn_Wq': _L1_xattn_in['Wq'], 'L1_xattn_bq': _L1_xattn_in['bq'], 'L1_xattn_Wk': _L1_xattn_in['Wk'], 'L1_xattn_bk': _L1_xattn_in['bk'], 'L1_xattn_Wv': _L1_xattn_in['Wv'], 'L1_xattn_bv': _L1_xattn_in['bv'], 'L1_xattn_Wo': _L1_xattn_in['Wo'], 'L1_xattn_bo': _L1_xattn_in['bo'], 'L1_ffn_router_w': _L1_ffn_in['router_w'], 'L1_ffn_router_bias': _L1_ffn_in['router_bias'], 'L1_ffn_sw1': _L1_ffn_in['sw1'], 'L1_ffn_sw3': _L1_ffn_in['sw3'], 'L1_ffn_sw2': _L1_ffn_in['sw2'], 'L1_ffn_ew1': _L1_ffn_in['ew1'], 'L1_ffn_ew2': _L1_ffn_in['ew2']}

def reference(x, ctx_1024, g_xattn, g_ffn, L0_xattn_w_sim, L0_xattn_b_sim, L0_xattn_W_qv, L0_xattn_b_qv, L0_ffn_gate_weight, L0_ffn_e_bias, L0_ffn_w1, L0_ffn_w2, L0_ffn_w3, L0_ffn_shared_gate, L0_ffn_shared_up, L0_ffn_shared_down, L1_xattn_Wq, L1_xattn_bq, L1_xattn_Wk, L1_xattn_bk, L1_xattn_Wv, L1_xattn_bv, L1_xattn_Wo, L1_xattn_bo, L1_ffn_router_w, L1_ffn_router_bias, L1_ffn_sw1, L1_ffn_sw3, L1_ffn_sw2, L1_ffn_ew1, L1_ffn_ew2):
    import jax
    import jax.numpy as jnp

    def _L0_xattn_ref(encoder_hc, decoder_hq, w_sim, b_sim, W_qv, b_qv):
        import jax, jax.numpy as jnp
        import numpy as np
        B, L_ENC, L_DEC, D = (16, 64, 128, 128)
        d = encoder_hc.shape[-1]
        w1, w2, w3 = (w_sim[:d], w_sim[d:2 * d], w_sim[2 * d:])
        Sim = (encoder_hc @ w1)[:, :, None] + (decoder_hq @ w2)[:, None, :] + jnp.einsum('bid,bjd->bij', encoder_hc * w3, decoder_hq) + b_sim[0]
        A = jax.nn.softmax(Sim, axis=2)
        hq_hat = jnp.einsum('bij,bjd->bid', A, decoder_hq)
        Batt = jax.nn.softmax(jnp.max(Sim, axis=2), axis=1)
        hc_bar = jnp.einsum('bi,bid->bd', Batt, encoder_hc)[:, None, :]
        hc_hat = jnp.broadcast_to(hc_bar, encoder_hc.shape)
        feats = jnp.concatenate([encoder_hc, hq_hat, encoder_hc * hq_hat, encoder_hc * hc_hat], axis=-1)
        hcq = feats @ W_qv + b_qv
        return hcq

    def _L0_ffn_ref(hidden_states, gate_weight, e_bias, w1, w2, w3, shared_gate, shared_up, shared_down):
        import jax, jax.numpy as jnp
        import numpy as np
        E, K, NG, TG = (64, 8, 8, 4)
        CAP = 128
        SCALE = 2.5

        def _route(x_flat, gate_weight, e_bias):
            T = x_flat.shape[0]
            logits = x_flat.astype(jnp.float32) @ gate_weight.astype(jnp.float32).T
            scores = jax.nn.sigmoid(logits)
            sfc = scores + e_bias[None, :]
            group_scores = jax.lax.top_k(sfc.reshape(T, NG, E // NG), 2)[0].sum(-1)
            _, gidx = jax.lax.top_k(group_scores, TG)
            gmask = jnp.zeros((T, NG), jnp.float32).at[jnp.arange(T)[:, None], gidx].set(1.0)
            smask = jnp.repeat(gmask, E // NG, axis=1)
            tmp = jnp.where(smask > 0, sfc, 0.0)
            _, topk_idx = jax.lax.top_k(tmp, K)
            topk_w = jnp.take_along_axis(scores, topk_idx, axis=1)
            topk_w = topk_w / (topk_w.sum(-1, keepdims=True) + 1e-20)
            return (topk_idx, topk_w * SCALE)

        def _moe_forward(hidden_states, gate_weight, e_bias, w1, w2, w3, shared_gate, shared_up, shared_down):
            B, S, H = hidden_states.shape
            T = B * S
            x = hidden_states.reshape(T, H)
            topk_idx, topk_w = _route(x, gate_weight, e_bias)
            Sk = T * K
            flat_e = topk_idx.reshape(-1)
            order = jnp.argsort(flat_e)
            sorted_e = flat_e[order]
            counts = jax.ops.segment_sum(jnp.ones((Sk,), jnp.int32), flat_e, num_segments=E)
            offsets = jnp.cumsum(counts) - counts
            pos = jnp.arange(Sk) - offsets[sorted_e]
            tok_sorted = x[order // K]
            xe = jnp.zeros((E, CAP, H), x.dtype).at[sorted_e, pos].set(tok_sorted, mode='drop')
            h = jax.nn.silu(jnp.einsum('ech,efh->ecf', xe, w1)) * jnp.einsum('ech,efh->ecf', xe, w3)
            ye = jnp.einsum('ecf,ehf->ech', h, w2)
            pos_c = jnp.minimum(pos, CAP - 1)
            vals = ye[sorted_e, pos_c]
            vals = jnp.where((pos < CAP)[:, None], vals, 0.0)
            flat_w = topk_w.reshape(-1)[order].astype(vals.dtype)
            flat_t = (jnp.arange(Sk) // K)[order]
            out = jax.ops.segment_sum(vals * flat_w[:, None], flat_t, num_segments=T)
            shared = jax.nn.silu(x @ shared_gate.T) * (x @ shared_up.T) @ shared_down.T
            return (out + shared).reshape(B, S, H)
        return _moe_forward(hidden_states, gate_weight, e_bias, w1, w2, w3, shared_gate, shared_up, shared_down)

    def _L1_xattn_ref(q, k, v, Wq, bq, Wk, bk, Wv, bv, Wo, bo):
        import jax, jax.numpy as jnp
        import numpy as np
        D_MODEL = 128
        NHEAD = 16
        HEAD_DIM = D_MODEL // NHEAD
        B, S, D = q.shape
        H, Hd = (NHEAD, HEAD_DIM)
        qh = (q @ Wq.T + bq).reshape(B, S, H, Hd).transpose(0, 2, 1, 3)
        kh = (k @ Wk.T + bk).reshape(B, S, H, Hd).transpose(0, 2, 1, 3)
        vh = (v @ Wv.T + bv).reshape(B, S, H, Hd).transpose(0, 2, 1, 3)
        scores = jnp.einsum('bhqd,bhkd->bhqk', qh, kh) / jnp.sqrt(jnp.float32(Hd))
        attn = jax.nn.softmax(scores, axis=-1)
        out = jnp.einsum('bhqk,bhkd->bhqd', attn, vh)
        out = out.transpose(0, 2, 1, 3).reshape(B, S, D)
        return out @ Wo.T + bo

    def _L1_ffn_ref(x, router_w, router_bias, sw1, sw3, sw2, ew1, ew2):
        import jax, jax.numpy as jnp
        import numpy as np
        D_MODEL = 128
        H_SHARED = 256
        H_ROUTED = 128
        N_EXPERTS = 8
        TOP_K = 2
        B, T, C = x.shape
        xf = x.reshape(-1, C)
        shared_out = jax.nn.silu(xf @ sw1) * (xf @ sw3) @ sw2
        s = jax.nn.sigmoid((xf @ router_w.T).astype(jnp.float32))
        sel_scores = s + router_bias.astype(jnp.float32)
        _, topk_idx = jax.lax.top_k(sel_scores, TOP_K)
        s_sel = jnp.take_along_axis(s, topk_idx, axis=1)
        denom = s_sel.sum(axis=1, keepdims=True)
        gates = jnp.where(denom > 1e-09, s_sel / (denom + 1e-09), 1.0 / TOP_K).astype(x.dtype)
        one_hot = jax.nn.one_hot(topk_idx, N_EXPERTS, dtype=x.dtype)
        comb = jnp.einsum('nke,nk->ne', one_hot, gates)
        h = jax.nn.gelu(jnp.einsum('nd,edh->neh', xf, ew1), approximate=False)
        y = jnp.einsum('neh,ehd->ned', h, ew2)
        routed_out = jnp.einsum('ned,ne->nd', y, comb)
        return (shared_out + routed_out).reshape(B, T, C)
    x = x + jnp.tanh(g_xattn[0]) * _L0_xattn_ref(_layernorm(x, axis=-1), ctx_1024, L0_xattn_w_sim, L0_xattn_b_sim, L0_xattn_W_qv, L0_xattn_b_qv)
    x = x + jnp.tanh(g_ffn[0]) * _L0_ffn_ref(_layernorm(x, axis=-1), L0_ffn_gate_weight, L0_ffn_e_bias, L0_ffn_w1, L0_ffn_w2, L0_ffn_w3, L0_ffn_shared_gate, L0_ffn_shared_up, L0_ffn_shared_down)
    x = x + jnp.tanh(g_xattn[1]) * _L1_xattn_ref(_layernorm(x, axis=-1), ctx_1024, ctx_1024, L1_xattn_Wq, L1_xattn_bq, L1_xattn_Wk, L1_xattn_bk, L1_xattn_Wv, L1_xattn_bv, L1_xattn_Wo, L1_xattn_bo)
    x = x + jnp.tanh(g_ffn[1]) * _L1_ffn_ref(_layernorm(x, axis=-1), L1_ffn_router_w, L1_ffn_router_bias, L1_ffn_sw1, L1_ffn_sw3, L1_ffn_sw2, L1_ffn_ew1, L1_ffn_ew2)
    return x

_drawn_inputs = setup_inputs


def setup_inputs(seed=0):
    import zlib

    import numpy as np

    out = dict(_drawn_inputs(seed))
    spreads = {'g_ffn': (-1.0, 0.2),
     'L0_ffn_e_bias': (0.0, 0.8),
     'L1_xattn_bq': (0.0, 0.1),
     'L1_xattn_bk': (0.0, 0.8),
     'L1_xattn_bv': (0.0, 0.1),
     'L1_xattn_bo': (0.0, 0.1),
     'L1_ffn_router_bias': (0.0, 0.1)}
    factors = {'L0_ffn_gate_weight': 8.0,
     'L0_ffn_w1': 8.0,
     'L0_ffn_w2': 8.0,
     'L0_ffn_w3': 8.0,
     'L0_ffn_shared_gate': 3.892,
     'L0_ffn_shared_up': 3.991,
     'L0_ffn_shared_down': 3.659}
    for name, (base, spread) in spreads.items():
        noise = np.random.default_rng([zlib.crc32(name.encode()), seed]).standard_normal(out[name].shape)
        drawn = base * np.exp(spread * noise) if base else spread * noise
        out[name] = jnp.asarray(drawn.astype(out[name].dtype))
    for name, factor in factors.items():
        out[name] = (out[name] * factor).astype(out[name].dtype)
    return out
```

```python
from contextlib import ExitStack

import concourse.bass as bass
from concourse import mybir

F32 = mybir.dt.float32
BF16 = mybir.dt.bfloat16
I32 = mybir.dt.int32
ALU = mybir.AluOpType
ACT = mybir.ActivationFunctionType
AX = mybir.AxisListType

P = 128
NT = 32
QT = 4
NQ = NT // QT
E0 = 64
F0 = 64
G0 = 8
CAP = 128
NPAIR = E0 // 2
E1 = 8
HEADS = 16
HD = P // HEADS
EPS = 1e-5
ROUTE_SCALE = 2.5
BIG = 1e30
GONE = -1e30
ROW = P + E0
NROWS = NT * P + P


def at(t, n=P):
    return slice(t * n, (t + 1) * n) if isinstance(t, int) else bass.ds(t * n, n)


def after(eng, sem, t, per=1):
    if isinstance(t, int) and t < 0:
        return
    eng.wait_ge(sem, t * per + per)


def hold(eng, passed):
    eng.sem_inc(passed, 1)


def pipeline(eng, count, ring, stages):
    last = max(lag for lag, _ in stages)
    first = -(-(last + ring) // ring) * ring
    turns = (count - first) // ring

    def one(s):
        for lag, step in stages:
            t = s - lag
            if 0 <= t < count:
                step(t, t % ring, t // ring)

    for s in range(first):
        one(s)
    with eng.Fori(0, turns) as i:
        for v in range(ring):
            for lag, step in stages:
                c = first + v - lag
                step(i * ring + c, c % ring, i + c // ring)
    for s in range(first + turns * ring, count + last):
        one(s)


def build(nc, A, out, dbg=None):
    ctx = ExitStack()
    with ctx:
        def sb(name, cols, dt=F32, parts=P):
            return ctx.enter_context(nc.sbuf_tensor(name, [parts, cols], dt))

        sems = {}

        def sem(name):
            if name not in sems:
                sems[name] = ctx.enter_context(nc.semaphore(name))
            return sems[name]

        bank = [ctx.enter_context(nc.psum_tensor(f"bank{k}", [P, 512], F32)) for k in range(8)]

        rows_dram = nc.dram_tensor("token_rows", (NT * P, ROW), F32).ap()
        acc_dram = [nc.dram_tensor(f"expert_sums{j}", (NROWS, P), F32).ap() for j in range(2)]

        x_all = sb("x_all", NT * P)
        xT_all = sb("xT_all", NT * P)
        kT_all = sb("kT_all", NT * P)
        v_all = sb("v_all", NT * P)

        ident = sb("ident", P)
        ones = sb("ones", P)
        ones_bf = sb("ones_bf", P, BF16)
        tri_bf = sb("tri_bf", P, BF16)
        ipart = sb("ipart", 1, I32)
        pcol = sb("pcol", 1)
        dump_row = sb("dump_row", 1)
        tile_no = sb("tile_no", NT)
        itile = sb("itile", NT, I32)
        iota_a = sb("iota_a", 16 * E0, BF16)
        iota_b = sb("iota_b", 8 * E0, BF16)
        mod8 = sb("mod8", 8)
        imod8 = sb("imod8", 8, I32)
        same8 = sb("same8", P)
        head_m = sb("head_m", 4)
        ihead = sb("ihead", 4, I32)
        group_m = sb("group_m", 4)
        vmask = sb("vmask", 4 * P)
        half_pow = sb("half_pow", 4)
        zeros = sb("zeros", 1408)

        rowin = sb("rowin", 512, F32)
        rowv = sb("rowv", 512)
        BQV, EB, BO, RB, BSIM, GX, GF, BV = 0, 128, 192, 320, 328, 329, 331, 333
        th = sb("th", 4)
        wcol = sb("wcol", 3)
        bq = sb("bq", 1)
        bk = sb("bk", 1)
        bv = sb("bv", 1)
        w2b = sb("w2b", P)
        wqv = sb("wqv", 4 * P)
        wnat = sb("wnat", 8 * P)
        wT = sb("wT", 8 * P)
        GATE, SG, SU, SD, WQ, WK, WV, WO = range(8)
        rw_nat = sb("rw_nat", P)
        rwT = sb("rwT", P)
        bqv_row = sb("bqv_row", P)
        bo_row = sb("bo_row", P)
        bv_rep = sb("bv_rep", P)
        sw1 = sb("sw1", 256)
        sw3 = sb("sw3", 256)
        sw2 = sb("sw2", 256)
        ew1 = sb("ew1", E1 * P)
        ew2 = sb("ew2", E1 * P)

        arena = sb("arena", 26200)
        used = [0]

        def carve(cols, dt=F32):
            words = cols if dt in (F32, I32) else (cols + 1) // 2
            a = arena[:, used[0]:used[0] + words]
            used[0] += words
            assert used[0] <= 26200, used[0]
            return a if dt == F32 else a.bitcast(dt)

        RA = 4
        ctx_in = [carve(P) for _ in range(RA)]
        xn = [carve(P) for _ in range(RA)]
        eT = [carve(P) for _ in range(RA)]
        cT = [carve(P) for _ in range(RA)]
        cw = [carve(P) for _ in range(RA)]
        st = [carve(6) for _ in range(RA)]
        mv = [carve(2) for _ in range(RA)]
        ve = [carve(1) for _ in range(RA)]
        rstd = [carve(1) for _ in range(RA)]
        mraw = [carve(1) for _ in range(RA)]
        msim = [carve(1) for _ in range(RA)]
        nb = [carve(1) for _ in range(RA)]
        gmax = [carve(1) for _ in range(RA)]
        ngmax = [carve(1) for _ in range(RA)]
        eb = [carve(P) for _ in range(RA)]
        pr = [carve(P) for _ in range(RA)]
        prn = [carve(P) for _ in range(RA)]
        ssum = [carve(1) for _ in range(RA)]
        rs = [carve(1) for _ in range(RA)]
        pT = [carve(P) for _ in range(RA)]
        hq = [carve(P) for _ in range(RA)]
        ehT = [carve(P) for _ in range(RA)]
        ecT = [carve(P) for _ in range(RA)]
        hcr = [carve(1) for _ in range(RA)]
        hc = [carve(1) for _ in range(RA)]
        xb = [carve(P) for _ in range(RA)]
        st1 = [carve(6) for _ in range(RA)]
        mv1 = [carve(2) for _ in range(RA)]
        ve1 = [carve(1) for _ in range(RA)]
        rstd1 = [carve(1) for _ in range(RA)]
        xn1 = [carve(P) for _ in range(RA)]
        xn1T = [carve(P) for _ in range(RA)]
        end_a = used[0]

        logits = carve(NT * E0)
        sc = carve(NT * E0)
        sfc = carve(NT * E0)
        wr = logits
        m_bf = carve(NT * E0, BF16)
        s_bf = carve((NT + 1) * E0, BF16)
        gs = carve(NT * G0)
        t1 = carve(NT * 32)
        t2 = carve(NT * 32)
        t3 = carve(NT * 16)
        rsum = carve(NT)
        gsx = carve(QT * 12)
        g8 = carve(QT * 8)
        g8x = carve(QT * 8)
        gleft = carve(QT * 12)
        gmask = carve(QT * 8)
        tmp = carve(QT * E0)
        k8 = carve(QT * 8)
        kleft = carve(QT * E0)
        key = carve(QT * E0, I32)
        da_i = carve(QT * E0, I32)
        db_i = carve(QT * E0, I32)
        da = carve(QT * E0, BF16)
        db = carve(QT * E0, BF16)
        hot_a = carve(QT * 16 * E0, BF16)
        hot_b = carve(QT * 8 * E0, BF16)
        hot_v = carve(QT * 2 * 8 * E0, BF16)
        tbl = [t1[:, 0:512], t1[:, 512:1024], t2[:, 0:512]]
        slot_tok = carve(E0)
        filled = carve(E0)
        cnt = carve(E0)
        slot_row = carve(E0)
        gidx = carve(E0, I32)
        sidx = carve(E0, I32)

        end_r = used[0]

        used[0] = 0
        RB_ = 4
        w1n = [carve(P) for _ in range(2)] * 2
        w3n = [carve(P) for _ in range(2)] * 2
        w2n = [carve(P) for _ in range(2)] * 2
        w13T = [carve(2 * P) for _ in range(2)] * 2
        w2T = [carve(2 * P) for _ in range(2)] * 2
        xe = [carve(2 * ROW) for _ in range(RB_)]
        xeT = [carve(2 * P) for _ in range(2)] * 2
        sil = [carve(P) for _ in range(2)] * 2
        hh = [carve(P) for _ in range(2)] * 2
        hhT = [carve(P) for _ in range(2)] * 2
        ye = [carve(2 * P) for _ in range(RB_)]
        gi = [carve(2, I32) for _ in range(RB_)]
        si = [carve(2, I32) for _ in range(RB_)]
        sh_s, sh_u, sh_h, sh_y = (carve(512) for _ in range(4))
        assert used[0] <= end_a

        used[0] = end_a
        a0 = [carve(P) for _ in range(2)]
        a1 = [carve(P) for _ in range(2)]
        x2 = [carve(P) for _ in range(2)]
        cst = [carve(6) for _ in range(2)]
        cmv = [carve(2) for _ in range(2)]
        cve = [carve(1) for _ in range(2)]
        crs = [carve(1) for _ in range(2)]
        cxn = [carve(P) for _ in range(2)]
        cxT = [carve(P) for _ in range(2)]
        qm = [carve(512) for _ in range(2)]
        kbd = [carve(512) for _ in range(2)]
        vbd = [carve(512) for _ in range(2)]
        smax = [carve(16) for _ in range(2)]
        sdif = [carve(512) for _ in range(4)]
        pexp = [carve(512) for _ in range(4)]
        ppT = [carve(2048) for _ in range(2)]
        rden = [carve(P) for _ in range(2)]
        oT = [carve(P) for _ in range(2)]
        x2b = [carve(P) for _ in range(2)]
        assert used[0] <= end_r

        used[0] = 0
        RD = 4
        dst = [carve(6) for _ in range(RD)]
        dmv = [carve(2) for _ in range(RD)]
        dve_ = [carve(1) for _ in range(RD)]
        drs = [carve(1) for _ in range(RD)]
        dxn = [carve(P) for _ in range(RD)]
        dxT = [carve(P) for _ in range(RD)]
        dlog = carve(NT * E1)
        dsc = carve(NT * E1)
        dsel = carve(NT * E1)
        dmask = carve(NT * E1)
        dgat = carve(NT * E1)
        dalt = carve(NT * E1)
        dden = carve(NT)
        dok = carve(NT)
        dno = carve(NT)
        selx = carve(NT * 14)
        s8 = carve(NT * 8)
        s8x = carve(NT * 8)
        sleft = carve(NT * 14)
        fh = [carve(512) for _ in range(2)]
        fg = [carve(512) for _ in range(2)]
        eh = [carve(512) for _ in range(2)]
        assert used[0] <= end_a

        FREE_AT_START = dict(pe=("lists_psum", "ey_psum", "fy_psum"), act=("eh_done", "shu_done", "shy_done"),
                             pool=("shh_done", "shx_done"), dve=("key_done", "fh_done", "fx_done", "y_added"))

        def start(eng, name):
            for n in FREE_AT_START[name]:
                eng.sem_inc(sem(n), 1)

        block = ctx.enter_context(nc.Block())

        IDENT_OK, ZEROS_OK, ROWV_OK, WCOL_OK, CONSTS_OK = 2, 5, 6, 8, 31
        BQV_OK, WQV_OK, BO_OK, WO_OK, SD_OK, HEAD_OK, SW_OK = 1, 2, 3, 4, 5, 6, 8

        @block.sync
        def _(sp):
            xd = A["x"].rearrange("t p d -> p t d")
            xv = x_all[:, :].rearrange("p (t d) -> p t d", d=P)
            sp.dma_start(xv[:, 0:8, :], xd[:, 0:8, :]).then_inc(sem("x_first"), 16)
            for name, o, n in (("L0_xattn_b_qv", BQV, 128), ("L0_ffn_e_bias", EB, 64), ("L1_xattn_bo", BO, 128),
                               ("L1_ffn_router_bias", RB, 8), ("L0_xattn_b_sim", BSIM, 1), ("g_xattn", GX, 2),
                               ("g_ffn", GF, 2)):
                sp.dma_start(rowin[0:1, o:o + n], A[name].rearrange("(a d) -> a d", a=1)).then_inc(sem("rows_in"), 16)
            sp.dma_start(wcol[:, :], A["L0_xattn_w_sim"].rearrange("(c p) -> p c", p=P),
                         allow_slow_non_contiguous=True).then_inc(sem("cols_in"), 16)
            for name, dst_ in (("L1_xattn_bq", bq), ("L1_xattn_bk", bk), ("L1_xattn_bv", bv)):
                sp.dma_start(dst_[:, :], A[name].rearrange("(p c) -> p c", c=1)).then_inc(sem("cols_in"), 16)
            sp.dma_start(wqv[:, :].rearrange("p (c n) -> p c n", c=4),
                         A["L0_xattn_W_qv"].rearrange("(c p) n -> p c n", p=P)).then_inc(sem("wqv_in"), 16)
            wn = wnat[:, :].rearrange("p (k d) -> p k d", d=P)
            sp.dma_start(wn[0:E0, GATE, :], A["L0_ffn_gate_weight"]).then_inc(sem("wnat_in"), 16)
            for name, k in (("L0_ffn_shared_gate", SG), ("L0_ffn_shared_up", SU), ("L0_ffn_shared_down", SD),
                            ("L1_xattn_Wq", WQ), ("L1_xattn_Wk", WK), ("L1_xattn_Wv", WV), ("L1_xattn_Wo", WO)):
                sp.dma_start(wn[:, k, :], A[name]).then_inc(sem("wnat_in"), 16)
            sp.dma_start(rw_nat[0:E1, :], A["L1_ffn_router_w"]).then_inc(sem("wnat_in"), 16)
            sp.dma_start(xv[:, 8:NT, :], xd[:, 8:NT, :]).then_inc(sem("x_rest"), 16)

            def ctx_tile(t, u, r):
                after(sp, sem("hqT_done"), t - RA)
                sp.dma_start(ctx_in[u], A["ctx_1024"][t:t + 1, :, :].rearrange("t p d -> p (t d)") if isinstance(t, int)
                             else A["ctx_1024"][bass.ds(t, 1), :, :].rearrange("t p d -> p (t d)")
                             ).then_inc(sem(f"ctx_in{u}"), 16)

            def rows_out(t, u, r):
                after(sp, sem("xn1_done"), t)
                sp.dma_start(rows_dram[at(t), 0:P], xn1[u]).then_inc(sem(f"rows_out{u}"), 16)

            pipeline(sp, NT, RA, [(0, ctx_tile), (4, rows_out)])

            sp.wait_ge(sem("pool_setup"), ZEROS_OK)
            for acc in acc_dram:
                av = acc.rearrange("(p r) d -> p (r d)", p=P)
                for k in range(3):
                    sp.dma_start(av[:, k * 1408:(k + 1) * 1408], zeros[:, :]).then_inc(sem("acc_zero"), 16)
            sp.dma_start(sw1[:, :], A["L1_ffn_sw1"]).then_inc(sem("w_late"), 16)
            sp.dma_start(sw3[:, :], A["L1_ffn_sw3"]).then_inc(sem("w_late"), 16)
            sp.dma_start(sw2[:, :].rearrange("p (c n) -> p c n", c=2),
                         A["L1_ffn_sw2"].rearrange("(c p) n -> p c n", p=P)).then_inc(sem("w_late"), 16)
            sp.dma_start(ew1[:, :].rearrange("p (e n) -> p e n", e=E1),
                         A["L1_ffn_ew1"].rearrange("e p n -> p e n")).then_inc(sem("w_late"), 16)
            sp.dma_start(ew2[:, :].rearrange("p (e n) -> p e n", e=E1),
                         A["L1_ffn_ew2"].rearrange("e p n -> p e n")).then_inc(sem("w_late"), 16)

            sp.wait_ge(sem("lg_done"), NT)
            for u in range(RA):
                sp.wait_ge(sem(f"rows_out{u}"), 16 * (NT // RA))

            sp.wait_ge(sem("wr_done"), 1)
            sp.dma_start(rows_dram[:, P:ROW].rearrange("(t p) e -> p t e", p=P),
                         wr.rearrange("p (t e) -> p t e", e=E0)).then_inc(sem("wr_out"), 16)

            def expert_weights(t, u, r):
                after(sp, sem("w2T_psum"), t - 2)
                for w, dst_ in (("L0_ffn_w1", w1n), ("L0_ffn_w3", w3n)):
                    src = A[w].rearrange("e f d -> (e f) d")
                    sp.dma_start(dst_[u], src[at(t), :]).then_inc(sem(f"w_in{u}"), 16)
                src = A["L0_ffn_w2"]
                e2 = src[2 * t:2 * t + 2] if isinstance(t, int) else src[bass.ds(t * 2, 2)]
                sp.dma_start(w2n[u].rearrange("p (e f) -> p e f", e=2),
                             e2.rearrange("e d f -> d e f")).then_inc(sem(f"w_in{u}"), 16)
            pipeline(sp, NPAIR, 2, [(0, expert_weights)])

            sp.wait_ge(sem("acc_done0"), 16 * NPAIR)
            sp.wait_ge(sem("acc_done1"), 16 * NPAIR)

            def sums_in(t, u, r):
                after(sp, sem("x2a"), t - 2)
                sp.dma_start(a0[u], acc_dram[0][at(t), :]).then_inc(sem(f"sums_in{u}"), 16)
                sp.dma_start(a1[u], acc_dram[1][at(t), :]).then_inc(sem(f"sums_in{u}"), 16)
            pipeline(sp, NT, 2, [(0, sums_in)])

            ov = out.rearrange("(q t) p d -> q p t d", t=QT)
            with sp.Fori(0, NQ) as q:
                sp.wait_ge(sem("y_added"), 1 + ((q * E1 + E1) * QT))
                sp.dma_start(ov[bass.ds(q, 1)].rearrange("q p t d -> p (q t) d"),
                             x_all[:, bass.ds(q * 512, 512)].rearrange("p (t d) -> p t d", d=P)
                             ).then_inc(sem("out_done"), 16)
            sp.wait_ge(sem("out_done"), 16 * NQ)
            if dbg:
                for k, v in dbg.items():
                    sp.dma_start(v, {"x_all": x_all, "kT_all": kT_all, "v_all": v_all, "slot_tok": slot_tok, "cnt": cnt,
                                     "bo_row": bo_row}[k][:, :]).then_inc(sem("dbg"), 16)
                sp.wait_ge(sem("dbg"), 16 * len(dbg))

        @block.gpsimd
        def _(pool):
            k = [0]

            def link(ins):
                k[0] += 1
                ins.then_inc(sem("pool_setup"), 1)
                pool.wait_ge(sem("pool_setup"), k[0])

            start(pool, "pool")
            link(pool.memset(ident[:, :], 0.0))
            link(pool.affine_select(out=ident[:, :], in_=ident[:, :], compare_op=ALU.not_equal, fill=1.0, base=0,
                               pattern=[[-1, P]], channel_multiplier=1))
            assert k[0] == IDENT_OK
            link(pool.memset(ones[:, :], 1.0))
            link(pool.memset(half_pow[:, :], -0.5))
            link(pool.memset(zeros[:, :], 0.0))
            assert k[0] == ZEROS_OK
            pool.wait_ge(sem("rows_in"), 16 * 7)
            link(pool.partition_broadcast(rowv[:, 0:BV], rowin[0:1, 0:BV]))
            assert k[0] == ROWV_OK
            pool.wait_ge(sem("cols_in"), 16 * 4)
            link(pool.tensor_scalar(w2b[:, :], ones[:, :], wcol[:, 1:2], None, ALU.mult))
            link(pool.tensor_scalar(bv_rep[:, :], ones[:, :], bv[:, 0:1], None, ALU.mult))
            assert k[0] == WCOL_OK
            link(pool.memset(ones_bf[:, :], 1.0))
            link(pool.memset(tri_bf[:, :], 1.0))
            link(pool.affine_select(out=tri_bf[:, :], in_=tri_bf[:, :], compare_op=ALU.is_gt, fill=0.0, base=0,
                                    pattern=[[1, P]], channel_multiplier=-1))
            link(pool.iota(ipart[:, 0:1], pattern=[[1, 1]], base=0, channel_multiplier=1))
            link(pool.tensor_copy(pcol[:, :], ipart[:, 0:1]))
            link(pool.tensor_scalar(dump_row[:, :], pcol[:, :], 1.0, float(NT * P), ALU.mult, ALU.add))
            link(pool.iota(itile[:, :], pattern=[[1, NT]], base=0, channel_multiplier=0))
            link(pool.tensor_copy(tile_no[:, :], itile[:, :]))
            link(pool.iota(iota_a[:, :], pattern=[[0, 8], [1, 16], [0, 8]], base=0, channel_multiplier=0,
                           allow_small_or_imprecise_dtypes=True))
            link(pool.iota(iota_b[:, :], pattern=[[1, 8], [0, E0]], base=0, channel_multiplier=0,
                           allow_small_or_imprecise_dtypes=True))
            link(pool.iota(imod8[:, :], pattern=[[-1, 8]], base=8, channel_multiplier=1))
            link(pool.iota(ihead[:, :], pattern=[[-8, 4]], base=32, channel_multiplier=1))
            link(pool.memset(same8[:, :], 1.0))
            sv = same8[:, :].rearrange("p (a b) -> p a b", b=8)
            link(pool.affine_select(out=sv, in_=sv, compare_op=ALU.is_ge, fill=0.0, base=0,
                                    pattern=[[-8, 16], [0, 8]], channel_multiplier=1))
            link(pool.affine_select(out=sv, in_=sv, compare_op=ALU.is_ge, fill=0.0, base=7,
                                    pattern=[[8, 16], [0, 8]], channel_multiplier=-1))
            link(pool.memset(group_m[:, :], 1.0))
            link(pool.affine_select(out=group_m[:, :], in_=group_m[:, :], compare_op=ALU.is_ge, fill=0.0, base=0,
                                    pattern=[[-32, 4]], channel_multiplier=1))
            link(pool.affine_select(out=group_m[:, :], in_=group_m[:, :], compare_op=ALU.is_ge, fill=0.0, base=31,
                                    pattern=[[32, 4]], channel_multiplier=-1))
            link(pool.memset(vmask[:, :], 0.0))
            vm = vmask[:, :].rearrange("p (x d) -> p x d", d=HD)
            for h in range(4):
                vh = vmask[:, h * P:(h + 1) * P].rearrange("p (g h d) -> p g h d", g=4, h=4)
                link(pool.affine_select(out=vh, in_=vh, compare_op=ALU.not_equal, fill=1.0, base=-h,
                                        pattern=[[0, 4], [1, 4], [0, HD]], channel_multiplier=0))
            assert k[0] == CONSTS_OK, k[0]

            def a_pow(t, u, r):
                after(pool, sem("ve_done"), t, 3)
                pool.tensor_tensor(rstd[u], ve[u], half_pow[:, 0:1], ALU.pow).then_inc(sem("rstd_done"), 1)

            def a_gmax(t, u, r):
                pool.wait_ge(sem("max_steps"), t * 3 + 2)
                hold(pool, sem("pool_passed"))
                pool.partition_all_reduce(gmax[u], msim[u], P, bass.bass_isa.ReduceOp.max).then_inc(sem("gmax_done"), 1)

            def a_bias(t, u, r):
                after(pool, sem("x1_done"), t - RA)
                if isinstance(t, int) and t == 0:
                    pool.wait_ge(sem("scaled"), BQV_OK)
                pool.tensor_tensor(xb[u], x_all[:, at(t)], bqv_row[:, :], ALU.add).then_inc(sem("xb_done"), 1)

            def a_pow1(t, u, r):
                after(pool, sem("ve1_done"), t, 3)
                pool.tensor_tensor(rstd1[u], ve1[u], half_pow[:, 0:1], ALU.pow).then_inc(sem("rstd1_done"), 1)

            def a_keep(t, u, r):
                after(pool, sem("xn1T_done"), t)
                pool.tensor_copy(xT_all[:, at(t)], xn1T[u]).then_inc(sem("xT_kept"), 1)

            pool.wait_ge(sem("x_rest"), 16)
            pipeline(pool, NT, RA, [(2, a_gmax), (4, a_pow1), (3, a_bias), (5, a_keep), (0, a_pow)])

            for u in range(RA):
                pool.wait_ge(sem(f"rows_out{u}"), 16 * (NT // RA))
            pool.wait_ge(sem("lg_done"), NT)
            pool.wait_ge(sem("xn1T_psum"), NT)
            pool.wait_ge(sem("out_psum"), NT)
            for u in range(2):
                pool.memset(w2T[u], 0.0).then_inc(sem("w2T_zero"), 1)

            with pool.Fori(0, NQ) as q:
                pool.wait_ge(sem("shu_done"), 1 + (q + 1))
                pool.tensor_tensor(sh_h, sh_s, sh_u, ALU.mult).then_inc(sem("shh_done"), 1)
                pool.wait_ge(sem("shy_done"), 1 + (q + 1))
                xq = x_all[:, bass.ds(q * 512, 512)]
                pool.tensor_tensor(xq, xq, sh_y, ALU.add).then_inc(sem("shx_done"), 1)

            pool.memset(s_bf[:, 0:E0], 0.0).then_inc(sem("s_done"), 1)
            with pool.Fori(0, NQ) as q:
                pool.wait_ge(sem("m_done"), q + 1)
                for j in range(QT):
                    c = q * (QT * E0) + j * E0
                    pool.wait_ge(sem("s_done"), q * QT + (j + 1))
                    pool.tensor_tensor(s_bf[:, bass.ds(c + E0, E0)], s_bf[:, bass.ds(c, E0)],
                                       m_bf[:, bass.ds(c, E0)], ALU.add).then_inc(sem("s_done"), 1)

            for s_ in ("acc_zero",):
                pool.wait_ge(sem(s_), 16 * 6)
            pool.wait_ge(sem("wr_out"), 16)
            pool.wait_ge(sem("idx_done"), 2)

            def gather(t, u, r):
                after(pool, sem("gi_done"), t)
                after(pool, sem("ye_done"), t - RB_)
                for j in range(2):
                    hold(pool, sem("pool_passed"))
                    pool.indirect_dma_start(out=xe[u][:, j * ROW:(j + 1) * ROW], out_offset=None, in_=rows_dram,
                                            in_offset=bass.IndirectOffsetOnAxis(ap=gi[u][:, j:j + 1], axis=0)
                                            ).then_inc(sem(f"xe_in{u}"), 16)

            def scatter(t, u, r):
                after(pool, sem("ye_done"), t)
                for j in range(2):
                    after(pool, sem(f"acc_done{j}"), t - 1, 16)
                    hold(pool, sem("pool_passed"))
                    pool.indirect_dma_start(out=acc_dram[j], out_offset=bass.IndirectOffsetOnAxis(ap=si[u][:, j:j + 1], axis=0),
                                            in_=ye[u][:, j * P:(j + 1) * P], in_offset=None, compute_op=ALU.add,
                                            bounds_check=NROWS - 1, oob_is_err=True).then_inc(sem(f"acc_done{j}"), 16)

            pipeline(pool, NPAIR, RB_, [(3, scatter), (0, gather)])

            pool.wait_ge(sem("v_done"), NT)

            def c_sum(t, u, r):
                after(pool, sem(f"sums_in{u}"), r, 32)
                after(pool, sem("x2_done"), t - 2)
                pool.tensor_tensor(x2[u], a0[u], a1[u], ALU.add).then_inc(sem("x2a"), 1)
                after(pool, sem("x2a"), t)
                pool.tensor_tensor(x_all[:, at(t)], x2[u], x_all[:, at(t)], ALU.add).then_inc(sem("x2_done"), 1)

            def c_pow(t, u, r):
                after(pool, sem("cve_done"), t, 3)
                pool.tensor_tensor(crs[u], cve[u], half_pow[:, 0:1], ALU.pow).then_inc(sem("crs_done"), 1)

            def c_kv(t, u, r):
                after(pool, sem("s_psum"), t - 2, 4)
                pool.tensor_tensor(kbd[u].rearrange("p (h k) -> p h k", h=4),
                                   kT_all[:, at(t)].rearrange("p (a k) -> p a k", a=1).broadcast_to([P, 4, P]),
                                   head_m[:, :].rearrange("p (h a) -> p h a", a=1).broadcast_to([P, 4, P]),
                                   ALU.mult).then_inc(sem("kbd_done"), 1)

            def c_v(t, u, r):
                after(pool, sem("pv_psum"), t - 2)
                pool.tensor_tensor(vbd[u].rearrange("p (h k) -> p h k", h=4),
                                   v_all[:, at(t)].rearrange("p (a k) -> p a k", a=1).broadcast_to([P, 4, P]),
                                   vmask[:, :].rearrange("p (h k) -> p h k", h=4),
                                   ALU.mult).then_inc(sem("vbd_done"), 1)

            def c_bias(t, u, r):
                after(pool, sem("x3_done"), t - 2)
                pool.tensor_tensor(x2b[u], x_all[:, at(t)], bo_row[:, :], ALU.add).then_inc(sem("x2b_done"), 1)

            pipeline(pool, NT, 2, [(0, c_sum), (0, c_kv), (0, c_pow), (1, c_v), (2, c_bias)])

            def d_pow(t, u, r):
                after(pool, sem("dve_done"), t, 3)
                pool.tensor_tensor(drs[u], dve_[u], half_pow[:, 0:1], ALU.pow).then_inc(sem("drs_done"), 1)

            def d_keep(t, u, r):
                after(pool, sem("dxT_done"), t)
                pool.tensor_copy(xT_all[:, at(t)], dxT[u]).then_inc(sem("xT2_kept"), 1)
            pipeline(pool, NT, RD, [(0, d_pow), (1, d_keep)])

        @block.tensor
        def _(pe):
            def T(dst_, src, n=P):
                return pe.transpose(dst_, src, ident[0:n, 0:n])

            start(pe, "pe")
            pe.wait_ge(sem("pool_setup"), IDENT_OK)
            pe.wait_ge(sem("wnat_in"), 16 * 9)
            for k in range(8):
                n = E0 if k == GATE else P
                m = T(bank[k // 4][:, (k % 4) * P:(k % 4) * P + n], wnat[0:n, k * P:(k + 1) * P], n)
                if k % 4 == 3:
                    m.then_inc(sem("wT_psum"), 1)
            T(bank[2][:, 0:E1], rw_nat[0:E1, :], E1).then_inc(sem("wT_psum"), 1)
            pe.wait_ge(sem("wT_done"), 4)
            pe.wait_ge(sem("pool_setup"), WCOL_OK)
            pe.matmul(bank[3][:, 0:P], bv_rep[:, :], wT[:, WO * P:(WO + 1) * P], start=True, stop=True
                      ).then_inc(sem("bvo_psum"), 1)
            pe.wait_ge(sem("pool_setup"), WCOL_OK)
            pe.wait_ge(sem("scaled"), BO_OK)
            pe.wait_ge(sem("scaled"), WQV_OK)

            def a_T(t, u, r):
                after(pe, sem("xn_done"), t)
                after(pe, sem(f"ctx_in{u}"), r, 16)
                after(pe, sem("eT_done"), t - 1, 2)
                b = bank[0]
                T(b[:, 0:P], xn[u])
                T(b[:, P:2 * P], ctx_in[u]).then_inc(sem("T_psum"), 1)

            def a_S(t, u, r):
                after(pe, sem("eT_done"), t, 2)
                after(pe, sem("pr_done"), t - 1)
                b = bank[1]
                pe.matmul(b[:, 0:P], w2b[:, :], cT[u], start=True, stop=False)
                after(pe, sem("cw_done"), t)
                pe.matmul(b[:, 0:P], eT[u], cw[u], start=False, stop=True).then_inc(sem("sim_psum"), 1)

            def a_PT(t, u, r):
                after(pe, sem("prn_done"), t)
                after(pe, sem("pT_done"), t - 1)
                T(bank[2][:, 0:P], prn[u]).then_inc(sem("pT_psum"), 1)

            def a_HC(t, u, r):
                after(pe, sem("eb_done"), t)
                after(pe, sem("hc_steps"), t - 1, 3)
                b = bank[4]
                pe.matmul(b[:, 0:P], xn[u], eb[u], start=True, stop=True)
                pe.matmul(b[:, P:2 * P], ones[:, :], eb[u], start=True, stop=True).then_inc(sem("hc_psum"), 1)

            def a_HQ(t, u, r):
                after(pe, sem("pT_done"), t)
                after(pe, sem("hq_done"), t - 1)
                pe.matmul(bank[3][:, 0:P], ctx_in[u], pT[u], start=True, stop=True).then_inc(sem("hqT_done"), 1)

            def a_OUT(t, u, r):
                after(pe, sem("x1_done"), t - 1)
                b = bank[5][:, 0:P]
                pe.matmul(b, eT[u], wqv[:, 0:P], start=True, stop=False)
                after(pe, sem("hq_done"), t)
                pe.matmul(b, hq[u], wqv[:, P:2 * P], start=False, stop=False)
                after(pe, sem("hc_steps"), t, 3)
                pe.matmul(b, ecT[u], wqv[:, 3 * P:4 * P], start=False, stop=False)
                after(pe, sem("ehT_done"), t)
                pe.matmul(b, ehT[u], wqv[:, 2 * P:3 * P], start=False, stop=True).then_inc(sem("out_psum"), 1)

            def a_XT(t, u, r):
                after(pe, sem("xn1_done"), t)
                after(pe, sem("lg_done"), t - 1)
                T(bank[6][:, 0:P], xn1[u]).then_inc(sem("xn1T_psum"), 1)

            def a_LG(t, u, r):
                after(pe, sem("xn1T_done"), t)
                pe.matmul(bank[6][:, P:2 * P], xn1T[u], wT[:, GATE * P:(GATE + 1) * P], start=True, stop=True
                          ).then_inc(sem("lg_psum"), 1)

            def a_KV(t, u, r):
                after(pe, sem("v_done"), t - 1)
                b = bank[7]
                pe.matmul(b[:, 0:P], wT[:, WK * P:(WK + 1) * P], cT[u], start=True, stop=True)
                pe.matmul(b[:, P:2 * P], cT[u], wT[:, WV * P:(WV + 1) * P], start=True, stop=True
                          ).then_inc(sem("kv_psum"), 1)

            pipeline(pe, NT, RA, [(2, a_S), (4, a_OUT), (3, a_PT), (1, a_T), (5, a_XT), (3, a_HC), (3, a_HQ),
                                  (2, a_KV), (5, a_LG)])

            pe.wait_ge(sem("xT_kept"), NT)
            pe.wait_ge(sem("eT_done"), 2 * NT)
            pe.wait_ge(sem("pr_done"), NT)
            pe.wait_ge(sem("pT_done"), NT)
            pe.wait_ge(sem("scaled"), SD_OK)
            with pe.Fori(0, NQ) as q:
                xq = xT_all[:, bass.ds(q * 512, 512)]
                pe.wait_ge(sem("shu_done"), 1 + q)
                pe.matmul(bank[0][:, :], wT[:, SG * P:(SG + 1) * P], xq, start=True, stop=True)
                pe.matmul(bank[1][:, :], wT[:, SU * P:(SU + 1) * P], xq, start=True, stop=True
                          ).then_inc(sem("sh_psum"), 1)
                pe.wait_ge(sem("shh_done"), 1 + (q + 1))
                pe.wait_ge(sem("shy_done"), 1 + q)
                for j in range(QT):
                    m = pe.matmul(bank[2][:, j * P:(j + 1) * P], sh_h[:, j * P:(j + 1) * P],
                                  wT[:, SD * P:(SD + 1) * P], start=True, stop=True)
                m.then_inc(sem("shy_psum"), 1)

            pe.wait_ge(sem("pool_setup"), CONSTS_OK)
            pe.wait_ge(sem("lg_done"), NT)
            pe.wait_ge(sem("xn1T_done"), NT)
            pe.wait_ge(sem("x1_done"), NT)
            pe.wait_ge(sem("pool_setup"), ZEROS_OK)
            for k in range(2):
                pe.matmul(bank[6 + k][:, :], zeros[:, 0:P], zeros[:, 0:512], start=True, stop=False,
                          skip_group_check=True)
            hb = hot_v.rearrange("p (j v b e) -> p j v b e", j=QT, v=2, e=E0)
            ha = hot_a.rearrange("p (j g x) -> p j g x", j=QT, g=8)
            with pe.Fori(0, NQ) as q:
                pe.wait_ge(sem("s_done"), q * QT + (QT + 1))
                pe.wait_ge(sem("key_done"), 1 + (q))
                pe.matmul(bank[5][:, 0:QT * E0], tri_bf[:, :], m_bf[:, bass.ds(q * (QT * E0), QT * E0)],
                          start=True, stop=False)
                pe.matmul(bank[5][:, 0:QT * E0], ones_bf[:, :], s_bf[:, bass.ds(q * (QT * E0), QT * E0)],
                          start=False, stop=True).then_inc(sem("pos_psum"), 1)
                pe.wait_ge(sem("hot_done"), q + 1)
                for j in range(QT):
                    for g in range(8):
                        o = (g % 4) * P
                        m = pe.matmul(bank[6 + g // 4][:, o:o + P], ha[:, j, g, :],
                                      hb[:, j, :, :, 8 * g:8 * g + 8], start=False, stop=False,
                                      skip_group_check=True)
                m.then_inc(sem("lists_psum"), 1)
            pe.wait_ge(sem("s_done"), NT + 1)
            pe.wait_ge(sem("key_done"), 1 + (NQ))
            pe.matmul(bank[5][:, 0:E0], ones_bf[:, :], s_bf[:, NT * E0:(NT + 1) * E0], start=True, stop=True
                      ).then_inc(sem("cnt_psum"), 1)
            pe.wait_ge(sem("tbl_done"), 1)
            pe.wait_ge(sem("hq_done"), NT)
            pe.matmul(bank[3][:, :], same8[:, :], tbl[2][:, :], start=True, stop=True).then_inc(sem("slot_psum"), 1)

            pe.wait_ge(sem("shy_done"), 1 + NQ)
            pe.wait_ge(sem("slot_done"), 1)

            def b_W(t, u, r):
                after(pe, sem(f"w_in{u % 2}"), r * 2 + u // 2, 48)
                after(pe, sem("w13T_done"), t - 1)
                T(bank[0][:, 0:P], w1n[u])
                T(bank[0][:, P:2 * P], w3n[u]).then_inc(sem("w13T_psum"), 1)
                after(pe, sem("w2T_done"), t - 1, 2)
                T(bank[1][:, 0:P], w2n[u]).then_inc(sem("w2T_psum"), 1)

            def b_X(t, u, r):
                after(pe, sem(f"xe_in{u}"), r, 32)
                after(pe, sem("xeT_done"), t - 1)
                T(bank[2][:, 0:P], xe[u][:, 0:P])
                T(bank[2][:, P:2 * P], xe[u][:, ROW:ROW + P]).then_inc(sem("xeT_psum"), 1)

            def b_H(t, u, r):
                after(pe, sem("xeT_done"), t)
                after(pe, sem("w13T_done"), t)
                after(pe, sem("hh_done"), t - 1)
                for j in range(2):
                    m = pe.matmul(bank[3][:, j * P:(j + 1) * P], xeT[u][:, j * P:(j + 1) * P],
                                  w13T[u][:, j * P:(j + 1) * P], start=True, stop=True)
                m.then_inc(sem("h_psum"), 1)

            def b_HT(t, u, r):
                after(pe, sem("hh_done"), t)
                after(pe, sem("hhT_done"), t - 1)
                T(bank[4][:, 0:P], hh[u]).then_inc(sem("hhT_psum"), 1)

            def b_Y(t, u, r):
                after(pe, sem("hhT_done"), t)
                after(pe, sem("w2T_done"), t, 2)
                after(pe, sem("ye_done"), t - 1)
                pe.matmul(bank[5][:, 0:2 * P], hhT[u], w2T[u], start=True, stop=True).then_inc(sem("y_psum"), 1)

            pipeline(pe, NPAIR, RB_, [(0, b_W), (1, b_X), (2, b_HT), (1, b_H), (2, b_Y)])

            pe.wait_ge(sem("ye_done"), NPAIR)
            pe.wait_ge(sem("w2T_done"), 2 * NPAIR)

            def c_XT(t, u, r):
                after(pe, sem("cxn_done"), t)
                after(pe, sem("cxT_done"), t - 1)
                T(bank[0][:, 0:P], cxn[u]).then_inc(sem("cxT_psum"), 1)

            def c_Q(t, u, r):
                after(pe, sem("cxT_done"), t)
                after(pe, sem("qm_done"), t - 1)
                pe.matmul(bank[1][:, 0:P], wT[:, WQ * P:(WQ + 1) * P], cxT[u], start=True, stop=True
                          ).then_inc(sem("q_psum"), 1)

            def c_S(t, u, g):
                if g == 0:
                    after(pe, sem("qm_done"), t)
                    after(pe, sem("kbd_done"), t)
                if isinstance(t, int):
                    after(pe, sem("sdif_done"), 4 * t + g - 2)
                else:
                    pe.wait_ge(sem("sdif_done"), t * 4 + (g - 1))
                pe.matmul(bank[2 + g % 2][:, :], qm[u][:, g * P:(g + 1) * P], kbd[u], start=True, stop=True
                          ).then_inc(sem("s_psum"), 1)

            def c_PT(t, u, g):
                pe.wait_ge(sem("pexp_done"), t * 4 + (g + 1))
                if isinstance(t, int):
                    after(pe, sem("ppT_done"), 4 * t + g - 2)
                else:
                    pe.wait_ge(sem("ppT_done"), t * 4 + (g - 1))
                for h in range(4):
                    m = T(bank[4 + g % 2][:, h * P:(h + 1) * P], pexp[g][:, h * P:(h + 1) * P])
                m.then_inc(sem("ppT_psum"), 1)

            def c_PV(t, u, r, half):
                if half == 0:
                    pe.wait_ge(sem("ppT_done"), t * 4 + 4)
                    after(pe, sem("vbd_done"), t)
                    after(pe, sem("oT_done"), t - 1)
                for h in (2 * half, 2 * half + 1):
                    for c in range(2):
                        for g in range(4):
                            lhsT = vbd[u][:, h * P + 32 * g:h * P + 32 * g + 32] if c == 0 else \
                                vmask[:, h * P:h * P + 32]
                            m = pe.matmul(bank[6][32 * g:32 * g + 32, c * P:(c + 1) * P], lhsT,
                                          ppT[u][:, (g * 4 + h) * P:(g * 4 + h + 1) * P],
                                          start=(h == 0 and c == 0), stop=(h == 3), skip_group_check=True)
                if half == 1:
                    m.then_inc(sem("pv_psum"), 1)

            def c_OUT(t, u, r):
                after(pe, sem("oT_done"), t)
                after(pe, sem("x3_done"), t - 1)
                pe.matmul(bank[7][:, 0:P], oT[u], wT[:, WO * P:(WO + 1) * P], start=True, stop=True
                          ).then_inc(sem("c_out_psum"), 1)

            pe.wait_ge(sem("scaled"), WO_OK)
            pipeline(pe, NT, 2, [
                (1, lambda t, u, r: c_S(t, u, 0)), (1, lambda t, u, r: c_S(t, u, 1)),
                (2, lambda t, u, r: c_PV(t, u, r, 0)),
                (0, c_XT),
                (1, lambda t, u, r: c_S(t, u, 2)), (1, lambda t, u, r: c_PT(t, u, 0)),
                (2, lambda t, u, r: c_PV(t, u, r, 1)),
                (0, c_Q),
                (1, lambda t, u, r: c_S(t, u, 3)), (1, lambda t, u, r: c_PT(t, u, 1)),
                (1, lambda t, u, r: c_PT(t, u, 2)), (2, c_OUT), (1, lambda t, u, r: c_PT(t, u, 3)),
            ])

            pe.wait_ge(sem("x3_done"), NT)

            def d_T(t, u, r):
                after(pe, sem("dxn_done"), t)
                after(pe, sem("dxT_done"), t - 1)
                T(bank[0][:, 0:P], dxn[u]).then_inc(sem("dxT_psum"), 1)

            def d_R(t, u, r):
                after(pe, sem("dxT_done"), t)
                after(pe, sem("dlog_done"), t - 1)
                pe.matmul(bank[1][:, 0:P], dxT[u], rwT[:, :], start=True, stop=True).then_inc(sem("dlog_psum"), 1)
            pipeline(pe, NT, RD, [(0, d_T), (1, d_R)])

            pe.wait_ge(sem("xT2_kept"), NT)
            pe.wait_ge(sem("w_late"), 16 * 5)
            pe.wait_ge(sem("dlog_done"), NT)
            pe.wait_ge(sem("scaled"), SW_OK)
            with pe.Fori(0, NQ) as q:
                xq = xT_all[:, bass.ds(q * 512, 512)]
                for c in range(2):
                    pe.wait_ge(sem("fh_done"), 1 + (q * 2 + c))
                    pe.matmul(bank[2][:, :], sw1[:, c * P:(c + 1) * P], xq, start=True, stop=True)
                    pe.matmul(bank[3][:, :], sw3[:, c * P:(c + 1) * P], xq, start=True, stop=True
                              ).then_inc(sem("f_psum"), 1)
                pe.wait_ge(sem("fh_done"), 1 + (q * 2 + 2))
                pe.wait_ge(sem("fx_done"), 1 + (q))
                for j in range(QT):
                    for c in range(2):
                        m = pe.matmul(bank[4][:, j * P:(j + 1) * P], fh[c][:, j * P:(j + 1) * P],
                                      sw2[:, c * P:(c + 1) * P], start=(c == 0), stop=(c == 1))
                m.then_inc(sem("fy_psum"), 1)

            pe.wait_ge(sem("fx_done"), 1 + (NQ))
            with pe.Fori(0, NQ) as q:
                xq = xT_all[:, bass.ds(q * 512, 512)]

                def up(e):
                    if e >= 0:
                        pe.wait_ge(sem("eh_done"), 1 + (q * E1 + (e - 1) if e >= 1 else q * E1))
                    pe.matmul(bank[5 + e % 2][:, :], ew1[:, e * P:(e + 1) * P], xq, start=True, stop=True
                              ).then_inc(sem("eh_psum"), 1)

                def down(e):
                    pe.wait_ge(sem("eh_done"), 1 + (q * E1 + (e + 1)))
                    if e >= 1:
                        pe.wait_ge(sem("y_added"), 1 + ((q * E1 + (e - 1)) * QT))
                    else:
                        pe.wait_ge(sem("y_added"), 1 + (q * (E1 * QT)))
                    for j in range(QT):
                        m = pe.matmul(bank[4 if e % 2 else 7][:, j * P:(j + 1) * P], eh[e % 2][:, j * P:(j + 1) * P],
                                      ew2[:, e * P:(e + 1) * P], start=True, stop=True)
                    m.then_inc(sem("ey_psum"), 1)
                for e in range(E1 + 1):
                    if e < E1:
                        up(e)
                    if e >= 1:
                        down(e - 1)

        @block.scalar
        def _(act):
            start(act, "act")
            act.wait_ge(sem("pool_setup"), ROWV_OK)
            act.activation(th[:, :], rowv[:, GX:GX + 4], ACT.Tanh).then_inc(sem("th_done"), 1)
            act.wait_ge(sem("wT_zero"), 1)
            act.wait_ge(sem("wT_psum"), 3)
            act.activation(wT[:, 0:E0], bank[0][:, 0:E0], ACT.Copy).then_inc(sem("wT_done"), 1)
            act.activation(wT[:, P:4 * P], bank[0][:, P:4 * P], ACT.Copy).then_inc(sem("wT_done"), 1)
            act.activation(wT[:, 4 * P:8 * P], bank[1][:, :], ACT.Copy).then_inc(sem("wT_done"), 1)
            act.activation(rwT[:, 0:E1], bank[2][:, 0:E1], ACT.Copy).then_inc(sem("wT_done"), 1)

            def a_E(t, u, r):
                after(act, sem("T_psum"), t)
                after(act, sem("out_psum"), t - RA)
                after(act, sem("kv_psum"), t - RA)
                act.activation(cT[u], bank[0][:, P:2 * P], ACT.Copy).then_inc(sem("eT_done"), 1)
                act.activation(eT[u], bank[0][:, 0:P], ACT.Copy).then_inc(sem("eT_done"), 1)

            def a_exp(t, u, r):
                after(act, sem("max_steps"), t, 3)
                after(act, sem("prn_done"), t - RA)
                act.activation(pr[u], bank[1][:, 0:P], ACT.Exp, bias=nb[u], accum_out=ssum[u]
                               ).then_inc(sem("pr_done"), 1)

            def a_eb(t, u, r):
                after(act, sem("ngmax_done"), t)
                after(act, sem("hc_psum"), t - RA)
                act.activation(eb[u], msim[u].broadcast_to([P, P]), ACT.Exp, bias=ngmax[u]).then_inc(sem("eb_done"), 1)

            def a_prn(t, u, r):
                after(act, sem("rs_done"), t)
                after(act, sem("pT_psum"), t - RA)
                act.activation(prn[u], pr[u], ACT.Copy, scale=rs[u]).then_inc(sem("prn_done"), 1)

            def a_pT(t, u, r):
                after(act, sem("pT_psum"), t)
                after(act, sem("hqT_done"), t - RA)
                act.activation(pT[u], bank[2][:, 0:P], ACT.Copy).then_inc(sem("pT_done"), 1)

            def a_hq(t, u, r):
                after(act, sem("hqT_done"), t)
                after(act, sem("out_psum"), t - RA)
                act.activation(hq[u], bank[3][:, 0:P], ACT.Copy).then_inc(sem("hq_done"), 1)

            def a_x1T(t, u, r):
                after(act, sem("xn1T_psum"), t)
                after(act, sem("lg_psum"), t - RA)
                after(act, sem("xT_kept"), t - RA)
                act.activation(xn1T[u], bank[6][:, 0:P], ACT.Copy).then_inc(sem("xn1T_done"), 1)

            def a_lg(t, u, r):
                after(act, sem("lg_psum"), t)
                act.activation(logits[:, at(t, E0)], bank[6][:, P:P + E0], ACT.Copy).then_inc(sem("lg_done"), 1)

            def a_kv(t, u, r):
                after(act, sem("kv_psum"), t)
                act.activation(kT_all[:, at(t)], bank[7][:, 0:P], ACT.Identity, bias=bk[:, 0:1])
                act.activation(v_all[:, at(t)], bank[7][:, P:2 * P], ACT.Copy).then_inc(sem("v_done"), 1)

            act.wait_ge(sem("cols_in"), 16 * 4)
            pipeline(act, NT, RA, [(3, a_eb), (2, a_exp), (3, a_pT), (1, a_E), (5, a_x1T), (3, a_hq), (2, a_prn),
                                   (2, a_kv), (5, a_lg)])

            act.wait_ge(sem("lg_done"), NT)
            act.activation(sc, logits, ACT.Sigmoid).then_inc(sem("sc_done"), 1)

            for u in range(RA):
                act.wait_ge(sem(f"rows_out{u}"), 16 * (NT // RA))
            with act.Fori(0, NQ) as q:
                act.wait_ge(sem("sh_psum"), q + 1)
                act.wait_ge(sem("shh_done"), 1 + q)
                act.activation(sh_s, bank[0][:, :], ACT.Silu)
                act.activation(sh_u, bank[1][:, :], ACT.Copy).then_inc(sem("shu_done"), 1)
                act.wait_ge(sem("shy_psum"), q + 1)
                act.wait_ge(sem("shx_done"), 1 + q)
                act.activation(sh_y, bank[2][:, :], ACT.Copy).then_inc(sem("shy_done"), 1)

            def b_w13(t, u, r):
                after(act, sem("w13T_psum"), t)
                after(act, sem("h_psum"), t - 2)
                act.activation(w13T[u].rearrange("p (e k f) -> p k e f", e=2, k=2),
                               bank[0][:, 0:2 * P].rearrange("p (k e f) -> p k e f", k=2, e=2), ACT.Copy
                               ).then_inc(sem("w13T_done"), 1)

            def b_xeT(t, u, r):
                after(act, sem("xeT_psum"), t)
                after(act, sem("h_psum"), t - 2)
                act.activation(xeT[u], bank[2][:, 0:2 * P], ACT.Copy).then_inc(sem("xeT_done"), 1)

            def b_silu(t, u, r):
                after(act, sem("h_psum"), t)
                after(act, sem("hh_done"), t - 2)
                act.activation(sil[u].rearrange("p (e f) -> p e f", e=2),
                               bank[3][:, 0:2 * P].rearrange("p (e k f) -> p e k f", e=2, k=2)[:, :, 0, :], ACT.Silu
                               ).then_inc(sem("sil_done"), 1)

            def b_hhT(t, u, r):
                after(act, sem("hhT_psum"), t)
                after(act, sem("y_psum"), t - 2)
                act.activation(hhT[u], bank[4][:, 0:P], ACT.Copy).then_inc(sem("hhT_done"), 1)
            pipeline(act, NPAIR, RB_, [(0, b_w13), (1, b_xeT), (2, b_hhT), (1, b_silu)])

            def c_xT(t, u, r):
                after(act, sem("cxT_psum"), t)
                after(act, sem("q_psum"), t - 2)
                act.activation(cxT[u], bank[0][:, 0:P], ACT.Copy).then_inc(sem("cxT_done"), 1)

            def c_exp(t, u, g):
                act.wait_ge(sem("sdif_done"), t * 4 + (g + 1))
                after(act, sem("ppT_psum"), t - 1, 4)
                act.activation(pexp[g], sdif[g], ACT.Exp, scale=float(HD) ** -0.5).then_inc(sem("pexp_done"), 1)

            def c_ppT(t, u, g):
                act.wait_ge(sem("ppT_psum"), t * 4 + (g + 1))
                after(act, sem("pv_psum"), t - 2)
                act.activation(ppT[u][:, g * 512:(g + 1) * 512], bank[4 + g % 2][:, :], ACT.Copy
                               ).then_inc(sem("ppT_done"), 1)

            pipeline(act, NT, 2, [
                (1, lambda t, u, r: c_exp(t, u, 0)), (0, c_xT), (1, lambda t, u, r: c_exp(t, u, 1)),
                (1, lambda t, u, r: c_ppT(t, u, 0)), (1, lambda t, u, r: c_exp(t, u, 2)),
                (1, lambda t, u, r: c_ppT(t, u, 1)), (1, lambda t, u, r: c_exp(t, u, 3)),
                (1, lambda t, u, r: c_ppT(t, u, 2)), (1, lambda t, u, r: c_ppT(t, u, 3)),
            ])

            def d_t(t, u, r):
                after(act, sem("dxT_psum"), t)
                after(act, sem("dlog_psum"), t - RD)
                after(act, sem("xT2_kept"), t - RD)
                act.activation(dxT[u], bank[0][:, 0:P], ACT.Copy).then_inc(sem("dxT_done"), 1)

            def d_l(t, u, r):
                after(act, sem("dlog_psum"), t)
                act.activation(dlog[:, at(t, E1)], bank[1][:, 0:E1], ACT.Copy).then_inc(sem("dlog_done"), 1)
            pipeline(act, NT, RD, [(0, d_t), (1, d_l)])
            act.wait_ge(sem("dlog_done"), NT)
            act.activation(dsc, dlog, ACT.Sigmoid).then_inc(sem("dsc_done"), 1)
            with act.Fori(0, NQ) as q:
                for c in range(2):
                    act.wait_ge(sem("f_psum"), q * 2 + (c + 1))
                    act.wait_ge(sem("fh_done"), 1 + (q * 2 + c))
                    act.activation(fg[c], bank[2][:, :], ACT.Silu).then_inc(sem("fg_done"), 1)
            with act.Fori(0, NQ) as q:
                for e in range(E1):
                    act.wait_ge(sem("eh_psum"), q * E1 + (e + 1))
                    act.wait_ge(sem("ey_psum"), 1 + (q * E1 + (e - 1) if e >= 1 else q * E1))
                    act.activation(eh[e % 2], bank[5 + e % 2][:, :], ACT.Gelu).then_inc(sem("eh_done"), 1)

        @block.vector
        def _(dve):
            k = [0]

            def link(ins):
                k[0] += 1
                ins.then_inc(sem("dve_setup"), 1)
                dve.wait_ge(sem("dve_setup"), k[0])

            start(dve, "dve")
            dve.memset(rwT[:, :], 0.0)
            dve.memset(wT[:, 0:P], 0.0).then_inc(sem("wT_zero"), 1)
            dve.wait_ge(sem("th_done"), 1)
            dve.tensor_scalar(bqv_row[:, :], rowv[:, BQV:BQV + P], th[:, 0:1], None, ALU.mult
                              ).then_inc(sem("scaled"), 1)
            dve.wait_ge(sem("wqv_in"), 16)
            dve.tensor_scalar(wqv[:, :], wqv[:, :], th[:, 0:1], None, ALU.mult).then_inc(sem("scaled"), 1)
            dve.wait_ge(sem("bvo_psum"), 1)
            link(dve.tensor_tensor(bo_row[:, :], bank[3][:, 0:P], rowv[:, BO:BO + P], ALU.add))
            dve.tensor_scalar(bo_row[:, :], bo_row[:, :], th[:, 1:2], None, ALU.mult).then_inc(sem("scaled"), 1)
            dve.tensor_scalar(wT[:, WO * P:(WO + 1) * P], wT[:, WO * P:(WO + 1) * P], th[:, 1:2], None, ALU.mult
                              ).then_inc(sem("scaled"), 1)
            dve.tensor_scalar(wT[:, SD * P:(SD + 1) * P], wT[:, SD * P:(SD + 1) * P], th[:, 2:3], None, ALU.mult
                              ).then_inc(sem("scaled"), 1)
            dve.wait_ge(sem("pool_setup"), CONSTS_OK)
            link(dve.tensor_scalar(imod8[:, :], imod8[:, :], 7, None, ALU.bitwise_and))
            link(dve.tensor_scalar(mod8[:, :], imod8[:, :], 0, None, ALU.is_equal))
            link(dve.tensor_scalar(ihead[:, :], ihead[:, :], 3, 3, ALU.logical_shift_right, ALU.bitwise_and))
            dve.tensor_scalar(head_m[:, :], ihead[:, :], 0, None, ALU.is_equal).then_inc(sem("scaled"), 1)

            def norm_steps(src, s_, m_, v_, stats, first=None):
                def sums(t, u, r):
                    if first:
                        first(t, u, r)
                    hold(dve, sem("dve_passed"))
                    dve.bn_stats(s_[u], src[:, at(t)]).then_inc(sem(stats), 1)

                def moments(t, u, r):
                    dve.wait_ge(sem(stats), t * 3 + 1)
                    hold(dve, sem("dve_passed"))
                    dve.bn_aggr(m_[u], s_[u]).then_inc(sem(stats), 1)

                def variance(t, u, r):
                    dve.wait_ge(sem(stats), t * 3 + 2)
                    dve.tensor_scalar(v_[u], m_[u][:, 1:2], EPS, None, ALU.add).then_inc(sem(stats), 1)
                return sums, moments, variance

            def x_there(t, u, r):
                if isinstance(t, int) and t in (0, 8):
                    dve.wait_ge(sem("x_first" if t == 0 else "x_rest"), 16)

            a_sums, a_moments, a_var = norm_steps(x_all, st, mv, ve, "ve_done", x_there)

            def a_xn(t, u, r):
                after(dve, sem("rstd_done"), t)
                after(dve, sem("hc_psum"), t - RA)
                dve.tensor_scalar(xn[u], x_all[:, at(t)], mv[u][:, 0:1], rstd[u], ALU.subtract, ALU.mult
                                  ).then_inc(sem("xn_done"), 1)

            def a_cw(t, u, r):
                dve.wait_ge(sem("eT_done"), t * 2 + 1)
                after(dve, sem("sim_psum"), t - RA)
                dve.tensor_scalar(cw[u], cT[u], wcol[:, 2:3], wcol[:, 0:1], ALU.mult, ALU.add
                                  ).then_inc(sem("cw_done"), 1)

            def a_max(t, u, r):
                after(dve, sem("sim_psum"), t)
                dve.tensor_reduce(mraw[u], bank[1][:, 0:P], AX.X, ALU.max).then_inc(sem("max_steps"), 1)

            def a_msim(t, u, r):
                dve.wait_ge(sem("max_steps"), t * 3 + 1)
                dve.tensor_scalar(msim[u], mraw[u], rowv[:, BSIM:BSIM + 1], None, ALU.add).then_inc(sem("max_steps"), 1)

            def a_nb(t, u, r):
                dve.wait_ge(sem("max_steps"), t * 3 + 2)
                dve.tensor_scalar(nb[u], msim[u], -1.0, rowv[:, BSIM:BSIM + 1], ALU.mult, ALU.add
                                  ).then_inc(sem("max_steps"), 1)

            def a_rs(t, u, r):
                after(dve, sem("pr_done"), t)
                dve.reciprocal(rs[u], ssum[u]).then_inc(sem("rs_done"), 1)

            def a_ng(t, u, r):
                after(dve, sem("gmax_done"), t)
                dve.tensor_scalar(ngmax[u], gmax[u], -1.0, None, ALU.mult).then_inc(sem("ngmax_done"), 1)

            def a_hcr(t, u, r):
                after(dve, sem("hc_psum"), t)
                dve.reciprocal(hcr[u], bank[4][:, P:P + 1]).then_inc(sem("hc_steps"), 1)

            def a_hc(t, u, r):
                dve.wait_ge(sem("hc_steps"), t * 3 + 1)
                dve.tensor_scalar(hc[u], bank[4][:, 0:1], hcr[u], None, ALU.mult).then_inc(sem("hc_steps"), 1)

            def a_ec(t, u, r):
                dve.wait_ge(sem("hc_steps"), t * 3 + 2)
                after(dve, sem("out_psum"), t - RA)
                dve.tensor_scalar(ecT[u], eT[u], hc[u], None, ALU.mult).then_inc(sem("hc_steps"), 1)

            def a_eh(t, u, r):
                after(dve, sem("hq_done"), t)
                dve.tensor_tensor(ehT[u], eT[u], hq[u], ALU.mult).then_inc(sem("ehT_done"), 1)

            def a_x1(t, u, r):
                after(dve, sem("out_psum"), t)
                after(dve, sem("xb_done"), t)
                dve.tensor_tensor(x_all[:, at(t)], bank[5][:, 0:P], xb[u], ALU.add).then_inc(sem("x1_done"), 1)

            def x1_there(t, u, r):
                after(dve, sem("x1_done"), t)

            b_sums, b_moments, b_var = norm_steps(x_all, st1, mv1, ve1, "ve1_done", x1_there)

            def a_xn1(t, u, r):
                after(dve, sem("rstd1_done"), t)
                after(dve, sem("xn1T_psum"), t - RA)
                after(dve, sem(f"rows_out{u}"), r - 1, 16)
                dve.tensor_scalar(xn1[u], x_all[:, at(t)], mv1[u][:, 0:1], rstd1[u], ALU.subtract, ALU.mult
                                  ).then_inc(sem("xn1_done"), 1)

            pipeline(dve, NT, RA, [
                (3, a_ng), (1, a_xn), (2, a_max), (4, a_x1), (2, a_msim), (4, b_sums), (2, a_nb), (4, b_moments),
                (1, a_cw), (4, b_var), (0, a_sums), (3, a_hcr), (2, a_rs), (0, a_moments), (3, a_hc), (4, a_xn1),
                (0, a_var), (3, a_ec), (3, a_eh)])

            dve.wait_ge(sem("sc_done"), 1)
            v3 = lambda b, n: b.rearrange("p (t e) -> p t e", e=n)
            eb_b = rowv[:, EB:EB + E0].rearrange("p (a e) -> p a e", a=1).broadcast_to([P, NT, E0])
            link(dve.tensor_tensor(v3(sfc, E0), v3(sc, E0), eb_b, ALU.add))
            s8v = sfc.rearrange("p (n k) -> p n k", k=8)
            h1, l1 = (b.rearrange("p (n k) -> p n k", k=4) for b in (t1, t2))
            for hf in range(2):
                n0 = hf * (NT * G0 // 2)
                n1 = n0 + NT * G0 // 2
                a_, b_ = s8v[:, n0:n1, 0:4], s8v[:, n0:n1, 4:8]
                hi4, lo4 = t1.rearrange("p (n k) -> p n k", k=4)[:, 0:128], t2.rearrange("p (n k) -> p n k", k=4)[:, 0:128]
                link(dve.tensor_tensor(hi4, a_, b_, ALU.max))
                link(dve.tensor_tensor(lo4, a_, b_, ALU.min))
                hi2 = t1[:, 512:768].rearrange("p (n k) -> p n k", k=2)
                mi2 = t1[:, 768:1024].rearrange("p (n k) -> p n k", k=2)
                lo2 = t2[:, 512:768].rearrange("p (n k) -> p n k", k=2)
                se2 = t2[:, 768:1024].rearrange("p (n k) -> p n k", k=2)
                link(dve.tensor_tensor(hi2, hi4[:, :, 0:2], hi4[:, :, 2:4], ALU.max))
                link(dve.tensor_tensor(mi2, hi4[:, :, 0:2], hi4[:, :, 2:4], ALU.min))
                link(dve.tensor_tensor(lo2, lo4[:, :, 0:2], lo4[:, :, 2:4], ALU.max))
                link(dve.tensor_tensor(se2, mi2, lo2, ALU.max))
                q3 = t3.rearrange("p (c n a) -> p c n a", c=4, a=1)
                link(dve.tensor_tensor(q3[:, 0], hi2[:, :, 0:1], hi2[:, :, 1:2], ALU.max))
                link(dve.tensor_tensor(q3[:, 1], hi2[:, :, 0:1], hi2[:, :, 1:2], ALU.min))
                link(dve.tensor_tensor(q3[:, 2], se2[:, :, 0:1], se2[:, :, 1:2], ALU.max))
                link(dve.tensor_tensor(q3[:, 3], q3[:, 1], q3[:, 2], ALU.max))
                link(dve.tensor_tensor(gs[:, n0:n1].rearrange("p (n a) -> p n a", a=1), q3[:, 0], q3[:, 3], ALU.add))
            link(dve.memset(gsx, BIG))
            link(dve.memset(g8x, BIG))
            gsxv, g8v, g8xv, glv, gmv = v3(gsx, 12), v3(g8, 8), v3(g8x, 8), v3(gleft, 12), v3(gmask, 8)
            tmv, k8v, klv = v3(tmp, E0), v3(k8, 8), v3(kleft, E0)
            with dve.Fori(0, NQ) as q:
                base = q * 9
                n = [0]

                def step(ins):
                    n[0] += 1
                    ins.then_inc(sem("route_steps"), 1)
                    dve.wait_ge(sem("route_steps"), base + n[0])

                step(dve.tensor_copy(gsxv[:, :, 0:8], v3(gs[:, bass.ds(q * (QT * 8), QT * 8)], 8)))
                hold(dve, sem("dve_passed"))
                for j in range(QT):
                    m = dve.max(g8v[:, j], gsxv[:, j, 0:8])
                step(m)
                step(dve.tensor_copy(g8xv[:, :, 0:4], g8v[:, :, 0:4]))
                hold(dve, sem("dve_passed"))
                for j in range(QT):
                    m = dve.match_replace(out=glv[:, j], in_to_replace=g8xv[:, j], in_values=gsxv[:, j], imm_value=GONE)
                step(m)
                step(dve.tensor_scalar(gmv, glv[:, :, 0:8], GONE / 2, None, ALU.is_lt))
                step(dve.tensor_tensor(tmp.rearrange("p (n k) -> p n k", k=8),
                                       sfc[:, bass.ds(q * (QT * E0), QT * E0)].rearrange("p (n k) -> p n k", k=8),
                                       gmask.rearrange("p (n a) -> p n a", a=1).broadcast_to([P, QT * G0, 8]),
                                       ALU.mult))
                hold(dve, sem("dve_passed"))
                for j in range(QT):
                    m = dve.max(k8v[:, j], tmv[:, j])
                step(m)
                hold(dve, sem("dve_passed"))
                for j in range(QT):
                    m = dve.match_replace(out=klv[:, j], in_to_replace=k8v[:, j], in_values=tmv[:, j], imm_value=GONE)
                step(m)
                dve.tensor_scalar(m_bf[:, bass.ds(q * (QT * E0), QT * E0)], kleft, GONE / 2, None, ALU.is_lt
                                  ).then_inc(sem("m_done"), 1)
                step(dve.tensor_copy(rsum[:, 0:1], g8[:, 0:1]))
                assert n[0] == 9
            dve.wait_ge(sem("m_done"), NQ)
            link(dve.tensor_tensor(wr, sc, m_bf, ALU.mult))
            link(dve.tensor_reduce(rsum, v3(wr, E0), AX.X, ALU.add))
            link(dve.tensor_scalar(rsum, rsum, 1e-20, None, ALU.add))
            link(dve.reciprocal(rsum, rsum))
            link(dve.tensor_scalar(rsum, rsum, ROUTE_SCALE, th[:, 2:3], ALU.mult, ALU.mult))
            dve.tensor_tensor(v3(wr, E0), v3(wr, E0), rsum.rearrange("p (t a) -> p t a", a=1).broadcast_to([P, NT, E0]),
                              ALU.mult).then_inc(sem("wr_done"), 1)

            hv = hot_v.rearrange("p (j v x) -> p j v x", j=QT, v=2)
            hbx = hot_b.rearrange("p (j x) -> p j x", j=QT)
            with dve.Fori(0, NQ) as q:
                base = q * 6 + 9 * NQ
                n = [0]

                def step(ins):
                    n[0] += 1
                    ins.then_inc(sem("route_steps"), 1)
                    dve.wait_ge(sem("route_steps"), base + n[0])

                dve.wait_ge(sem("pos_psum"), q + 1)
                dve.scalar_tensor_tensor(out=key, in0=m_bf[:, bass.ds(q * (QT * E0), QT * E0)], scalar=-8192.0,
                                         in1=bank[5][:, 0:QT * E0], op0=ALU.mult, op1=ALU.add
                                         ).then_inc(sem("key_done"), 1)
                dve.wait_ge(sem("key_done"), 1 + (q + 1))
                step(dve.tensor_scalar(da_i, key, 3, None, ALU.arith_shift_right))
                step(dve.tensor_scalar(db_i, key, 7, None, ALU.bitwise_and))
                step(dve.tensor_scalar(da, da_i, 1024.0, None, ALU.add))
                step(dve.tensor_copy(db, db_i))
                dve.wait_ge(sem("lists_psum"), 1 + (q))
                def digit(d, n_, buf, iot):
                    return dve.tensor_tensor(
                        buf, d.rearrange("p (a e) -> p a e", a=1).broadcast_to([P, n_, E0]),
                        iot[:, :].rearrange("p (a e) -> p a e", e=E0), ALU.is_equal)
                for j in range(QT):
                    m = digit(db[:, j * E0:(j + 1) * E0], 8, hbx[:, j].rearrange("p (b e) -> p b e", e=E0), iota_b)
                step(m)
                for j in range(QT):
                    dve.tensor_tensor(
                        hot_a.rearrange("p (j g a e) -> p j g a e", j=QT, g=8, a=16)[:, j],
                        da[:, j * E0:(j + 1) * E0].rearrange("p (g a e) -> p g a e", g=8, a=1
                                                             ).broadcast_to([P, 8, 16, 8]),
                        iota_a[:, :].rearrange("p (g a e) -> p g a e", g=8, a=16), ALU.is_equal)
                step(dve.tensor_scalar(hv[:, :, 0, :], hbx, pcol[:, 0:1], None, ALU.mult))
                assert n[0] == 6
                for j in range(QT):
                    m = dve.tensor_scalar(hv[:, j, 1, :], hbx[:, j], tile_no[:, bass.ds(q * QT + j, 1)], None, ALU.mult)
                m.then_inc(sem("hot_done"), 1)
            dve.wait_ge(sem("lists_psum"), 1 + (NQ))
            for b in range(2):
                bv_ = bank[6 + b][:, :].rearrange("p (g v x) -> p g v x", g=4, v=2)
                tv = [t_[:, b * 256:(b + 1) * 256].rearrange("p (g x) -> p g x", g=4) for t_ in tbl]
                link(dve.tensor_scalar(tv[0], bv_[:, :, 1, :], float(P), None, ALU.mult))
                link(dve.tensor_tensor(tv[1], bv_[:, :, 0, :], tv[0], ALU.add))
            link(dve.tensor_tensor(tbl[2][:, :].rearrange("p (x e) -> p x e", e=8),
                                   tbl[1][:, :].rearrange("p (x e) -> p x e", e=8),
                                   mod8[:, :].rearrange("p (a e) -> p a e", a=1).broadcast_to([P, 64, 8]), ALU.mult))
            dve.tensor_copy(filled[:, 0:1], mod8[:, 0:1]).then_inc(sem("tbl_done"), 1)
            dve.wait_ge(sem("slot_psum"), 1)
            link(dve.tensor_tensor(tbl[0][:, :].rearrange("p (g b e) -> p g b e", g=8, b=8),
                                   bank[3][:, :].rearrange("p (g b e) -> p g b e", g=8, b=8),
                                   mod8[:, :].rearrange("p (a b c) -> p a b c", a=1, c=1).broadcast_to([P, 8, 8, 8]),
                                   ALU.mult))
            link(dve.tensor_reduce(slot_tok[:, :].rearrange("p (g e) -> p g e", g=8),
                                   tbl[0][:, :].rearrange("p (g b e) -> p g e b", g=8, b=8), AX.X, ALU.add))
            dve.tensor_copy(gidx[:, :], slot_tok[:, :]).then_inc(sem("idx_done"), 1)
            dve.wait_ge(sem("cnt_psum"), 1)
            link(dve.tensor_copy(cnt[:, :], bank[5][:, 0:E0]))
            link(dve.tensor_scalar(filled[:, :], cnt[:, :], pcol[:, 0:1], None, ALU.is_gt))
            link(dve.tensor_scalar(slot_row[:, :], slot_tok[:, :], dump_row[:, 0:1], None, ALU.subtract))
            link(dve.tensor_tensor(slot_row[:, :], slot_row[:, :], filled[:, :], ALU.mult))
            link(dve.tensor_scalar(slot_row[:, :], slot_row[:, :], dump_row[:, 0:1], None, ALU.add))
            dve.tensor_copy(sidx[:, :], slot_row[:, :]).then_inc(sem("idx_done"), 1)
            dve.tensor_copy(rsum[:, 1:2], cnt[:, 0:1]).then_inc(sem("slot_done"), 1)

            def b_w2(t, u, r):
                if isinstance(t, int) and t < 2:
                    dve.wait_ge(sem("w2T_zero"), 2)
                after(dve, sem("w2T_psum"), t)
                after(dve, sem("y_psum"), t - 2)
                dve.tensor_copy(w2T[u][0:F0, 0:P], bank[1][0:F0, 0:P]).then_inc(sem("w2T_done"), 1)
                dve.tensor_copy(w2T[u][F0:P, P:2 * P], bank[1][F0:P, 0:P]).then_inc(sem("w2T_done"), 1)

            def b_hh(t, u, r):
                after(dve, sem("sil_done"), t)
                after(dve, sem("hhT_psum"), t - 2)
                dve.tensor_tensor(hh[u].rearrange("p (e f) -> p e f", e=2),
                                  bank[3][:, 0:2 * P].rearrange("p (e k f) -> p e k f", e=2, k=2)[:, :, 1, :],
                                  sil[u].rearrange("p (e f) -> p e f", e=2), ALU.mult).then_inc(sem("hh_done"), 1)

            def b_gi(t, u, r):
                after(dve, sem(f"xe_in{u}"), r - 1, 32)
                dve.tensor_copy(gi[u], gidx[:, at(t, 2)]).then_inc(sem("gi_done"), 1)

            def b_y(t, u, r):
                after(dve, sem("y_psum"), t)
                for j in range(2):
                    after(dve, sem(f"acc_done{j}"), t - RB_, 16)
                dve.tensor_copy(si[u], sidx[:, at(t, 2)])
                for j in range(2):
                    e = 2 * t + j if isinstance(t, int) else t * 2 + j
                    col = j * ROW + P + e
                    w = xe[u][:, col:col + 1] if isinstance(t, int) else xe[u][:, bass.ds(col, 1)]
                    m = dve.tensor_scalar(ye[u][:, j * P:(j + 1) * P], bank[5][:, j * P:(j + 1) * P], w, None, ALU.mult)
                m.then_inc(sem("ye_done"), 1)
            dve.wait_ge(sem("idx_done"), 2)
            pipeline(dve, NPAIR, RB_, [(0, b_gi), (0, b_w2), (1, b_hh), (2, b_y)])

            dve.wait_ge(sem("scaled"), HEAD_OK)

            def x2_there(t, u, r):
                after(dve, sem("x2_done"), t)

            c_sums, c_moments, c_var = norm_steps(x_all, cst, cmv, cve, "cve_done", x2_there)

            def c_xn(t, u, r):
                after(dve, sem("crs_done"), t)
                after(dve, sem("cxT_psum"), t - 2)
                dve.tensor_scalar(cxn[u], x_all[:, at(t)], cmv[u][:, 0:1], crs[u], ALU.subtract, ALU.mult
                                  ).then_inc(sem("cxn_done"), 1)

            def c_qm(t, u, r):
                after(dve, sem("q_psum"), t)
                after(dve, sem("s_psum"), t - 2, 4)
                dve.scalar_tensor_tensor(
                    out=qm[u].rearrange("p (g q) -> p g q", g=4),
                    in0=bank[1][:, 0:P].rearrange("p (a q) -> p a q", a=1).broadcast_to([P, 4, P]), scalar=bq[:, 0:1],
                    in1=group_m[:, :].rearrange("p (g a) -> p g a", a=1).broadcast_to([P, 4, P]),
                    op0=ALU.add, op1=ALU.mult).then_inc(sem("qm_done"), 1)

            def c_max(t, u, g):
                dve.wait_ge(sem("s_psum"), t * 4 + (g + 1))
                dve.tensor_reduce(smax[u][:, g * 4:g * 4 + 4], bank[2 + g % 2][:, :].rearrange("p (h k) -> p h k", h=4),
                                  AX.X, ALU.max).then_inc(sem("smax_done"), 1)

            def c_dif(t, u, g):
                dve.wait_ge(sem("smax_done"), t * 4 + (g + 1))
                after(dve, sem("pexp_done"), t - 1, 4)
                dve.tensor_tensor(sdif[g].rearrange("p (h k) -> p h k", h=4),
                                  bank[2 + g % 2][:, :].rearrange("p (h k) -> p h k", h=4),
                                  smax[u][:, g * 4:g * 4 + 4].rearrange("p (h a) -> p h a", a=1).broadcast_to([P, 4, P]),
                                  ALU.subtract).then_inc(sem("sdif_done"), 1)

            def c_o(t, u, r):
                after(dve, sem("pv_psum"), t)
                dve.reciprocal(rden[u], bank[6][:, P:2 * P]).then_inc(sem("rden_done"), 1)

            def c_o2(t, u, r):
                after(dve, sem("rden_done"), t)
                after(dve, sem("c_out_psum"), t - 2)
                dve.tensor_tensor(oT[u], bank[6][:, 0:P], rden[u], ALU.mult).then_inc(sem("oT_done"), 1)

            def c_x3(t, u, r):
                after(dve, sem("c_out_psum"), t)
                after(dve, sem("x2b_done"), t)
                dve.tensor_tensor(x_all[:, at(t)], bank[7][:, 0:P], x2b[u], ALU.add).then_inc(sem("x3_done"), 1)

            pipeline(dve, NT, 2, [
                (1, lambda t, u, r: c_max(t, u, 0)), (1, lambda t, u, r: c_max(t, u, 1)),
                (0, c_sums), (0, c_moments), (0, c_var),
                (1, lambda t, u, r: c_dif(t, u, 0)), (1, lambda t, u, r: c_dif(t, u, 1)), (0, c_xn),
                (1, lambda t, u, r: c_max(t, u, 2)), (2, c_o), (1, lambda t, u, r: c_dif(t, u, 2)), (2, c_o2),
                (1, lambda t, u, r: c_max(t, u, 3)), (0, c_qm), (1, lambda t, u, r: c_dif(t, u, 3)), (2, c_x3),
            ])

            dve.wait_ge(sem("w_late"), 16 * 5)
            dve.tensor_scalar(sw2[:, :], sw2[:, :], th[:, 3:4], None, ALU.mult).then_inc(sem("scaled"), 1)
            dve.tensor_scalar(ew2[:, :], ew2[:, :], th[:, 3:4], None, ALU.mult).then_inc(sem("scaled"), 1)

            def x3_there(t, u, r):
                if isinstance(t, int) and t == 0:
                    dve.wait_ge(sem("x3_done"), NT)

            d_sums, d_moments, d_var = norm_steps(x_all, dst, dmv, dve_, "dve_done", x3_there)

            def d_xn(t, u, r):
                after(dve, sem("drs_done"), t)
                after(dve, sem("dxT_psum"), t - RD)
                dve.tensor_scalar(dxn[u], x_all[:, at(t)], dmv[u][:, 0:1], drs[u], ALU.subtract, ALU.mult
                                  ).then_inc(sem("dxn_done"), 1)
            pipeline(dve, NT, RD, [(0, d_sums), (1, d_xn), (0, d_moments), (0, d_var)])

            selv, s8v_, s8xv, slv = v3(selx, 14), v3(s8, 8), v3(s8x, 8), v3(sleft, 14)
            link(dve.memset(selx, BIG))
            link(dve.memset(s8x, BIG))
            dve.wait_ge(sem("dsc_done"), 1)
            link(dve.tensor_tensor(selv[:, :, 0:8], v3(dsc, E1),
                                   rowv[:, RB:RB + E1].rearrange("p (a e) -> p a e", a=1).broadcast_to([P, NT, E1]),
                                   ALU.add))
            for t in range(NT):
                m = dve.max(s8v_[:, t], selv[:, t, 0:8])
            link(m)
            link(dve.tensor_copy(s8xv[:, :, 0:2], s8v_[:, :, 0:2]))
            for t in range(NT):
                m = dve.match_replace(out=slv[:, t], in_to_replace=s8xv[:, t], in_values=selv[:, t], imm_value=GONE)
            link(m)
            link(dve.tensor_scalar(v3(dmask, E1), slv[:, :, 0:8], GONE / 2, None, ALU.is_lt))
            link(dve.tensor_tensor(dgat, dsc, dmask, ALU.mult))
            link(dve.tensor_reduce(dden, v3(dgat, E1), AX.X, ALU.add))
            link(dve.tensor_scalar(dok, dden, 1e-9, None, ALU.is_gt))
            link(dve.tensor_scalar(dno, dok, -0.5, 0.5, ALU.mult, ALU.add))
            link(dve.tensor_scalar(dden, dden, 1e-9, None, ALU.add))
            link(dve.reciprocal(dden, dden))
            link(dve.tensor_tensor(dden, dden, dok, ALU.mult))
            bc = lambda b: b.rearrange("p (t a) -> p t a", a=1).broadcast_to([P, NT, E1])
            link(dve.tensor_tensor(v3(dgat, E1), v3(dgat, E1), bc(dden), ALU.mult))
            link(dve.tensor_tensor(v3(dalt, E1), v3(dmask, E1), bc(dno), ALU.mult))
            link(dve.tensor_tensor(dgat, dgat, dalt, ALU.add))

            with dve.Fori(0, NQ) as q:
                for c in range(2):
                    dve.wait_ge(sem("fg_done"), q * 2 + (c + 1))
                    dve.wait_ge(sem("fy_psum"), 1 + (q))
                    dve.tensor_tensor(fh[c], bank[3][:, :], fg[c], ALU.mult).then_inc(sem("fh_done"), 1)
                dve.wait_ge(sem("fy_psum"), 1 + (q + 1))
                xq = x_all[:, bass.ds(q * 512, 512)]
                dve.tensor_tensor(xq, bank[4][:, :], xq, ALU.add).then_inc(sem("fx_done"), 1)
            dve.wait_ge(sem("fx_done"), 1 + (NQ))
            with dve.Fori(0, NQ) as q:
                for e in range(E1):
                    dve.wait_ge(sem("ey_psum"), 1 + (q * E1 + (e + 1)))
                    dve.wait_ge(sem("y_added"), 1 + ((q * E1 + e) * QT))
                    for j in range(QT):
                        xt = x_all[:, bass.ds((q * QT + j) * P, P)]
                        dve.scalar_tensor_tensor(out=xt, in0=bank[4 if e % 2 else 7][:, j * P:(j + 1) * P],
                                                 scalar=dgat[:, bass.ds((q * QT + j) * E1 + e, 1)], in1=xt,
                                                 op0=ALU.mult, op1=ALU.add).then_inc(sem("y_added"), 1)


_INS = ['x', 'ctx_1024', 'g_xattn', 'g_ffn', 'L0_xattn_w_sim', 'L0_xattn_b_sim', 'L0_xattn_W_qv', 'L0_xattn_b_qv',
        'L0_ffn_gate_weight', 'L0_ffn_e_bias', 'L0_ffn_w1', 'L0_ffn_w2', 'L0_ffn_w3', 'L0_ffn_shared_gate',
        'L0_ffn_shared_up', 'L0_ffn_shared_down', 'L1_xattn_Wq', 'L1_xattn_bq', 'L1_xattn_Wk', 'L1_xattn_bk',
        'L1_xattn_Wv', 'L1_xattn_bv', 'L1_xattn_Wo', 'L1_xattn_bo', 'L1_ffn_router_w', 'L1_ffn_router_bias',
        'L1_ffn_sw1', 'L1_ffn_sw3', 'L1_ffn_sw2', 'L1_ffn_ew1', 'L1_ffn_ew2']


def kernel(**inputs):
    import numpy as _np
    import concourse.bacc as _bacc
    from concourse import mybir as _mybir
    from concourse.bass_utils import run_bass_kernel_spmd as _run

    nc = _bacc.Bacc("TRN2", target_bir_lowering=False, num_devices=1)
    arrays, aps = {}, {}
    for name in _INS:
        a = _np.ascontiguousarray(inputs[name])
        arrays[f"in_{name}"] = a
        aps[name] = nc.dram_tensor(f"in_{name}", a.shape, _mybir.dt.from_np(a.dtype), kind="ExternalInput").ap()
    out = nc.dram_tensor("out_0", (NT, P, P), _mybir.dt.float32, kind="ExternalOutput").ap()
    build(nc, aps, out)
    r = _run(nc, [arrays], core_ids=[0])
    return r.results[0]["out_0"]
```

```python
from contextlib import ExitStack

import concourse.bass as bass
from concourse import mybir

F32 = mybir.dt.float32
BF16 = mybir.dt.bfloat16
I32 = mybir.dt.int32
ALU = mybir.AluOpType
ACT = mybir.ActivationFunctionType
AX = mybir.AxisListType

P = 128
NT = 32
QT = 4
NQ = NT // QT
E0 = 64
F0 = 64
G0 = 8
CAP = 128
NPAIR = E0 // 2
E1 = 8
HEADS = 16
HD = P // HEADS
EPS = 1e-5
ROUTE_SCALE = 2.5
BIG = 1e30
GONE = -1e30
ROW = P + E0
NROWS = NT * P + P


def at(t, n=P):
    return slice(t * n, (t + 1) * n) if isinstance(t, int) else bass.ds(t * n, n)


def after(eng, sem, t, per=1):
    if isinstance(t, int) and t < 0:
        return
    eng.wait_ge(sem, t * per + per)


def hold(eng, passed):
    eng.sem_inc(passed, 1)


def pipeline(eng, count, ring, stages):
    last = max(lag for lag, _ in stages)
    first = -(-(last + ring) // ring) * ring
    turns = (count - first) // ring

    def one(s):
        for lag, step in stages:
            t = s - lag
            if 0 <= t < count:
                step(t, t % ring, t // ring)

    for s in range(first):
        one(s)
    with eng.Fori(0, turns) as i:
        for v in range(ring):
            for lag, step in stages:
                c = first + v - lag
                step(i * ring + c, c % ring, i + c // ring)
    for s in range(first + turns * ring, count + last):
        one(s)


def build(nc, A, out, dbg=None):
    ctx = ExitStack()
    with ctx:
        def sb(name, cols, dt=F32, parts=P):
            return ctx.enter_context(nc.sbuf_tensor(name, [parts, cols], dt))

        sems = {}

        def sem(name):
            if name not in sems:
                sems[name] = ctx.enter_context(nc.semaphore(name))
            return sems[name]

        bank = [ctx.enter_context(nc.psum_tensor(f"bank{k}", [P, 512], F32)) for k in range(8)]

        rows_dram = nc.dram_tensor("token_rows", (NT * P, ROW), F32).ap()
        acc_dram = [nc.dram_tensor(f"expert_sums{j}", (NROWS, P), F32).ap() for j in range(2)]

        x_all = sb("x_all", NT * P)
        xT_all = sb("xT_all", NT * P)
        kT_all = sb("kT_all", NT * P)
        v_all = sb("v_all", NT * P)

        ident = sb("ident", P)
        ones = sb("ones", P)
        ones_bf = sb("ones_bf", P, BF16)
        tri_bf = sb("tri_bf", P, BF16)
        ipart = sb("ipart", 1, I32)
        pcol = sb("pcol", 1)
        dump_row = sb("dump_row", 1)
        tile_no = sb("tile_no", NT)
        itile = sb("itile", NT, I32)
        iota_a = sb("iota_a", 16 * E0, BF16)
        iota_b = sb("iota_b", 8 * E0, BF16)
        mod8 = sb("mod8", 8)
        imod8 = sb("imod8", 8, I32)
        same8 = sb("same8", P)
        head_m = sb("head_m", 4)
        ihead = sb("ihead", 4, I32)
        group_m = sb("group_m", 4)
        vmask = sb("vmask", 4 * P)
        half_pow = sb("half_pow", 4)
        zeros = sb("zeros", 1408)

        rowin = sb("rowin", 512, F32)
        rowv = sb("rowv", 512)
        BQV, EB, BO, RB, BSIM, GX, GF, BV = 0, 128, 192, 320, 328, 329, 331, 333
        th = sb("th", 4)
        wcol = sb("wcol", 3)
        bq = sb("bq", 1)
        bk = sb("bk", 1)
        bv = sb("bv", 1)
        w2b = sb("w2b", P)
        wqv = sb("wqv", 4 * P)
        wnat = sb("wnat", 8 * P)
        wT = sb("wT", 8 * P)
        GATE, SG, SU, SD, WQ, WK, WV, WO = range(8)
        rw_nat = sb("rw_nat", P)
        rwT = sb("rwT", P)
        bqv_row = sb("bqv_row", P)
        bo_row = sb("bo_row", P)
        bv_rep = sb("bv_rep", P)
        sw1 = sb("sw1", 256)
        sw3 = sb("sw3", 256)
        sw2 = sb("sw2", 256)
        ew1 = sb("ew1", E1 * P)
        ew2 = sb("ew2", E1 * P)

        arena = sb("arena", 26200)
        used = [0]

        def carve(cols, dt=F32):
            words = cols if dt in (F32, I32) else (cols + 1) // 2
            a = arena[:, used[0]:used[0] + words]
            used[0] += words
            assert used[0] <= 26200, used[0]
            return a if dt == F32 else a.bitcast(dt)

        RA = 4
        ctx_in = [carve(P) for _ in range(RA)]
        xn = [carve(P) for _ in range(RA)]
        eT = [carve(P) for _ in range(RA)]
        cT = [carve(P) for _ in range(RA)]
        cw = [carve(P) for _ in range(RA)]
        st = [carve(6) for _ in range(RA)]
        mv = [carve(2) for _ in range(RA)]
        ve = [carve(1) for _ in range(RA)]
        rstd = [carve(1) for _ in range(RA)]
        mraw = [carve(1) for _ in range(RA)]
        msim = [carve(1) for _ in range(RA)]
        nb = [carve(1) for _ in range(RA)]
        gmax = [carve(1) for _ in range(RA)]
        ngmax = [carve(1) for _ in range(RA)]
        eb = [carve(P) for _ in range(RA)]
        pr = [carve(P) for _ in range(RA)]
        prn = [carve(P) for _ in range(RA)]
        ssum = [carve(1) for _ in range(RA)]
        rs = [carve(1) for _ in range(RA)]
        pT = [carve(P) for _ in range(RA)]
        hq = [carve(P) for _ in range(RA)]
        ehT = [carve(P) for _ in range(RA)]
        ecT = [carve(P) for _ in range(RA)]
        hcr = [carve(1) for _ in range(RA)]
        hc = [carve(1) for _ in range(RA)]
        xb = [carve(P) for _ in range(RA)]
        st1 = [carve(6) for _ in range(RA)]
        mv1 = [carve(2) for _ in range(RA)]
        ve1 = [carve(1) for _ in range(RA)]
        rstd1 = [carve(1) for _ in range(RA)]
        xn1 = [carve(P) for _ in range(RA)]
        xn1T = [carve(P) for _ in range(RA)]
        end_a = used[0]

        logits = carve(NT * E0)
        sc = carve(NT * E0)
        sfc = carve(NT * E0)
        wr = logits
        m_bf = carve(NT * E0, BF16)
        s_bf = carve((NT + 1) * E0, BF16)
        gs = carve(NT * G0)
        t1 = carve(NT * 32)
        t2 = carve(NT * 32)
        t3 = carve(NT * 16)
        rsum = carve(NT)
        gsx = carve(QT * 12)
        g8 = carve(QT * 8)
        g8x = carve(QT * 8)
        gleft = carve(QT * 12)
        gmask = carve(QT * 8)
        tmp = carve(QT * E0)
        k8 = carve(QT * 8)
        kleft = carve(QT * E0)
        key = carve(QT * E0, I32)
        da_i = carve(QT * E0, I32)
        db_i = carve(QT * E0, I32)
        da = carve(QT * E0, BF16)
        db = carve(QT * E0, BF16)
        hot_a = carve(QT * 16 * E0, BF16)
        hot_b = carve(QT * 8 * E0, BF16)
        hot_v = carve(QT * 2 * 8 * E0, BF16)
        tbl = [t1[:, 0:512], t1[:, 512:1024], t2[:, 0:512]]
        slot_tok = carve(E0)
        filled = carve(E0)
        cnt = carve(E0)
        slot_row = carve(E0)
        gidx = carve(E0, I32)
        sidx = carve(E0, I32)

        end_r = used[0]

        used[0] = 0
        RB_ = 4
        w1n = [carve(P) for _ in range(2)] * 2
        w3n = [carve(P) for _ in range(2)] * 2
        w2n = [carve(P) for _ in range(2)] * 2
        w13T = [carve(2 * P) for _ in range(2)] * 2
        w2T = [carve(2 * P) for _ in range(2)] * 2
        xe = [carve(2 * ROW) for _ in range(RB_)]
        xeT = [carve(2 * P) for _ in range(2)] * 2
        sil = [carve(P) for _ in range(2)] * 2
        hh = [carve(P) for _ in range(2)] * 2
        hhT = [carve(P) for _ in range(2)] * 2
        ye = [carve(2 * P) for _ in range(RB_)]
        gi = [carve(2, I32) for _ in range(RB_)]
        si = [carve(2, I32) for _ in range(RB_)]
        sh_s, sh_u, sh_h, sh_y = (carve(512) for _ in range(4))
        assert used[0] <= end_a

        RC = 4
        S_BANK = (1, 2, 3, 6)
        used[0] = end_a
        def two_turns(cols):
            return [carve(cols) for _ in range(2)] * 2

        a0, a1, x2 = two_turns(P), two_turns(P), two_turns(P)
        cst = [carve(6) for _ in range(RC)]
        cmv = [carve(2) for _ in range(RC)]
        cve = [carve(1) for _ in range(RC)]
        crs = [carve(1) for _ in range(RC)]
        cxn, cxT, qs = two_turns(P), two_turns(P), two_turns(P)
        qm, kbd, vbd = two_turns(512), two_turns(512), two_turns(512)
        smax, nmax = two_turns(HEADS), two_turns(HEADS)
        ssum_, srec = two_turns(HEADS), two_turns(HEADS)
        srow, srT = two_turns(P), two_turns(P)
        pexp = [carve(512) for _ in range(4)]
        ppT = two_turns(2048)
        oT, x2b = two_turns(P), two_turns(P)
        assert used[0] <= end_r

        used[0] = 0
        RD = RC
        dst = [carve(6) for _ in range(RD)]
        dmv = [carve(2) for _ in range(RD)]
        dve_ = [carve(1) for _ in range(RD)]
        drs = [carve(1) for _ in range(RD)]
        dxn = [carve(P) for _ in range(RD)]
        dxT = [carve(P) for _ in range(RD)]
        dlog = carve(NT * E1)
        dsc = carve(NT * E1)
        dsel = carve(NT * E1)
        dmask = carve(NT * E1)
        dgat = carve(NT * E1)
        dalt = carve(NT * E1)
        dden = carve(NT)
        dok = carve(NT)
        dno = carve(NT)
        selx = carve(NT * 14)
        s8 = carve(NT * 8)
        s8x = carve(NT * 8)
        sleft = carve(NT * 14)
        fh = [carve(512) for _ in range(2)]
        fg = [carve(512) for _ in range(2)]
        eh = [carve(512) for _ in range(2)]
        assert used[0] <= end_a

        FREE_AT_START = dict(pe=("ey_psum", "fy_psum"), act=("eh_done", "shu_done", "shy_done"),
                             pool=("shh_done", "shx_done"), dve=("key_done", "fh_done", "fx_done", "y_added"))

        def start(eng, name):
            for n in FREE_AT_START[name]:
                eng.sem_inc(sem(n), 1)

        block = ctx.enter_context(nc.Block())

        IDENT_OK, ZEROS_OK, ROWV_OK, WCOL_OK, CONSTS_OK = 2, 5, 6, 8, 31
        BQV_OK, WQV_OK, BO_OK, WO_OK, SD_OK, HEAD_OK, SW_OK = 1, 2, 3, 4, 5, 6, 8

        @block.sync
        def _(sp):
            xd = A["x"].rearrange("t p d -> p t d")
            xv = x_all[:, :].rearrange("p (t d) -> p t d", d=P)
            sp.dma_start(xv[:, 0:8, :], xd[:, 0:8, :]).then_inc(sem("x_first"), 16)
            for name, o, n in (("L0_xattn_b_qv", BQV, 128), ("L0_ffn_e_bias", EB, 64), ("L1_xattn_bo", BO, 128),
                               ("L1_ffn_router_bias", RB, 8), ("L0_xattn_b_sim", BSIM, 1), ("g_xattn", GX, 2),
                               ("g_ffn", GF, 2)):
                sp.dma_start(rowin[0:1, o:o + n], A[name].rearrange("(a d) -> a d", a=1)).then_inc(sem("rows_in"), 16)
            sp.dma_start(wcol[:, :], A["L0_xattn_w_sim"].rearrange("(c p) -> p c", p=P),
                         allow_slow_non_contiguous=True).then_inc(sem("cols_in"), 16)
            for name, dst_ in (("L1_xattn_bq", bq), ("L1_xattn_bk", bk), ("L1_xattn_bv", bv)):
                sp.dma_start(dst_[:, :], A[name].rearrange("(p c) -> p c", c=1)).then_inc(sem("cols_in"), 16)
            sp.dma_start(wqv[:, :].rearrange("p (c n) -> p c n", c=4),
                         A["L0_xattn_W_qv"].rearrange("(c p) n -> p c n", p=P)).then_inc(sem("wqv_in"), 16)
            wn = wnat[:, :].rearrange("p (k d) -> p k d", d=P)
            sp.dma_start(wn[0:E0, GATE, :], A["L0_ffn_gate_weight"]).then_inc(sem("wnat_in"), 16)
            for name, k in (("L0_ffn_shared_gate", SG), ("L0_ffn_shared_up", SU), ("L0_ffn_shared_down", SD),
                            ("L1_xattn_Wq", WQ), ("L1_xattn_Wk", WK), ("L1_xattn_Wv", WV), ("L1_xattn_Wo", WO)):
                sp.dma_start(wn[:, k, :], A[name]).then_inc(sem("wnat_in"), 16)
            sp.dma_start(rw_nat[0:E1, :], A["L1_ffn_router_w"]).then_inc(sem("wnat_in"), 16)
            sp.dma_start(xv[:, 8:NT, :], xd[:, 8:NT, :]).then_inc(sem("x_rest"), 16)

            def ctx_tile(t, u, r):
                after(sp, sem("hqT_done"), t - RA)
                sp.dma_start(ctx_in[u], A["ctx_1024"][t:t + 1, :, :].rearrange("t p d -> p (t d)") if isinstance(t, int)
                             else A["ctx_1024"][bass.ds(t, 1), :, :].rearrange("t p d -> p (t d)")
                             ).then_inc(sem(f"ctx_in{u}"), 16)

            def rows_out(t, u, r):
                after(sp, sem("xn1_done"), t)
                sp.dma_start(rows_dram[at(t), 0:P], xn1[u]).then_inc(sem(f"rows_out{u}"), 16)

            pipeline(sp, NT, RA, [(0, ctx_tile), (4, rows_out)])

            sp.wait_ge(sem("pool_setup"), ZEROS_OK)
            for acc in acc_dram:
                av = acc.rearrange("(p r) d -> p (r d)", p=P)
                for k in range(3):
                    sp.dma_start(av[:, k * 1408:(k + 1) * 1408], zeros[:, :]).then_inc(sem("acc_zero"), 16)
            sp.dma_start(sw1[:, :], A["L1_ffn_sw1"]).then_inc(sem("w_late"), 16)
            sp.dma_start(sw3[:, :], A["L1_ffn_sw3"]).then_inc(sem("w_late"), 16)
            sp.dma_start(sw2[:, :].rearrange("p (c n) -> p c n", c=2),
                         A["L1_ffn_sw2"].rearrange("(c p) n -> p c n", p=P)).then_inc(sem("w_late"), 16)
            sp.dma_start(ew1[:, :].rearrange("p (e n) -> p e n", e=E1),
                         A["L1_ffn_ew1"].rearrange("e p n -> p e n")).then_inc(sem("w_late"), 16)
            sp.dma_start(ew2[:, :].rearrange("p (e n) -> p e n", e=E1),
                         A["L1_ffn_ew2"].rearrange("e p n -> p e n")).then_inc(sem("w_late"), 16)

            sp.wait_ge(sem("lg_done"), NT)
            for u in range(RA):
                sp.wait_ge(sem(f"rows_out{u}"), 16 * (NT // RA))

            sp.wait_ge(sem("wr_done"), 1)
            sp.dma_start(rows_dram[:, P:ROW].rearrange("(t p) e -> p t e", p=P),
                         wr.rearrange("p (t e) -> p t e", e=E0)).then_inc(sem("wr_out"), 16)

            def expert_weights(t, u, r):
                after(sp, sem("w2T_psum"), t - 2)
                for w, dst_ in (("L0_ffn_w1", w1n), ("L0_ffn_w3", w3n)):
                    src = A[w].rearrange("e f d -> (e f) d")
                    sp.dma_start(dst_[u], src[at(t), :]).then_inc(sem(f"w_in{u}"), 16)
                src = A["L0_ffn_w2"]
                e2 = src[2 * t:2 * t + 2] if isinstance(t, int) else src[bass.ds(t * 2, 2)]
                sp.dma_start(w2n[u].rearrange("p (e f) -> p e f", e=2),
                             e2.rearrange("e d f -> d e f")).then_inc(sem(f"w_in{u}"), 16)
            pipeline(sp, NPAIR, 2, [(0, expert_weights)])

            sp.wait_ge(sem("acc_done0"), 16 * NPAIR)
            sp.wait_ge(sem("acc_done1"), 16 * NPAIR)

            def sums_in(t, u, r):
                after(sp, sem("x2a"), t - 2)
                sp.dma_start(a0[u], acc_dram[0][at(t), :]).then_inc(sem(f"sums_in{u}"), 16)
                sp.dma_start(a1[u], acc_dram[1][at(t), :]).then_inc(sem(f"sums_in{u}"), 16)
            pipeline(sp, NT, 2, [(0, sums_in)])

            ov = out.rearrange("(q t) p d -> q p t d", t=QT)
            with sp.Fori(0, NQ) as q:
                sp.wait_ge(sem("y_added"), 1 + ((q * E1 + E1) * QT))
                sp.dma_start(ov[bass.ds(q, 1)].rearrange("q p t d -> p (q t) d"),
                             x_all[:, bass.ds(q * 512, 512)].rearrange("p (t d) -> p t d", d=P)
                             ).then_inc(sem("out_done"), 16)
            sp.wait_ge(sem("out_done"), 16 * NQ)
            if dbg:
                for k, v in dbg.items():
                    sp.dma_start(v, {"x_all": x_all, "kT_all": kT_all, "v_all": v_all, "slot_tok": slot_tok, "cnt": cnt,
                                     "bo_row": bo_row}[k][:, :]).then_inc(sem("dbg"), 16)
                sp.wait_ge(sem("dbg"), 16 * len(dbg))

        @block.gpsimd
        def _(pool):
            k = [0]

            def link(ins):
                k[0] += 1
                ins.then_inc(sem("pool_setup"), 1)
                pool.wait_ge(sem("pool_setup"), k[0])

            start(pool, "pool")
            link(pool.memset(ident[:, :], 0.0))
            link(pool.affine_select(out=ident[:, :], in_=ident[:, :], compare_op=ALU.not_equal, fill=1.0, base=0,
                               pattern=[[-1, P]], channel_multiplier=1))
            assert k[0] == IDENT_OK
            link(pool.memset(ones[:, :], 1.0))
            link(pool.memset(half_pow[:, :], -0.5))
            link(pool.memset(zeros[:, :], 0.0))
            assert k[0] == ZEROS_OK
            pool.wait_ge(sem("rows_in"), 16 * 7)
            link(pool.partition_broadcast(rowv[:, 0:BV], rowin[0:1, 0:BV]))
            assert k[0] == ROWV_OK
            pool.wait_ge(sem("cols_in"), 16 * 4)
            link(pool.tensor_scalar(w2b[:, :], ones[:, :], wcol[:, 1:2], None, ALU.mult))
            link(pool.tensor_scalar(bv_rep[:, :], ones[:, :], bv[:, 0:1], None, ALU.mult))
            assert k[0] == WCOL_OK
            link(pool.memset(ones_bf[:, :], 1.0))
            link(pool.memset(tri_bf[:, :], 1.0))
            link(pool.affine_select(out=tri_bf[:, :], in_=tri_bf[:, :], compare_op=ALU.is_gt, fill=0.0, base=0,
                                    pattern=[[1, P]], channel_multiplier=-1))
            link(pool.iota(ipart[:, 0:1], pattern=[[1, 1]], base=0, channel_multiplier=1))
            link(pool.tensor_copy(pcol[:, :], ipart[:, 0:1]))
            link(pool.tensor_scalar(dump_row[:, :], pcol[:, :], 1.0, float(NT * P), ALU.mult, ALU.add))
            link(pool.iota(itile[:, :], pattern=[[1, NT]], base=0, channel_multiplier=0))
            link(pool.tensor_copy(tile_no[:, :], itile[:, :]))
            link(pool.iota(iota_a[:, :], pattern=[[0, 8], [1, 16], [0, 8]], base=0, channel_multiplier=0,
                           allow_small_or_imprecise_dtypes=True))
            link(pool.iota(iota_b[:, :], pattern=[[1, 8], [0, E0]], base=0, channel_multiplier=0,
                           allow_small_or_imprecise_dtypes=True))
            link(pool.iota(imod8[:, :], pattern=[[-1, 8]], base=8, channel_multiplier=1))
            link(pool.iota(ihead[:, :], pattern=[[-8, 4]], base=32, channel_multiplier=1))
            link(pool.memset(same8[:, :], 1.0))
            sv = same8[:, :].rearrange("p (a b) -> p a b", b=8)
            link(pool.affine_select(out=sv, in_=sv, compare_op=ALU.is_ge, fill=0.0, base=0,
                                    pattern=[[-8, 16], [0, 8]], channel_multiplier=1))
            link(pool.affine_select(out=sv, in_=sv, compare_op=ALU.is_ge, fill=0.0, base=7,
                                    pattern=[[8, 16], [0, 8]], channel_multiplier=-1))
            link(pool.memset(group_m[:, :], 1.0))
            link(pool.affine_select(out=group_m[:, :], in_=group_m[:, :], compare_op=ALU.is_ge, fill=0.0, base=0,
                                    pattern=[[-32, 4]], channel_multiplier=1))
            link(pool.affine_select(out=group_m[:, :], in_=group_m[:, :], compare_op=ALU.is_ge, fill=0.0, base=31,
                                    pattern=[[32, 4]], channel_multiplier=-1))
            link(pool.memset(vmask[:, :], 0.0))
            vm = vmask[:, :].rearrange("p (x d) -> p x d", d=HD)
            for h in range(4):
                vh = vmask[:, h * P:(h + 1) * P].rearrange("p (g h d) -> p g h d", g=4, h=4)
                link(pool.affine_select(out=vh, in_=vh, compare_op=ALU.not_equal, fill=1.0, base=-h,
                                        pattern=[[0, 4], [1, 4], [0, HD]], channel_multiplier=0))
            assert k[0] == CONSTS_OK, k[0]

            def a_pow(t, u, r):
                after(pool, sem("ve_done"), t, 3)
                pool.tensor_tensor(rstd[u], ve[u], half_pow[:, 0:1], ALU.pow).then_inc(sem("rstd_done"), 1)

            def a_gmax(t, u, r):
                pool.wait_ge(sem("max_steps"), t * 3 + 2)
                hold(pool, sem("pool_passed"))
                pool.partition_all_reduce(gmax[u], msim[u], P, bass.bass_isa.ReduceOp.max).then_inc(sem("gmax_done"), 1)

            def a_bias(t, u, r):
                after(pool, sem("x1_done"), t - RA)
                if isinstance(t, int) and t == 0:
                    pool.wait_ge(sem("scaled"), BQV_OK)
                pool.tensor_tensor(xb[u], x_all[:, at(t)], bqv_row[:, :], ALU.add).then_inc(sem("xb_done"), 1)

            def a_pow1(t, u, r):
                after(pool, sem("ve1_done"), t, 3)
                pool.tensor_tensor(rstd1[u], ve1[u], half_pow[:, 0:1], ALU.pow).then_inc(sem("rstd1_done"), 1)

            def a_keep(t, u, r):
                after(pool, sem("xn1T_done"), t)
                pool.tensor_copy(xT_all[:, at(t)], xn1T[u]).then_inc(sem("xT_kept"), 1)

            pool.wait_ge(sem("x_rest"), 16)
            pipeline(pool, NT, RA, [(2, a_gmax), (4, a_pow1), (3, a_bias), (5, a_keep), (0, a_pow)])

            for u in range(RA):
                pool.wait_ge(sem(f"rows_out{u}"), 16 * (NT // RA))
            pool.wait_ge(sem("lg_done"), NT)
            pool.wait_ge(sem("xn1T_psum"), NT)
            pool.wait_ge(sem("out_psum"), NT)
            for u in range(2):
                pool.memset(w2T[u], 0.0).then_inc(sem("w2T_zero"), 1)

            pool.memset(s_bf[:, 0:E0], 0.0).then_inc(sem("s_done"), 1)

            def sh_product(q):
                pool.wait_ge(sem("shu_done"), 1 + (q + 1))
                if not isinstance(q, int):
                    pool.wait_ge(sem("shy_psum"), q)
                pool.tensor_tensor(sh_h, sh_s, sh_u, ALU.mult).then_inc(sem("shh_done"), 1)

            def sh_add(q):
                pool.wait_ge(sem("shy_done"), 1 + (q + 1))
                xq = x_all[:, (NQ - 1) * 512:] if isinstance(q, int) else x_all[:, bass.ds(q * 512, 512)]
                pool.tensor_tensor(xq, xq, sh_y, ALU.add).then_inc(sem("shx_done"), 1)

            def running_sums(q):
                pool.wait_ge(sem("m_done"), q + 1)
                for j in range(QT):
                    c = q * (QT * E0) + j * E0
                    pool.wait_ge(sem("s_done"), q * QT + (j + 1))
                    sc_ = (lambda a: slice(a, a + E0)) if isinstance(q, int) else (lambda a: bass.ds(a, E0))
                    pool.tensor_tensor(s_bf[:, sc_(c + E0)], s_bf[:, sc_(c)], m_bf[:, sc_(c)], ALU.add
                                       ).then_inc(sem("s_done"), 1)
            sh_product(0)
            with pool.Fori(0, NQ - 1) as q:
                sh_product(q + 1)
                running_sums(q)
                sh_add(q)
            running_sums(NQ - 1)
            sh_add(NQ - 1)

            for s_ in ("acc_zero",):
                pool.wait_ge(sem(s_), 16 * 6)
            pool.wait_ge(sem("wr_out"), 16)
            pool.wait_ge(sem("idx_done"), 2)

            def gather(t, u, r):
                after(pool, sem("gi_done"), t)
                after(pool, sem("ye_done"), t - RB_)
                for j in range(2):
                    hold(pool, sem("pool_passed"))
                    pool.indirect_dma_start(out=xe[u][:, j * ROW:(j + 1) * ROW], out_offset=None, in_=rows_dram,
                                            in_offset=bass.IndirectOffsetOnAxis(ap=gi[u][:, j:j + 1], axis=0)
                                            ).then_inc(sem(f"xe_in{u}"), 16)

            def scatter(t, u, r):
                after(pool, sem("ye_done"), t)
                for j in range(2):
                    after(pool, sem(f"acc_done{j}"), t - 1, 16)
                    hold(pool, sem("pool_passed"))
                    pool.indirect_dma_start(out=acc_dram[j], out_offset=bass.IndirectOffsetOnAxis(ap=si[u][:, j:j + 1], axis=0),
                                            in_=ye[u][:, j * P:(j + 1) * P], in_offset=None, compute_op=ALU.add,
                                            bounds_check=NROWS - 1, oob_is_err=True).then_inc(sem(f"acc_done{j}"), 16)

            pipeline(pool, NPAIR, RB_, [(4, scatter), (0, gather)])

            pool.wait_ge(sem("v_done"), NT)

            def c_sum(t, u, r):
                after(pool, sem(f"sums_in{u % 2}"), r * 2 + u // 2, 32)
                after(pool, sem("x2_done"), t - 2)
                pool.tensor_tensor(x2[u], a0[u], a1[u], ALU.add).then_inc(sem("x2a"), 1)
                after(pool, sem("x2a"), t)
                pool.tensor_tensor(x_all[:, at(t)], x2[u], x_all[:, at(t)], ALU.add).then_inc(sem("x2_done"), 1)

            def c_pow(t, u, r):
                after(pool, sem("cve_done"), t, 3)
                pool.tensor_tensor(crs[u], cve[u], half_pow[:, 0:1], ALU.pow).then_inc(sem("crs_done"), 1)

            def c_k(t, u, r):
                after(pool, sem("s_psum"), t - 2, 4)
                pool.tensor_tensor(kbd[u].rearrange("p (h k) -> p h k", h=4),
                                   kT_all[:, at(t)].rearrange("p (a k) -> p a k", a=1).broadcast_to([P, 4, P]),
                                   head_m[:, :].rearrange("p (h a) -> p h a", a=1).broadcast_to([P, 4, P]),
                                   ALU.mult).then_inc(sem("kbd_done"), 1)

            def c_qm(t, u, r):
                after(pool, sem("q_done"), t)
                after(pool, sem("s_psum"), t - 2, 4)
                pool.tensor_tensor(qm[u].rearrange("p (g q) -> p g q", g=4),
                                   qs[u].rearrange("p (a q) -> p a q", a=1).broadcast_to([P, 4, P]),
                                   group_m[:, :].rearrange("p (g a) -> p g a", a=1).broadcast_to([P, 4, P]),
                                   ALU.mult).then_inc(sem("qm_done"), 1)

            def c_v(t, u, r):
                after(pool, sem("pv_psum"), t - 2)
                pool.tensor_tensor(vbd[u].rearrange("p (h k) -> p h k", h=4),
                                   v_all[:, at(t)].rearrange("p (a k) -> p a k", a=1).broadcast_to([P, 4, P]),
                                   vmask[:, :].rearrange("p (h k) -> p h k", h=4),
                                   ALU.mult).then_inc(sem("vbd_done"), 1)

            def c_row(t, u, r):
                after(pool, sem("srec_done"), t)
                after(pool, sem("rec_psum"), t - 2)
                pool.tensor_tensor(srow[u].rearrange("p (h d) -> p h d", d=HD),
                                   srec[u].rearrange("p (h a) -> p h a", a=1).broadcast_to([P, HEADS, HD]),
                                   ones[:, :].rearrange("p (h d) -> p h d", d=HD), ALU.mult).then_inc(sem("srow_done"), 1)

            def c_bias(t, u, r):
                after(pool, sem("x3_done"), t - 2)
                pool.tensor_tensor(x2b[u], x_all[:, at(t)], bo_row[:, :], ALU.add).then_inc(sem("x2b_done"), 1)

            def d_pow(t, u, r):
                after(pool, sem("dve_done"), t, 3)
                pool.tensor_tensor(drs[u], dve_[u], half_pow[:, 0:1], ALU.pow).then_inc(sem("drs_done"), 1)

            pipeline(pool, NT, RC, [(4, c_row), (0, c_sum), (1, c_k), (0, c_pow), (3, c_v), (5, d_pow), (1, c_qm),
                                    (4, c_bias)])

        @block.tensor
        def _(pe):
            def T(dst_, src, n=P):
                return pe.transpose(dst_, src, ident[0:n, 0:n])

            start(pe, "pe")
            pe.wait_ge(sem("pool_setup"), IDENT_OK)
            pe.wait_ge(sem("wnat_in"), 16 * 9)
            for k in range(8):
                n = E0 if k == GATE else P
                m = T(bank[k // 4][:, (k % 4) * P:(k % 4) * P + n], wnat[0:n, k * P:(k + 1) * P], n)
                if k % 4 == 3:
                    m.then_inc(sem("wT_psum"), 1)
            T(bank[2][:, 0:E1], rw_nat[0:E1, :], E1).then_inc(sem("wT_psum"), 1)
            pe.wait_ge(sem("wT_done"), 4)
            pe.wait_ge(sem("pool_setup"), WCOL_OK)
            pe.matmul(bank[3][:, 0:P], bv_rep[:, :], wT[:, WO * P:(WO + 1) * P], start=True, stop=True
                      ).then_inc(sem("bvo_psum"), 1)
            pe.wait_ge(sem("pool_setup"), WCOL_OK)
            pe.wait_ge(sem("scaled"), BO_OK)
            pe.wait_ge(sem("scaled"), WQV_OK)

            def a_T(t, u, r):
                after(pe, sem("xn_done"), t)
                after(pe, sem(f"ctx_in{u}"), r, 16)
                after(pe, sem("eT_done"), t - 1, 2)
                b = bank[0]
                T(b[:, 0:P], xn[u])
                T(b[:, P:2 * P], ctx_in[u]).then_inc(sem("T_psum"), 1)

            def a_S(t, u, r):
                after(pe, sem("eT_done"), t, 2)
                after(pe, sem("pr_done"), t - 1)
                b = bank[1]
                pe.matmul(b[:, 0:P], w2b[:, :], cT[u], start=True, stop=False)
                after(pe, sem("cw_done"), t)
                pe.matmul(b[:, 0:P], eT[u], cw[u], start=False, stop=True).then_inc(sem("sim_psum"), 1)

            def a_PT(t, u, r):
                after(pe, sem("prn_done"), t)
                after(pe, sem("pT_done"), t - 1)
                T(bank[2][:, 0:P], prn[u]).then_inc(sem("pT_psum"), 1)

            def a_HC(t, u, r):
                after(pe, sem("eb_done"), t)
                after(pe, sem("hc_steps"), t - 1, 3)
                b = bank[4]
                pe.matmul(b[:, 0:P], xn[u], eb[u], start=True, stop=True)
                pe.matmul(b[:, P:2 * P], ones[:, :], eb[u], start=True, stop=True).then_inc(sem("hc_psum"), 1)

            def a_HQ(t, u, r):
                after(pe, sem("pT_done"), t)
                after(pe, sem("hq_done"), t - 1)
                pe.matmul(bank[3][:, 0:P], ctx_in[u], pT[u], start=True, stop=True).then_inc(sem("hqT_done"), 1)

            def a_OUT(t, u, r):
                after(pe, sem("x1_done"), t - 1)
                b = bank[5][:, 0:P]
                pe.matmul(b, eT[u], wqv[:, 0:P], start=True, stop=False)
                after(pe, sem("hq_done"), t)
                pe.matmul(b, hq[u], wqv[:, P:2 * P], start=False, stop=False)
                after(pe, sem("hc_steps"), t, 3)
                pe.matmul(b, ecT[u], wqv[:, 3 * P:4 * P], start=False, stop=False)
                after(pe, sem("ehT_done"), t)
                pe.matmul(b, ehT[u], wqv[:, 2 * P:3 * P], start=False, stop=True).then_inc(sem("out_psum"), 1)

            def a_XT(t, u, r):
                after(pe, sem("xn1_done"), t)
                after(pe, sem("lg_done"), t - 1)
                T(bank[6][:, 0:P], xn1[u]).then_inc(sem("xn1T_psum"), 1)

            def a_LG(t, u, r):
                after(pe, sem("xn1T_done"), t)
                pe.matmul(bank[6][:, P:2 * P], xn1T[u], wT[:, GATE * P:(GATE + 1) * P], start=True, stop=True
                          ).then_inc(sem("lg_psum"), 1)

            def a_KV(t, u, r):
                after(pe, sem("v_done"), t - 1)
                b = bank[7]
                pe.matmul(b[:, 0:P], wT[:, WK * P:(WK + 1) * P], cT[u], start=True, stop=True)
                pe.matmul(b[:, P:2 * P], cT[u], wT[:, WV * P:(WV + 1) * P], start=True, stop=True
                          ).then_inc(sem("kv_psum"), 1)

            pipeline(pe, NT, RA, [(2, a_S), (4, a_OUT), (3, a_PT), (1, a_T), (5, a_XT), (3, a_HC), (3, a_HQ),
                                  (2, a_KV), (5, a_LG)])

            pe.wait_ge(sem("xT_kept"), NT)
            pe.wait_ge(sem("eT_done"), 2 * NT)
            pe.wait_ge(sem("pr_done"), NT)
            pe.wait_ge(sem("pT_done"), NT)
            pe.wait_ge(sem("scaled"), SD_OK)

            def sh_up(q):
                xq = xT_all[:, 0:512] if isinstance(q, int) else xT_all[:, bass.ds(q * 512, 512)]
                pe.wait_ge(sem("shu_done"), 1 + q)
                pe.matmul(bank[0][:, :], wT[:, SG * P:(SG + 1) * P], xq, start=True, stop=True)
                pe.matmul(bank[1][:, :], wT[:, SU * P:(SU + 1) * P], xq, start=True, stop=True
                          ).then_inc(sem("sh_psum"), 1)

            def sh_down(q):
                pe.wait_ge(sem("shh_done"), 1 + (q + 1))
                pe.wait_ge(sem("shy_done"), 1 + q)
                for j in range(QT):
                    m = pe.matmul(bank[2][:, j * P:(j + 1) * P], sh_h[:, j * P:(j + 1) * P],
                                  wT[:, SD * P:(SD + 1) * P], start=True, stop=True)
                m.then_inc(sem("shy_psum"), 1)
            sh_up(0)
            with pe.Fori(0, NQ - 1) as q:
                sh_up(q + 1)
                sh_down(q)
            sh_down(NQ - 1)

            pe.wait_ge(sem("pool_setup"), CONSTS_OK)
            pe.wait_ge(sem("lg_done"), NT)
            pe.wait_ge(sem("xn1T_done"), NT)
            pe.wait_ge(sem("x1_done"), NT)
            pe.wait_ge(sem("pool_setup"), ZEROS_OK)
            for k in range(2):
                pe.matmul(bank[6 + k][:, :], zeros[:, 0:P], zeros[:, 0:512], start=True, stop=False,
                          skip_group_check=True)
            hb = hot_v.rearrange("p (j v b e) -> p j v b e", j=QT, v=2, e=E0)
            ha = hot_a.rearrange("p (j g x) -> p j g x", j=QT, g=8)
            pe.sem_inc(sem("lists_psum"), QT)

            def positions(q):
                pe.wait_ge(sem("s_done"), q * QT + (QT + 1))
                pe.wait_ge(sem("key_done"), 1 + q)
                cols = slice(0, QT * E0) if isinstance(q, int) else bass.ds(q * (QT * E0), QT * E0)
                pe.matmul(bank[5][:, 0:QT * E0], tri_bf[:, :], m_bf[:, cols], start=True, stop=False)
                pe.matmul(bank[5][:, 0:QT * E0], ones_bf[:, :], s_bf[:, cols], start=False, stop=True
                          ).then_inc(sem("pos_psum"), 1)

            def lists(q, j):
                pe.wait_ge(sem("hot_a_done"), q * QT + (j + 1))
                pe.wait_ge(sem("hot_v_done"), q * QT + (j + 1))
                for g in range(8):
                    o = (g % 4) * P
                    m = pe.matmul(bank[6 + g // 4][:, o:o + P], ha[:, j, g, :],
                                  hb[:, j, :, :, 8 * g:8 * g + 8], start=False, stop=False,
                                  skip_group_check=True)
                m.then_inc(sem("lists_psum"), 1)
            positions(0)
            with pe.Fori(0, NQ - 1) as q:
                lists(q, 0)
                positions(q + 1)
                for j in range(1, QT):
                    lists(q, j)
            for j in range(QT):
                lists(NQ - 1, j)
            pe.wait_ge(sem("s_done"), NT + 1)
            pe.wait_ge(sem("key_done"), 1 + (NQ))
            pe.matmul(bank[5][:, 0:E0], ones_bf[:, :], s_bf[:, NT * E0:(NT + 1) * E0], start=True, stop=True
                      ).then_inc(sem("cnt_psum"), 1)
            pe.wait_ge(sem("tbl_done"), 1)
            pe.wait_ge(sem("hq_done"), NT)
            pe.matmul(bank[3][:, :], same8[:, :], tbl[2][:, :], start=True, stop=True).then_inc(sem("slot_psum"), 1)

            pe.wait_ge(sem("shy_done"), 1 + NQ)
            pe.wait_ge(sem("slot_done"), 1)

            def b_W(t, u, r):
                after(pe, sem(f"w_in{u % 2}"), r * 2 + u // 2, 48)
                after(pe, sem("w13T_done"), t - 1)
                T(bank[0][:, 0:P], w1n[u])
                T(bank[0][:, P:2 * P], w3n[u]).then_inc(sem("w13T_psum"), 1)
                after(pe, sem("w2T_done"), t - 1, 2)
                T(bank[1][:, 0:P], w2n[u]).then_inc(sem("w2T_psum"), 1)

            def b_X(t, u, r):
                after(pe, sem(f"xe_in{u}"), r, 32)
                after(pe, sem("xeT_done"), t - 1)
                T(bank[2][:, 0:P], xe[u][:, 0:P])
                T(bank[2][:, P:2 * P], xe[u][:, ROW:ROW + P]).then_inc(sem("xeT_psum"), 1)

            def b_H(t, u, r):
                after(pe, sem("xeT_done"), t)
                after(pe, sem("w13T_done"), t)
                after(pe, sem("hh_done"), t - 1)
                for j in range(2):
                    m = pe.matmul(bank[3][:, j * P:(j + 1) * P], xeT[u][:, j * P:(j + 1) * P],
                                  w13T[u][:, j * P:(j + 1) * P], start=True, stop=True)
                m.then_inc(sem("h_psum"), 1)

            def b_HT(t, u, r):
                after(pe, sem("hh_done"), t)
                after(pe, sem("hhT_done"), t - 1)
                T(bank[4][:, 0:P], hh[u]).then_inc(sem("hhT_psum"), 1)

            def b_Y(t, u, r):
                after(pe, sem("hhT_done"), t)
                after(pe, sem("w2T_done"), t, 2)
                after(pe, sem("ye_done"), t - 1)
                pe.matmul(bank[5][:, 0:2 * P], hhT[u], w2T[u], start=True, stop=True).then_inc(sem("y_psum"), 1)

            pipeline(pe, NPAIR, RB_, [(1, b_W), (2, b_X), (3, b_HT), (2, b_H), (3, b_Y)])

            pe.wait_ge(sem("ye_done"), NPAIR)
            pe.wait_ge(sem("w2T_done"), 2 * NPAIR)

            def c_XT(t, u, r):
                after(pe, sem("cxn_done"), t)
                after(pe, sem("dlog_done"), t - 6)
                T(bank[0][:, 0:P], cxn[u]).then_inc(sem("cxT_psum"), 1)

            def c_Q(t, u, r):
                after(pe, sem("cxT_done"), t)
                pe.matmul(bank[0][:, P:2 * P], wT[:, WQ * P:(WQ + 1) * P], cxT[u], start=True, stop=True
                          ).then_inc(sem("q_psum"), 1)

            def d_T(t, u, r):
                after(pe, sem("dxn_done"), t)
                after(pe, sem("dlog_done"), t - 1)
                after(pe, sem("q_done"), min(t + 5, NT - 1) if isinstance(t, int) else t + 5)
                T(bank[0][:, 2 * P:3 * P], dxn[u]).then_inc(sem("dxT_psum"), 1)

            def d_R(t, u, r):
                after(pe, sem("dxT_done"), t)
                pe.matmul(bank[0][:, 3 * P:4 * P], dxT[u], rwT[:, :], start=True, stop=True
                          ).then_inc(sem("dlog_psum"), 1)

            def c_S(t, u, g):
                if g == 0:
                    after(pe, sem("qm_done"), t)
                    after(pe, sem("kbd_done"), t)
                if not isinstance(t, int):
                    pe.wait_ge(sem("pexp_done"), t * 4 + (g - 3))
                elif t >= 1:
                    pe.wait_ge(sem("pexp_done"), 4 * t + g - 3)
                pe.matmul(bank[S_BANK[g]][:, :], qm[u][:, g * P:(g + 1) * P], kbd[u], start=True, stop=True
                          ).then_inc(sem("s_psum"), 1)

            def c_PT(t, u, g):
                pe.wait_ge(sem("pexp_done"), t * 4 + (g + 1))
                done = sem("ppT_even" if g % 2 == 0 else "ppT_odd")
                if not isinstance(t, int):
                    pe.wait_ge(done, t * 2 + g // 2)
                elif 2 * t + g // 2 > 0:
                    pe.wait_ge(done, 2 * t + g // 2)
                for h in range(4):
                    m = T(bank[4 + g % 2][:, h * P:(h + 1) * P], pexp[g][:, h * P:(h + 1) * P])
                m.then_inc(sem("ppT_psum"), 1)

            def c_PV(t, u, r, half):
                if half == 0:
                    after(pe, sem("ppT_even"), t, 2)
                    after(pe, sem("ppT_odd"), t, 2)
                    after(pe, sem("vbd_done"), t)
                    after(pe, sem("x3_done"), t - 1)
                for h in (2 * half, 2 * half + 1):
                    for g in range(4):
                        m = pe.matmul(bank[7][32 * g:32 * g + 32, 0:P], vbd[u][:, h * P + 32 * g:h * P + 32 * g + 32],
                                      ppT[u][:, (g * 4 + h) * P:(g * 4 + h + 1) * P],
                                      start=(h == 0), stop=(h == 3), skip_group_check=True)
                if half == 1:
                    m.then_inc(sem("pv_psum"), 1)

            def c_RT(t, u, r):
                after(pe, sem("srow_done"), t)
                T(bank[7][:, P:2 * P], srow[u]).then_inc(sem("rec_psum"), 1)

            def c_OUT(t, u, r):
                after(pe, sem("oT_done"), t)
                pe.matmul(bank[7][:, 2 * P:3 * P], oT[u], wT[:, WO * P:(WO + 1) * P], start=True, stop=True
                          ).then_inc(sem("c_out_psum"), 1)

            pe.wait_ge(sem("scaled"), WO_OK)
            of = lambda step, g: lambda t, u, r: step(t, u, g)
            pipeline(pe, NT, RC, [
                (7, d_R), (3, of(c_PT, 0)), (2, of(c_S, 0)), (1, c_XT), (4, lambda t, u, r: c_PV(t, u, r, 0)),
                (3, of(c_PT, 1)), (2, of(c_S, 1)), (1, c_Q), (4, lambda t, u, r: c_PV(t, u, r, 1)), (4, c_RT),
                (3, of(c_PT, 2)), (2, of(c_S, 2)), (6, d_T), (4, c_OUT), (3, of(c_PT, 3)), (2, of(c_S, 3)),
            ])

            pe.wait_ge(sem("xT2_kept"), NT)
            pe.wait_ge(sem("pexp_done"), 4 * NT)
            pe.wait_ge(sem("ppT_even"), 2 * NT)
            pe.wait_ge(sem("ppT_odd"), 2 * NT)
            pe.wait_ge(sem("x3_done"), NT)
            pe.wait_ge(sem("w_late"), 16 * 5)
            pe.wait_ge(sem("dlog_done"), NT)
            pe.wait_ge(sem("scaled"), SW_OK)
            with pe.Fori(0, NQ) as q:
                xq = xT_all[:, bass.ds(q * 512, 512)]

                def shared_up(c):
                    if c == 0:
                        pe.wait_ge(sem("fx_done"), 1 + q)
                    pe.wait_ge(sem("fh_done"), 1 + (q * 2 + c))
                    pe.matmul(bank[2 - 2 * c][:, :], sw1[:, c * P:(c + 1) * P], xq, start=True, stop=True)
                    pe.matmul(bank[3 - 2 * c][:, :], sw3[:, c * P:(c + 1) * P], xq, start=True, stop=True
                              ).then_inc(sem("f_psum"), 1)

                def shared_down():
                    pe.wait_ge(sem("fh_done"), 1 + (q * 2 + 2))
                    for j in range(QT):
                        for c in range(2):
                            m = pe.matmul(bank[2][:, j * P:(j + 1) * P], fh[c][:, j * P:(j + 1) * P],
                                          sw2[:, c * P:(c + 1) * P], start=(c == 0), stop=(c == 1))
                    m.then_inc(sem("fy_psum"), 1)

                def up(e):
                    pe.wait_ge(sem("eh_done"), 1 + (q * E1 + (e - 1) if e >= 1 else q * E1))
                    pe.matmul(bank[5 + e % 2][:, :], ew1[:, e * P:(e + 1) * P], xq, start=True, stop=True
                              ).then_inc(sem("eh_psum"), 1)

                def down(e):
                    pe.wait_ge(sem("eh_done"), 1 + (q * E1 + (e + 1)))
                    if e >= 1:
                        pe.wait_ge(sem("y_added"), 1 + ((q * E1 + (e - 1)) * QT))
                    else:
                        pe.wait_ge(sem("y_added"), 1 + (q * (E1 * QT)))
                    for j in range(QT):
                        m = pe.matmul(bank[4 if e % 2 else 7][:, j * P:(j + 1) * P], eh[e % 2][:, j * P:(j + 1) * P],
                                      ew2[:, e * P:(e + 1) * P], start=True, stop=True)
                    m.then_inc(sem("ey_psum"), 1)
                shared_up(0)
                shared_up(1)
                up(0)
                up(1)
                shared_down()
                for e in range(2, E1):
                    down(e - 2)
                    up(e)
                down(E1 - 2)
                down(E1 - 1)

        @block.scalar
        def _(act):
            start(act, "act")
            act.wait_ge(sem("pool_setup"), ROWV_OK)
            act.activation(th[:, :], rowv[:, GX:GX + 4], ACT.Tanh).then_inc(sem("th_done"), 1)
            act.wait_ge(sem("wT_zero"), 1)
            act.wait_ge(sem("wT_psum"), 3)
            act.activation(wT[:, 0:E0], bank[0][:, 0:E0], ACT.Copy).then_inc(sem("wT_done"), 1)
            act.activation(wT[:, P:4 * P], bank[0][:, P:4 * P], ACT.Copy).then_inc(sem("wT_done"), 1)
            act.activation(wT[:, 4 * P:8 * P], bank[1][:, :], ACT.Copy).then_inc(sem("wT_done"), 1)
            act.activation(rwT[:, 0:E1], bank[2][:, 0:E1], ACT.Copy).then_inc(sem("wT_done"), 1)

            def a_E(t, u, r):
                after(act, sem("T_psum"), t)
                after(act, sem("out_psum"), t - RA)
                after(act, sem("kv_psum"), t - RA)
                act.activation(cT[u], bank[0][:, P:2 * P], ACT.Copy).then_inc(sem("eT_done"), 1)
                act.activation(eT[u], bank[0][:, 0:P], ACT.Copy).then_inc(sem("eT_done"), 1)

            def a_exp(t, u, r):
                after(act, sem("max_steps"), t, 3)
                after(act, sem("prn_done"), t - RA)
                act.activation(pr[u], bank[1][:, 0:P], ACT.Exp, bias=nb[u], accum_out=ssum[u]
                               ).then_inc(sem("pr_done"), 1)

            def a_eb(t, u, r):
                after(act, sem("ngmax_done"), t)
                after(act, sem("hc_psum"), t - RA)
                act.activation(eb[u], msim[u].broadcast_to([P, P]), ACT.Exp, bias=ngmax[u]).then_inc(sem("eb_done"), 1)

            def a_prn(t, u, r):
                after(act, sem("rs_done"), t)
                after(act, sem("pT_psum"), t - RA)
                act.activation(prn[u], pr[u], ACT.Copy, scale=rs[u]).then_inc(sem("prn_done"), 1)

            def a_pT(t, u, r):
                after(act, sem("pT_psum"), t)
                after(act, sem("hqT_done"), t - RA)
                act.activation(pT[u], bank[2][:, 0:P], ACT.Copy).then_inc(sem("pT_done"), 1)

            def a_hq(t, u, r):
                after(act, sem("hqT_done"), t)
                after(act, sem("out_psum"), t - RA)
                act.activation(hq[u], bank[3][:, 0:P], ACT.Copy).then_inc(sem("hq_done"), 1)

            def a_x1T(t, u, r):
                after(act, sem("xn1T_psum"), t)
                after(act, sem("lg_psum"), t - RA)
                after(act, sem("xT_kept"), t - RA)
                act.activation(xn1T[u], bank[6][:, 0:P], ACT.Copy).then_inc(sem("xn1T_done"), 1)

            def a_lg(t, u, r):
                after(act, sem("lg_psum"), t)
                act.activation(logits[:, at(t, E0)], bank[6][:, P:P + E0], ACT.Copy).then_inc(sem("lg_done"), 1)

            def a_kv(t, u, r):
                after(act, sem("kv_psum"), t)
                act.activation(kT_all[:, at(t)], bank[7][:, 0:P], ACT.Identity, bias=bk[:, 0:1])
                act.activation(v_all[:, at(t)], bank[7][:, P:2 * P], ACT.Copy).then_inc(sem("v_done"), 1)

            act.wait_ge(sem("cols_in"), 16 * 4)
            pipeline(act, NT, RA, [(3, a_eb), (2, a_exp), (3, a_pT), (1, a_E), (5, a_x1T), (3, a_hq), (2, a_prn),
                                   (2, a_kv), (5, a_lg)])

            act.wait_ge(sem("lg_done"), NT)
            act.activation(sc, logits, ACT.Sigmoid).then_inc(sem("sc_done"), 1)

            for u in range(RA):
                act.wait_ge(sem(f"rows_out{u}"), 16 * (NT // RA))
            def sh_halves(q):
                act.wait_ge(sem("sh_psum"), q + 1)
                act.wait_ge(sem("shh_done"), 1 + q)
                act.activation(sh_s, bank[0][:, :], ACT.Silu)
                act.activation(sh_u, bank[1][:, :], ACT.Copy).then_inc(sem("shu_done"), 1)

            def sh_out(q):
                act.wait_ge(sem("shy_psum"), q + 1)
                act.wait_ge(sem("shx_done"), 1 + q)
                act.activation(sh_y, bank[2][:, :], ACT.Copy).then_inc(sem("shy_done"), 1)
            sh_halves(0)
            with act.Fori(0, NQ - 1) as q:
                sh_halves(q + 1)
                sh_out(q)
            sh_out(NQ - 1)

            hv = hot_v.rearrange("p (j v x) -> p j v x", j=QT, v=2)
            hbx = hot_b.rearrange("p (j x) -> p j x", j=QT)
            act.wait_ge(sem("pool_setup"), CONSTS_OK)
            with act.Fori(0, NQ) as q:
                for j in range(QT):
                    act.wait_ge(sem("hot_b_done"), q * QT + (j + 1))
                    act.wait_ge(sem("lists_psum"), q * QT + (j + 1))
                    act.activation(hv[:, j, 0, :], hbx[:, j], ACT.Copy, scale=pcol[:, 0:1])
                    act.activation(hv[:, j, 1, :], hbx[:, j], ACT.Copy, scale=tile_no[:, bass.ds(q * QT + j, 1)]
                                   ).then_inc(sem("hot_v_done"), 1)

            def b_w13(t, u, r):
                after(act, sem("w13T_psum"), t)
                after(act, sem("h_psum"), t - 2)
                act.activation(w13T[u].rearrange("p (e k f) -> p k e f", e=2, k=2),
                               bank[0][:, 0:2 * P].rearrange("p (k e f) -> p k e f", k=2, e=2), ACT.Copy
                               ).then_inc(sem("w13T_done"), 1)

            def b_xeT(t, u, r):
                after(act, sem("xeT_psum"), t)
                after(act, sem("h_psum"), t - 2)
                act.activation(xeT[u], bank[2][:, 0:2 * P], ACT.Copy).then_inc(sem("xeT_done"), 1)

            def b_silu(t, u, r):
                after(act, sem("h_psum"), t)
                after(act, sem("hh_done"), t - 2)
                act.activation(sil[u].rearrange("p (e f) -> p e f", e=2),
                               bank[3][:, 0:2 * P].rearrange("p (e k f) -> p e k f", e=2, k=2)[:, :, 0, :], ACT.Silu
                               ).then_inc(sem("sil_done"), 1)

            def b_hhT(t, u, r):
                after(act, sem("hhT_psum"), t)
                after(act, sem("y_psum"), t - 2)
                act.activation(hhT[u], bank[4][:, 0:P], ACT.Copy).then_inc(sem("hhT_done"), 1)
            pipeline(act, NPAIR, RB_, [(1, b_w13), (2, b_xeT), (3, b_hhT), (2, b_silu)])

            def c_xT(t, u, r):
                after(act, sem("cxT_psum"), t)
                after(act, sem("q_psum"), t - 2)
                act.activation(cxT[u], bank[0][:, 0:P], ACT.Copy).then_inc(sem("cxT_done"), 1)

            def c_q(t, u, r):
                after(act, sem("q_psum"), t)
                after(act, sem("qm_done"), t - 2)
                act.activation(qs[u], bank[0][:, P:2 * P], ACT.Identity, bias=bq[:, 0:1]).then_inc(sem("q_done"), 1)

            def c_exp(t, u, g):
                act.wait_ge(sem("nmax_done"), t * 4 + (g + 1))
                after(act, sem("ppT_psum"), t - 1, 4)
                after(act, sem("srec_done"), t - 2)
                for h in range(4):
                    c = g * 4 + h
                    m = act.activation(pexp[g][:, h * P:(h + 1) * P], bank[S_BANK[g]][:, h * P:(h + 1) * P], ACT.Exp,
                                       bias=nmax[u][:, c:c + 1], scale=float(HD) ** -0.5, accum_out=ssum_[u][:, c:c + 1])
                m.then_inc(sem("pexp_done"), 1)

            def c_ppT(t, u, g):
                act.wait_ge(sem("ppT_psum"), t * 4 + (g + 1))
                after(act, sem("pv_psum"), t - 2)
                act.activation(ppT[u][:, g * 512:(g + 1) * 512], bank[4][:, :], ACT.Copy).then_inc(sem("ppT_even"), 1)

            def d_t(t, u, r):
                after(act, sem("dxT_psum"), t)
                after(act, sem("dlog_psum"), t - RC)
                after(act, sem("xT2_kept"), t - RC)
                act.activation(dxT[u], bank[0][:, 2 * P:3 * P], ACT.Copy).then_inc(sem("dxT_done"), 1)

            def d_l(t, u, r):
                after(act, sem("dlog_psum"), t)
                act.activation(dlog[:, at(t, E1)], bank[0][:, 3 * P:3 * P + E1], ACT.Copy).then_inc(sem("dlog_done"), 1)

            of = lambda step, g: lambda t, u, r: step(t, u, g)
            pipeline(act, NT, RC, [
                (3, of(c_exp, 0)), (7, d_l), (3, of(c_exp, 1)), (1, c_xT), (3, of(c_ppT, 0)), (3, of(c_exp, 2)),
                (1, c_q), (3, of(c_exp, 3)), (6, d_t), (3, of(c_ppT, 2)),
            ])
            act.wait_ge(sem("dlog_done"), NT)
            act.activation(dsc, dlog, ACT.Sigmoid).then_inc(sem("dsc_done"), 1)
            with act.Fori(0, NQ) as q:
                for c in range(2):
                    act.wait_ge(sem("f_psum"), q * 2 + (c + 1))
                    act.wait_ge(sem("fh_done"), 1 + (q * 2 + c))
                    act.activation(fg[c], bank[2 - 2 * c][:, :], ACT.Silu).then_inc(sem("fg_done"), 1)
                for e in range(E1):
                    act.wait_ge(sem("eh_psum"), q * E1 + (e + 1))
                    act.wait_ge(sem("ey_psum"), 1 + (q * E1 + (e - 1) if e >= 1 else q * E1))
                    act.activation(eh[e % 2], bank[5 + e % 2][:, :], ACT.Gelu).then_inc(sem("eh_done"), 1)

        @block.vector
        def _(dve):
            k = [0]

            def link(ins):
                k[0] += 1
                ins.then_inc(sem("dve_setup"), 1)
                dve.wait_ge(sem("dve_setup"), k[0])

            start(dve, "dve")
            dve.memset(rwT[:, :], 0.0)
            dve.memset(wT[:, 0:P], 0.0).then_inc(sem("wT_zero"), 1)
            dve.wait_ge(sem("th_done"), 1)
            dve.tensor_scalar(bqv_row[:, :], rowv[:, BQV:BQV + P], th[:, 0:1], None, ALU.mult
                              ).then_inc(sem("scaled"), 1)
            dve.wait_ge(sem("wqv_in"), 16)
            dve.tensor_scalar(wqv[:, :], wqv[:, :], th[:, 0:1], None, ALU.mult).then_inc(sem("scaled"), 1)
            dve.wait_ge(sem("bvo_psum"), 1)
            link(dve.tensor_tensor(bo_row[:, :], bank[3][:, 0:P], rowv[:, BO:BO + P], ALU.add))
            dve.tensor_scalar(bo_row[:, :], bo_row[:, :], th[:, 1:2], None, ALU.mult).then_inc(sem("scaled"), 1)
            dve.tensor_scalar(wT[:, WO * P:(WO + 1) * P], wT[:, WO * P:(WO + 1) * P], th[:, 1:2], None, ALU.mult
                              ).then_inc(sem("scaled"), 1)
            dve.tensor_scalar(wT[:, SD * P:(SD + 1) * P], wT[:, SD * P:(SD + 1) * P], th[:, 2:3], None, ALU.mult
                              ).then_inc(sem("scaled"), 1)
            dve.wait_ge(sem("pool_setup"), CONSTS_OK)
            link(dve.tensor_scalar(imod8[:, :], imod8[:, :], 7, None, ALU.bitwise_and))
            link(dve.tensor_scalar(mod8[:, :], imod8[:, :], 0, None, ALU.is_equal))
            link(dve.tensor_scalar(ihead[:, :], ihead[:, :], 3, 3, ALU.logical_shift_right, ALU.bitwise_and))
            dve.tensor_scalar(head_m[:, :], ihead[:, :], 0, None, ALU.is_equal).then_inc(sem("scaled"), 1)

            def norm_steps(src, s_, m_, v_, stats, first=None):
                def sums(t, u, r):
                    if first:
                        first(t, u, r)
                    hold(dve, sem("dve_passed"))
                    dve.bn_stats(s_[u], src[:, at(t)]).then_inc(sem(stats), 1)

                def moments(t, u, r):
                    dve.wait_ge(sem(stats), t * 3 + 1)
                    hold(dve, sem("dve_passed"))
                    dve.bn_aggr(m_[u], s_[u]).then_inc(sem(stats), 1)

                def variance(t, u, r):
                    dve.wait_ge(sem(stats), t * 3 + 2)
                    dve.tensor_scalar(v_[u], m_[u][:, 1:2], EPS, None, ALU.add).then_inc(sem(stats), 1)
                return sums, moments, variance

            def x_there(t, u, r):
                if isinstance(t, int) and t in (0, 8):
                    dve.wait_ge(sem("x_first" if t == 0 else "x_rest"), 16)

            a_sums, a_moments, a_var = norm_steps(x_all, st, mv, ve, "ve_done", x_there)

            def a_xn(t, u, r):
                after(dve, sem("rstd_done"), t)
                after(dve, sem("hc_psum"), t - RA)
                dve.tensor_scalar(xn[u], x_all[:, at(t)], mv[u][:, 0:1], rstd[u], ALU.subtract, ALU.mult
                                  ).then_inc(sem("xn_done"), 1)

            def a_cw(t, u, r):
                dve.wait_ge(sem("eT_done"), t * 2 + 1)
                after(dve, sem("sim_psum"), t - RA)
                dve.tensor_scalar(cw[u], cT[u], wcol[:, 2:3], wcol[:, 0:1], ALU.mult, ALU.add
                                  ).then_inc(sem("cw_done"), 1)

            def a_max(t, u, r):
                after(dve, sem("sim_psum"), t)
                dve.tensor_reduce(mraw[u], bank[1][:, 0:P], AX.X, ALU.max).then_inc(sem("max_steps"), 1)

            def a_msim(t, u, r):
                dve.wait_ge(sem("max_steps"), t * 3 + 1)
                dve.tensor_scalar(msim[u], mraw[u], rowv[:, BSIM:BSIM + 1], None, ALU.add).then_inc(sem("max_steps"), 1)

            def a_nb(t, u, r):
                dve.wait_ge(sem("max_steps"), t * 3 + 2)
                dve.tensor_scalar(nb[u], msim[u], -1.0, rowv[:, BSIM:BSIM + 1], ALU.mult, ALU.add
                                  ).then_inc(sem("max_steps"), 1)

            def a_rs(t, u, r):
                after(dve, sem("pr_done"), t)
                dve.reciprocal(rs[u], ssum[u]).then_inc(sem("rs_done"), 1)

            def a_ng(t, u, r):
                after(dve, sem("gmax_done"), t)
                dve.tensor_scalar(ngmax[u], gmax[u], -1.0, None, ALU.mult).then_inc(sem("ngmax_done"), 1)

            def a_hcr(t, u, r):
                after(dve, sem("hc_psum"), t)
                dve.reciprocal(hcr[u], bank[4][:, P:P + 1]).then_inc(sem("hc_steps"), 1)

            def a_hc(t, u, r):
                dve.wait_ge(sem("hc_steps"), t * 3 + 1)
                dve.tensor_scalar(hc[u], bank[4][:, 0:1], hcr[u], None, ALU.mult).then_inc(sem("hc_steps"), 1)

            def a_ec(t, u, r):
                dve.wait_ge(sem("hc_steps"), t * 3 + 2)
                after(dve, sem("out_psum"), t - RA)
                dve.tensor_scalar(ecT[u], eT[u], hc[u], None, ALU.mult).then_inc(sem("hc_steps"), 1)

            def a_eh(t, u, r):
                after(dve, sem("hq_done"), t)
                dve.tensor_tensor(ehT[u], eT[u], hq[u], ALU.mult).then_inc(sem("ehT_done"), 1)

            def a_x1(t, u, r):
                after(dve, sem("out_psum"), t)
                after(dve, sem("xb_done"), t)
                dve.tensor_tensor(x_all[:, at(t)], bank[5][:, 0:P], xb[u], ALU.add).then_inc(sem("x1_done"), 1)

            def x1_there(t, u, r):
                after(dve, sem("x1_done"), t)

            b_sums, b_moments, b_var = norm_steps(x_all, st1, mv1, ve1, "ve1_done", x1_there)

            def a_xn1(t, u, r):
                after(dve, sem("rstd1_done"), t)
                after(dve, sem("xn1T_psum"), t - RA)
                after(dve, sem(f"rows_out{u}"), r - 1, 16)
                dve.tensor_scalar(xn1[u], x_all[:, at(t)], mv1[u][:, 0:1], rstd1[u], ALU.subtract, ALU.mult
                                  ).then_inc(sem("xn1_done"), 1)

            pipeline(dve, NT, RA, [
                (3, a_ng), (1, a_xn), (2, a_max), (4, a_x1), (2, a_msim), (4, b_sums), (2, a_nb), (4, b_moments),
                (1, a_cw), (4, b_var), (0, a_sums), (3, a_hcr), (2, a_rs), (0, a_moments), (3, a_hc), (4, a_xn1),
                (0, a_var), (3, a_ec), (3, a_eh)])

            dve.wait_ge(sem("sc_done"), 1)
            v3 = lambda b, n: b.rearrange("p (t e) -> p t e", e=n)
            eb_b = rowv[:, EB:EB + E0].rearrange("p (a e) -> p a e", a=1).broadcast_to([P, NT, E0])
            link(dve.tensor_tensor(v3(sfc, E0), v3(sc, E0), eb_b, ALU.add))
            s8v = sfc.rearrange("p (n k) -> p n k", k=8)
            h1, l1 = (b.rearrange("p (n k) -> p n k", k=4) for b in (t1, t2))
            for hf in range(2):
                n0 = hf * (NT * G0 // 2)
                n1 = n0 + NT * G0 // 2
                a_, b_ = s8v[:, n0:n1, 0:4], s8v[:, n0:n1, 4:8]
                hi4, lo4 = t1.rearrange("p (n k) -> p n k", k=4)[:, 0:128], t2.rearrange("p (n k) -> p n k", k=4)[:, 0:128]
                link(dve.tensor_tensor(hi4, a_, b_, ALU.max))
                link(dve.tensor_tensor(lo4, a_, b_, ALU.min))
                hi2 = t1[:, 512:768].rearrange("p (n k) -> p n k", k=2)
                mi2 = t1[:, 768:1024].rearrange("p (n k) -> p n k", k=2)
                lo2 = t2[:, 512:768].rearrange("p (n k) -> p n k", k=2)
                se2 = t2[:, 768:1024].rearrange("p (n k) -> p n k", k=2)
                link(dve.tensor_tensor(hi2, hi4[:, :, 0:2], hi4[:, :, 2:4], ALU.max))
                link(dve.tensor_tensor(mi2, hi4[:, :, 0:2], hi4[:, :, 2:4], ALU.min))
                link(dve.tensor_tensor(lo2, lo4[:, :, 0:2], lo4[:, :, 2:4], ALU.max))
                link(dve.tensor_tensor(se2, mi2, lo2, ALU.max))
                q3 = t3.rearrange("p (c n a) -> p c n a", c=4, a=1)
                link(dve.tensor_tensor(q3[:, 0], hi2[:, :, 0:1], hi2[:, :, 1:2], ALU.max))
                link(dve.tensor_tensor(q3[:, 1], hi2[:, :, 0:1], hi2[:, :, 1:2], ALU.min))
                link(dve.tensor_tensor(q3[:, 2], se2[:, :, 0:1], se2[:, :, 1:2], ALU.max))
                link(dve.tensor_tensor(q3[:, 3], q3[:, 1], q3[:, 2], ALU.max))
                link(dve.tensor_tensor(gs[:, n0:n1].rearrange("p (n a) -> p n a", a=1), q3[:, 0], q3[:, 3], ALU.add))
            link(dve.memset(gsx, BIG))
            link(dve.memset(g8x, BIG))
            gsxv, g8v, g8xv, glv, gmv = v3(gsx, 12), v3(g8, 8), v3(g8x, 8), v3(gleft, 12), v3(gmask, 8)
            tmv, k8v, klv = v3(tmp, E0), v3(k8, 8), v3(kleft, E0)
            with dve.Fori(0, NQ) as q:
                base = q * 9
                n = [0]

                def step(ins):
                    n[0] += 1
                    ins.then_inc(sem("route_steps"), 1)
                    dve.wait_ge(sem("route_steps"), base + n[0])

                step(dve.tensor_copy(gsxv[:, :, 0:8], v3(gs[:, bass.ds(q * (QT * 8), QT * 8)], 8)))
                hold(dve, sem("dve_passed"))
                for j in range(QT):
                    m = dve.max(g8v[:, j], gsxv[:, j, 0:8])
                step(m)
                step(dve.tensor_copy(g8xv[:, :, 0:4], g8v[:, :, 0:4]))
                hold(dve, sem("dve_passed"))
                for j in range(QT):
                    m = dve.match_replace(out=glv[:, j], in_to_replace=g8xv[:, j], in_values=gsxv[:, j], imm_value=GONE)
                step(m)
                step(dve.tensor_scalar(gmv, glv[:, :, 0:8], GONE / 2, None, ALU.is_lt))
                step(dve.tensor_tensor(tmp.rearrange("p (n k) -> p n k", k=8),
                                       sfc[:, bass.ds(q * (QT * E0), QT * E0)].rearrange("p (n k) -> p n k", k=8),
                                       gmask.rearrange("p (n a) -> p n a", a=1).broadcast_to([P, QT * G0, 8]),
                                       ALU.mult))
                hold(dve, sem("dve_passed"))
                for j in range(QT):
                    m = dve.max(k8v[:, j], tmv[:, j])
                step(m)
                hold(dve, sem("dve_passed"))
                for j in range(QT):
                    m = dve.match_replace(out=klv[:, j], in_to_replace=k8v[:, j], in_values=tmv[:, j], imm_value=GONE)
                step(m)
                dve.tensor_scalar(m_bf[:, bass.ds(q * (QT * E0), QT * E0)], kleft, GONE / 2, None, ALU.is_lt
                                  ).then_inc(sem("m_done"), 1)
                step(dve.tensor_copy(rsum[:, 0:1], g8[:, 0:1]))
                assert n[0] == 9
            dve.wait_ge(sem("m_done"), NQ)
            link(dve.tensor_tensor(wr, sc, m_bf, ALU.mult))
            link(dve.tensor_reduce(rsum, v3(wr, E0), AX.X, ALU.add))
            link(dve.tensor_scalar(rsum, rsum, 1e-20, None, ALU.add))
            link(dve.reciprocal(rsum, rsum))
            link(dve.tensor_scalar(rsum, rsum, ROUTE_SCALE, th[:, 2:3], ALU.mult, ALU.mult))
            dve.tensor_tensor(v3(wr, E0), v3(wr, E0), rsum.rearrange("p (t a) -> p t a", a=1).broadcast_to([P, NT, E0]),
                              ALU.mult).then_inc(sem("wr_done"), 1)

            hbx = hot_b.rearrange("p (j x) -> p j x", j=QT)
            with dve.Fori(0, NQ) as q:
                base = q * 4 + 9 * NQ
                n = [0]

                def step(ins):
                    n[0] += 1
                    ins.then_inc(sem("route_steps"), 1)
                    dve.wait_ge(sem("route_steps"), base + n[0])

                dve.wait_ge(sem("pos_psum"), q + 1)
                dve.scalar_tensor_tensor(out=key, in0=m_bf[:, bass.ds(q * (QT * E0), QT * E0)], scalar=-8192.0,
                                         in1=bank[5][:, 0:QT * E0], op0=ALU.mult, op1=ALU.add
                                         ).then_inc(sem("key_done"), 1)
                dve.wait_ge(sem("key_done"), 1 + (q + 1))
                step(dve.tensor_scalar(db_i, key, 7, None, ALU.bitwise_and))
                step(dve.tensor_scalar(da_i, key, 3, None, ALU.arith_shift_right))
                step(dve.tensor_copy(db, db_i))
                step(dve.tensor_scalar(da, da_i, 1024.0, None, ALU.add))
                assert n[0] == 4

                def digit(d, n_, buf, iot):
                    return dve.tensor_tensor(
                        buf, d.rearrange("p (a e) -> p a e", a=1).broadcast_to([P, n_, E0]),
                        iot[:, :].rearrange("p (a e) -> p a e", e=E0), ALU.is_equal)
                for j in range(QT):
                    dve.wait_ge(sem("lists_psum"), q * QT + (j + 1))
                    digit(db[:, j * E0:(j + 1) * E0], 8, hbx[:, j].rearrange("p (b e) -> p b e", e=E0), iota_b
                          ).then_inc(sem("hot_b_done"), 1)
                    dve.tensor_tensor(
                        hot_a.rearrange("p (j g a e) -> p j g a e", j=QT, g=8, a=16)[:, j],
                        da[:, j * E0:(j + 1) * E0].rearrange("p (g a e) -> p g a e", g=8, a=1
                                                             ).broadcast_to([P, 8, 16, 8]),
                        iota_a[:, :].rearrange("p (g a e) -> p g a e", g=8, a=16), ALU.is_equal
                    ).then_inc(sem("hot_a_done"), 1)
            dve.wait_ge(sem("lists_psum"), QT + NT)
            for b in range(2):
                bv_ = bank[6 + b][:, :].rearrange("p (g v x) -> p g v x", g=4, v=2)
                tv = [t_[:, b * 256:(b + 1) * 256].rearrange("p (g x) -> p g x", g=4) for t_ in tbl]
                link(dve.tensor_scalar(tv[0], bv_[:, :, 1, :], float(P), None, ALU.mult))
                link(dve.tensor_tensor(tv[1], bv_[:, :, 0, :], tv[0], ALU.add))
            link(dve.tensor_tensor(tbl[2][:, :].rearrange("p (x e) -> p x e", e=8),
                                   tbl[1][:, :].rearrange("p (x e) -> p x e", e=8),
                                   mod8[:, :].rearrange("p (a e) -> p a e", a=1).broadcast_to([P, 64, 8]), ALU.mult))
            dve.tensor_copy(filled[:, 0:1], mod8[:, 0:1]).then_inc(sem("tbl_done"), 1)
            dve.wait_ge(sem("slot_psum"), 1)
            link(dve.tensor_tensor(tbl[0][:, :].rearrange("p (g b e) -> p g b e", g=8, b=8),
                                   bank[3][:, :].rearrange("p (g b e) -> p g b e", g=8, b=8),
                                   mod8[:, :].rearrange("p (a b c) -> p a b c", a=1, c=1).broadcast_to([P, 8, 8, 8]),
                                   ALU.mult))
            link(dve.tensor_reduce(slot_tok[:, :].rearrange("p (g e) -> p g e", g=8),
                                   tbl[0][:, :].rearrange("p (g b e) -> p g e b", g=8, b=8), AX.X, ALU.add))
            dve.tensor_copy(gidx[:, :], slot_tok[:, :]).then_inc(sem("idx_done"), 1)
            dve.wait_ge(sem("cnt_psum"), 1)
            link(dve.tensor_copy(cnt[:, :], bank[5][:, 0:E0]))
            link(dve.tensor_scalar(filled[:, :], cnt[:, :], pcol[:, 0:1], None, ALU.is_gt))
            link(dve.tensor_scalar(slot_row[:, :], slot_tok[:, :], dump_row[:, 0:1], None, ALU.subtract))
            link(dve.tensor_tensor(slot_row[:, :], slot_row[:, :], filled[:, :], ALU.mult))
            link(dve.tensor_scalar(slot_row[:, :], slot_row[:, :], dump_row[:, 0:1], None, ALU.add))
            dve.tensor_copy(sidx[:, :], slot_row[:, :]).then_inc(sem("idx_done"), 1)
            dve.tensor_copy(rsum[:, 1:2], cnt[:, 0:1]).then_inc(sem("slot_done"), 1)

            def b_w2(t, u, r):
                if isinstance(t, int) and t < 2:
                    dve.wait_ge(sem("w2T_zero"), 2)
                after(dve, sem("w2T_psum"), t)
                after(dve, sem("y_psum"), t - 2)
                dve.tensor_copy(w2T[u][0:F0, 0:P], bank[1][0:F0, 0:P]).then_inc(sem("w2T_done"), 1)
                dve.tensor_copy(w2T[u][F0:P, P:2 * P], bank[1][F0:P, 0:P]).then_inc(sem("w2T_done"), 1)

            def b_hh(t, u, r):
                after(dve, sem("sil_done"), t)
                after(dve, sem("hhT_psum"), t - 2)
                dve.tensor_tensor(hh[u].rearrange("p (e f) -> p e f", e=2),
                                  bank[3][:, 0:2 * P].rearrange("p (e k f) -> p e k f", e=2, k=2)[:, :, 1, :],
                                  sil[u].rearrange("p (e f) -> p e f", e=2), ALU.mult).then_inc(sem("hh_done"), 1)

            def b_gi(t, u, r):
                after(dve, sem(f"xe_in{u}"), r - 1, 32)
                dve.tensor_copy(gi[u], gidx[:, at(t, 2)]).then_inc(sem("gi_done"), 1)

            def b_y(t, u, r):
                after(dve, sem("y_psum"), t)
                for j in range(2):
                    after(dve, sem(f"acc_done{j}"), t - RB_, 16)
                dve.tensor_copy(si[u], sidx[:, at(t, 2)])
                for j in range(2):
                    e = 2 * t + j if isinstance(t, int) else t * 2 + j
                    col = j * ROW + P + e
                    w = xe[u][:, col:col + 1] if isinstance(t, int) else xe[u][:, bass.ds(col, 1)]
                    m = dve.tensor_scalar(ye[u][:, j * P:(j + 1) * P], bank[5][:, j * P:(j + 1) * P], w, None, ALU.mult)
                m.then_inc(sem("ye_done"), 1)
            dve.wait_ge(sem("idx_done"), 2)
            pipeline(dve, NPAIR, RB_, [(0, b_gi), (1, b_w2), (2, b_hh), (3, b_y)])

            dve.wait_ge(sem("scaled"), HEAD_OK)

            def x2_there(t, u, r):
                after(dve, sem("x2_done"), t)

            c_sums, c_moments, c_var = norm_steps(x_all, cst, cmv, cve, "cve_done", x2_there)

            def c_xn(t, u, r):
                after(dve, sem("crs_done"), t)
                after(dve, sem("cxT_psum"), t - 2)
                dve.tensor_scalar(cxn[u], x_all[:, at(t)], cmv[u][:, 0:1], crs[u], ALU.subtract, ALU.mult
                                  ).then_inc(sem("cxn_done"), 1)

            def c_max(t, u, g):
                dve.wait_ge(sem("s_psum"), t * 4 + (g + 1))
                dve.tensor_reduce(smax[u][:, g * 4:g * 4 + 4], bank[S_BANK[g]][:, :].rearrange("p (h k) -> p h k", h=4),
                                  AX.X, ALU.max).then_inc(sem("smax_done"), 1)

            def c_nmax(t, u, g):
                dve.wait_ge(sem("smax_done"), t * 4 + (g + 1))
                after(dve, sem("pexp_done"), t - 2, 4)
                dve.tensor_scalar(nmax[u][:, g * 4:g * 4 + 4], smax[u][:, g * 4:g * 4 + 4], -float(HD) ** -0.5, None,
                                  ALU.mult).then_inc(sem("nmax_done"), 1)

            def c_ppT(t, u, g):
                dve.wait_ge(sem("ppT_psum"), t * 4 + (g + 1))
                after(dve, sem("pv_psum"), t - 2)
                dve.tensor_copy(ppT[u][:, g * 512:(g + 1) * 512], bank[5][:, :]).then_inc(sem("ppT_odd"), 1)

            def c_rec(t, u, r):
                after(dve, sem("pexp_done"), t, 4)
                after(dve, sem("srow_done"), t - 2)
                dve.reciprocal(srec[u], ssum_[u]).then_inc(sem("srec_done"), 1)

            def c_o(t, u, r):
                after(dve, sem("pv_psum"), t)
                after(dve, sem("rec_psum"), t)
                after(dve, sem("c_out_psum"), t - 2)
                dve.tensor_copy(srT[u], bank[7][:, P:2 * P]).then_inc(sem("srT_done"), 1)
                after(dve, sem("srT_done"), t)
                dve.tensor_tensor(oT[u], bank[7][:, 0:P], srT[u], ALU.mult).then_inc(sem("oT_done"), 1)

            def c_x3(t, u, r):
                after(dve, sem("c_out_psum"), t)
                after(dve, sem("x2b_done"), t)
                dve.tensor_tensor(x_all[:, at(t)], bank[7][:, 2 * P:3 * P], x2b[u], ALU.add).then_inc(sem("x3_done"), 1)

            def x3_there(t, u, r):
                after(dve, sem("x3_done"), t)

            d_sums, d_moments, d_var = norm_steps(x_all, dst, dmv, dve_, "dve_done", x3_there)

            def d_xn(t, u, r):
                after(dve, sem("drs_done"), t)
                after(dve, sem("dxT_psum"), t - RC)
                dve.tensor_scalar(dxn[u], x_all[:, at(t)], dmv[u][:, 0:1], drs[u], ALU.subtract, ALU.mult
                                  ).then_inc(sem("dxn_done"), 1)

            def d_keep(t, u, r):
                after(dve, sem("dxT_done"), t)
                dve.tensor_copy(xT_all[:, at(t)], dxT[u]).then_inc(sem("xT2_kept"), 1)

            of = lambda step, g: lambda t, u, r: step(t, u, g)
            pipeline(dve, NT, RC, [
                (1, c_xn), (4, c_rec), (5, c_x3), (6, d_xn), (2, of(c_max, 0)), (5, d_sums), (0, c_sums),
                (5, d_moments), (0, c_moments), (5, d_var), (2, of(c_nmax, 0)), (0, c_var), (3, of(c_ppT, 1)),
                (2, of(c_max, 1)), (4, c_o), (2, of(c_nmax, 1)), (2, of(c_max, 2)), (7, d_keep), (3, of(c_ppT, 3)),
                (2, of(c_nmax, 2)), (2, of(c_max, 3)), (2, of(c_nmax, 3)),
            ])

            dve.wait_ge(sem("w_late"), 16 * 5)
            dve.tensor_scalar(sw2[:, :], sw2[:, :], th[:, 3:4], None, ALU.mult).then_inc(sem("scaled"), 1)
            dve.tensor_scalar(ew2[:, :], ew2[:, :], th[:, 3:4], None, ALU.mult).then_inc(sem("scaled"), 1)

            selv, s8v_, s8xv, slv = v3(selx, 14), v3(s8, 8), v3(s8x, 8), v3(sleft, 14)
            link(dve.memset(selx, BIG))
            link(dve.memset(s8x, BIG))
            dve.wait_ge(sem("dsc_done"), 1)
            link(dve.tensor_tensor(selv[:, :, 0:8], v3(dsc, E1),
                                   rowv[:, RB:RB + E1].rearrange("p (a e) -> p a e", a=1).broadcast_to([P, NT, E1]),
                                   ALU.add))
            for t in range(NT):
                m = dve.max(s8v_[:, t], selv[:, t, 0:8])
            link(m)
            link(dve.tensor_copy(s8xv[:, :, 0:2], s8v_[:, :, 0:2]))
            for t in range(NT):
                m = dve.match_replace(out=slv[:, t], in_to_replace=s8xv[:, t], in_values=selv[:, t], imm_value=GONE)
            link(m)
            link(dve.tensor_scalar(v3(dmask, E1), slv[:, :, 0:8], GONE / 2, None, ALU.is_lt))
            link(dve.tensor_tensor(dgat, dsc, dmask, ALU.mult))
            link(dve.tensor_reduce(dden, v3(dgat, E1), AX.X, ALU.add))
            link(dve.tensor_scalar(dok, dden, 1e-9, None, ALU.is_gt))
            link(dve.tensor_scalar(dno, dok, -0.5, 0.5, ALU.mult, ALU.add))
            link(dve.tensor_scalar(dden, dden, 1e-9, None, ALU.add))
            link(dve.reciprocal(dden, dden))
            link(dve.tensor_tensor(dden, dden, dok, ALU.mult))
            bc = lambda b: b.rearrange("p (t a) -> p t a", a=1).broadcast_to([P, NT, E1])
            link(dve.tensor_tensor(v3(dgat, E1), v3(dgat, E1), bc(dden), ALU.mult))
            link(dve.tensor_tensor(v3(dalt, E1), v3(dmask, E1), bc(dno), ALU.mult))
            link(dve.tensor_tensor(dgat, dgat, dalt, ALU.add))

            with dve.Fori(0, NQ) as q:
                for c in range(2):
                    dve.wait_ge(sem("fg_done"), q * 2 + (c + 1))
                    dve.wait_ge(sem("fy_psum"), 1 + (q))
                    dve.tensor_tensor(fh[c], bank[3 - 2 * c][:, :], fg[c], ALU.mult).then_inc(sem("fh_done"), 1)
                dve.wait_ge(sem("fy_psum"), 1 + (q + 1))
                xq = x_all[:, bass.ds(q * 512, 512)]
                dve.tensor_tensor(xq, bank[2][:, :], xq, ALU.add).then_inc(sem("fx_done"), 1)
                dve.wait_ge(sem("fx_done"), 1 + (q + 1))
                for e in range(E1):
                    dve.wait_ge(sem("ey_psum"), 1 + (q * E1 + (e + 1)))
                    dve.wait_ge(sem("y_added"), 1 + ((q * E1 + e) * QT))
                    for j in range(QT):
                        xt = x_all[:, bass.ds((q * QT + j) * P, P)]
                        dve.scalar_tensor_tensor(out=xt, in0=bank[4 if e % 2 else 7][:, j * P:(j + 1) * P],
                                                 scalar=dgat[:, bass.ds((q * QT + j) * E1 + e, 1)], in1=xt,
                                                 op0=ALU.mult, op1=ALU.add).then_inc(sem("y_added"), 1)


_INS = ['x', 'ctx_1024', 'g_xattn', 'g_ffn', 'L0_xattn_w_sim', 'L0_xattn_b_sim', 'L0_xattn_W_qv', 'L0_xattn_b_qv',
        'L0_ffn_gate_weight', 'L0_ffn_e_bias', 'L0_ffn_w1', 'L0_ffn_w2', 'L0_ffn_w3', 'L0_ffn_shared_gate',
        'L0_ffn_shared_up', 'L0_ffn_shared_down', 'L1_xattn_Wq', 'L1_xattn_bq', 'L1_xattn_Wk', 'L1_xattn_bk',
        'L1_xattn_Wv', 'L1_xattn_bv', 'L1_xattn_Wo', 'L1_xattn_bo', 'L1_ffn_router_w', 'L1_ffn_router_bias',
        'L1_ffn_sw1', 'L1_ffn_sw3', 'L1_ffn_sw2', 'L1_ffn_ew1', 'L1_ffn_ew2']


def kernel(**inputs):
    import numpy as _np
    import concourse.bacc as _bacc
    from concourse import mybir as _mybir
    from concourse.bass_utils import run_bass_kernel_spmd as _run

    nc = _bacc.Bacc("TRN2", target_bir_lowering=False, num_devices=1)
    arrays, aps = {}, {}
    for name in _INS:
        a = _np.ascontiguousarray(inputs[name])
        arrays[f"in_{name}"] = a
        aps[name] = nc.dram_tensor(f"in_{name}", a.shape, _mybir.dt.from_np(a.dtype), kind="ExternalInput").ap()
    out = nc.dram_tensor("out_0", (NT, P, P), _mybir.dt.float32, kind="ExternalOutput").ap()
    build(nc, aps, out)
    r = _run(nc, [arrays], core_ids=[0])
    return r.results[0]["out_0"]
```

```python
from contextlib import ExitStack

import concourse.bass as bass
from concourse import mybir

F32 = mybir.dt.float32
BF16 = mybir.dt.bfloat16
F16 = mybir.dt.float16
I32 = mybir.dt.int32
ALU = mybir.AluOpType
ACT = mybir.ActivationFunctionType
AX = mybir.AxisListType

P = 128
NT = 32
QT = 4
NQ = NT // QT
E0 = 64
F0 = 64
G0 = 8
CAP = 128
NPAIR = E0 // 2
E1 = 8
HEADS = 16
HD = P // HEADS
EPS = 1e-5
ROUTE_SCALE = 2.5
BIG = 1e30
GONE = -1e30
ROW = P + E0
HALF = NT * P // 2
NROWS = NT * P + P


def at(t, n=P):
    return slice(t * n, (t + 1) * n) if isinstance(t, int) else bass.ds(t * n, n)


def after(eng, sem, t, per=1):
    if isinstance(t, int) and t < 0:
        return
    eng.wait_ge(sem, t * per + per)


def hold(eng, passed):
    eng.sem_inc(passed, 1)


def once_a_turn(step):
    return lambda t, u, r: step(r) if u == QT - 1 else None


def pipeline(eng, count, ring, stages):
    last = max(lag for lag, _ in stages)
    first = -(-(last + ring) // ring) * ring
    turns = (count - first) // ring

    def one(s):
        for lag, step in stages:
            t = s - lag
            if 0 <= t < count:
                step(t, t % ring, t // ring)

    for s in range(first):
        one(s)
    with eng.Fori(0, turns) as i:
        for v in range(ring):
            for lag, step in stages:
                c = first + v - lag
                step(i * ring + c, c % ring, i + c // ring)
    for s in range(first + turns * ring, count + last):
        one(s)


def build(nc, A, out):
    ctx = ExitStack()
    with ctx:
        def sb(name, cols, dt=F32, parts=P):
            return ctx.enter_context(nc.sbuf_tensor(name, [parts, cols], dt))

        sems = {}

        def sem(name):
            if name not in sems:
                sems[name] = ctx.enter_context(nc.semaphore(name))
            return sems[name]

        bank = [ctx.enter_context(nc.psum_tensor(f"bank{k}", [P, 512], F32)) for k in range(8)]

        rows_dram = nc.dram_tensor("token_rows", (NT * P, ROW), F32).ap()
        acc_dram = [nc.dram_tensor(f"expert_sums{j}", (NROWS, P), F32).ap() for j in range(2)]

        x_all = sb("x_all", NT * P)
        xT_all = sb("xT_all", NT * P)
        kT_all = sb("kT_all", NT * P)
        v_all = sb("v_all", NT * P)

        ident = sb("ident", P)
        ones = sb("ones", P)
        ones_bf = sb("ones_bf", P, BF16)
        tri_bf = sb("tri_bf", P, BF16)
        ipart = sb("ipart", 1, I32)
        pcol = sb("pcol", 1)
        dump_row = sb("dump_row", 1)
        tok_no = sb("tok_no", NT)
        itile = sb("itile", NT, I32)
        iota_a = sb("iota_a", 16 * E0, F16)
        iota_b = sb("iota_b", 8 * E0, F16)
        mod8 = sb("mod8", 8)
        imod8 = sb("imod8", 8, I32)
        same8 = sb("same8", P)
        head_m = sb("head_m", 4)
        ihead = sb("ihead", 4, I32)
        group_m = sb("group_m", 4)
        vmask = sb("vmask", 4 * P)
        half_pow = sb("half_pow", 4)
        zeros = sb("zeros", 1408)

        rowin = sb("rowin", 512, F32)
        rowv = sb("rowv", 512)
        BQV, EB, BO, RB, BSIM, GX, GF, BV = 0, 128, 192, 320, 328, 329, 331, 333
        th = sb("th", 4)
        wcol = sb("wcol", 3)
        bq = sb("bq", 1)
        bk = sb("bk", 1)
        bv = sb("bv", 1)
        w2b = sb("w2b", P)
        wqv = sb("wqv", 4 * P)
        wnat = sb("wnat", 8 * P)
        wT = sb("wT", 8 * P)
        GATE, SG, SU, SD, WQ, WK, WV, WO = range(8)
        rw_nat = sb("rw_nat", P)
        rwT = sb("rwT", P)
        bqv_row = sb("bqv_row", P)
        bo_row = sb("bo_row", P)
        bv_rep = sb("bv_rep", P)
        sw1 = sb("sw1", 256)
        sw3 = sb("sw3", 256)
        sw2 = sb("sw2", 256)
        ew1 = sb("ew1", E1 * P)
        ew2 = sb("ew2", E1 * P)

        arena = sb("arena", 26200)
        used = [0]

        def carve(cols, dt=F32):
            words = cols if dt in (F32, I32) else (cols + 1) // 2
            a = arena[:, used[0]:used[0] + words]
            used[0] += words
            assert used[0] <= 26200, used[0]
            return a if dt == F32 else a.bitcast(dt)

        RA = 4
        ctx_in = [carve(P) for _ in range(RA)]
        xn = [carve(P) for _ in range(RA)]
        eT = [carve(P) for _ in range(RA)]
        cT = [carve(P) for _ in range(RA)]
        cw = [carve(P) for _ in range(RA)]
        st = [carve(6) for _ in range(RA)]
        mv = [carve(2) for _ in range(RA)]
        ve = [carve(1) for _ in range(RA)]
        rstd = [carve(1) for _ in range(RA)]
        mraw = [carve(1) for _ in range(RA)]
        msim = [carve(1) for _ in range(RA)]
        nb = [carve(1) for _ in range(RA)]
        gmax = [carve(1) for _ in range(RA)]
        ngmax = [carve(1) for _ in range(RA)]
        eb = [carve(P) for _ in range(RA)]
        pr = [carve(P) for _ in range(RA)]
        prn = [carve(P) for _ in range(RA)]
        ssum = [carve(1) for _ in range(RA)]
        rs = [carve(1) for _ in range(RA)]
        pT = [carve(P) for _ in range(RA)]
        hq = [carve(P) for _ in range(RA)]
        ehT = [carve(P) for _ in range(RA)]
        ecT = [carve(P) for _ in range(RA)]
        hcr = [carve(1) for _ in range(RA)]
        hc = [carve(1) for _ in range(RA)]
        xb = [carve(P) for _ in range(RA)]
        st1 = [carve(6) for _ in range(RA)]
        mv1 = [carve(2) for _ in range(RA)]
        ve1 = [carve(1) for _ in range(RA)]
        rstd1 = [carve(1) for _ in range(RA)]
        xn1 = [carve(P) for _ in range(RA)]
        xn1T = [carve(P) for _ in range(RA)]
        end_a = used[0]

        logits = carve(NT * E0)
        sc = carve(NT * E0)
        sfc = carve(NT * E0)
        wr = logits
        m_bf = carve(NT * E0, BF16)
        s_bf = carve((NT + 1) * E0, BF16)
        t1 = carve(NT * 32)
        t2 = carve(NT * 32)
        t3 = carve(NT * 16)
        rsum = carve(NT)
        gsx = carve(QT * 12)
        g8 = carve(QT * 8)
        g8x = carve(QT * 8)
        gleft = carve(QT * 12)
        gmask = carve(QT * 8)
        tmp = carve(QT * E0)
        k8 = carve(QT * 8)
        kleft = carve(QT * E0)
        key = carve(QT * E0, I32)
        da_i = carve(QT * E0, I32)
        db_i = carve(QT * E0, I32)
        da = carve(QT * E0, F16)
        db = carve(QT * E0, F16)
        hot_a = carve(QT * 16 * E0, F16)
        hot_b = carve(QT * 8 * E0, F16)
        hot_v = carve(QT * 8 * E0, F16)
        tbl = [t1[:, 0:512], t1[:, 512:1024], t2[:, 0:512]]
        slot_tok = carve(E0)
        filled = carve(E0)
        cnt = carve(E0)
        slot_row = carve(E0)
        gidx = carve(E0, I32)
        sidx = carve(E0, I32)

        end_r = used[0]

        used[0] = 0
        RE = 4
        w1n = [carve(P) for _ in range(2)] * 2
        w3n = [carve(P) for _ in range(2)] * 2
        w2n = [carve(P) for _ in range(2)] * 2
        w13T = [carve(2 * P) for _ in range(2)] * 2
        w2T = [carve(2 * P) for _ in range(2)] * 2
        xe = [carve(2 * ROW) for _ in range(RE)]
        xeT = [carve(2 * P) for _ in range(2)] * 2
        sil = [carve(P) for _ in range(2)] * 2
        hh = [carve(P) for _ in range(2)] * 2
        hhT = [carve(P) for _ in range(2)] * 2
        ye = [carve(2 * P) for _ in range(RE)]
        gi = [carve(2, I32) for _ in range(RE)]
        si = [carve(2, I32) for _ in range(RE)]
        sh_s, sh_h = (carve(512) for _ in range(2))
        assert used[0] <= end_a

        RC = 4
        S_BANK = (1, 2, 3, 6)
        used[0] = end_a
        def two_turns(cols):
            return [carve(cols) for _ in range(2)] * 2

        a0, a1, x2 = two_turns(P), two_turns(P), two_turns(P)
        cst = [carve(6) for _ in range(RC)]
        cmv = [carve(2) for _ in range(RC)]
        cve = [carve(1) for _ in range(RC)]
        crs = [carve(1) for _ in range(RC)]
        cxn, cxT, qs = two_turns(P), two_turns(P), two_turns(P)
        qm, kbd, vbd = two_turns(512), two_turns(512), two_turns(512)
        smax, nmax = two_turns(HEADS), two_turns(HEADS)
        ssum_, srec = two_turns(HEADS), two_turns(HEADS)
        srow, srT = two_turns(P), two_turns(P)
        pexp = [carve(512) for _ in range(4)]
        ppT = two_turns(2048)
        oT, x2b = two_turns(P), two_turns(P)
        assert used[0] <= end_r

        used[0] = 0
        RD = RC
        dst = [carve(6) for _ in range(RD)]
        dmv = [carve(2) for _ in range(RD)]
        dve_ = [carve(1) for _ in range(RD)]
        drs = [carve(1) for _ in range(RD)]
        dxn = [carve(P) for _ in range(RD)]
        dxT = [carve(P) for _ in range(RD)]
        dlog = carve(NT * E1)
        dsc = carve(NT * E1)
        dmask = carve(NT * E1)
        dgat = carve(NT * E1)
        dalt = carve(NT * E1)
        dden = carve(NT)
        dok = carve(NT)
        dno = carve(NT)
        selx = carve(QT * 14)
        s8 = carve(QT * 8)
        s8x = carve(QT * 8)
        sleft = carve(QT * 14)
        fh = [carve(512) for _ in range(2)]
        fg = [carve(512) for _ in range(2)]
        eh = [carve(512) for _ in range(2)]
        assert used[0] <= end_a

        FREE_AT_START = dict(pe=("ey_psum", "fy_psum"), act=("eh_done",),
                             pool=(), dve=("key_done", "fh_done", "fx_done", "y_added"))

        def start(eng, name):
            for n in FREE_AT_START[name]:
                eng.sem_inc(sem(n), 1)

        def one_hot_b(eng, j):
            return eng.tensor_tensor(
                hot_b.rearrange("p (j b e) -> p j b e", j=QT, e=E0)[:, j],
                db[:, j * E0:(j + 1) * E0].rearrange("p (a e) -> p a e", a=1).broadcast_to([P, 8, E0]),
                iota_b[:, :].rearrange("p (a e) -> p a e", e=E0), ALU.is_equal)

        def one_hot_a(eng, j):
            return eng.tensor_tensor(
                hot_a.rearrange("p (j g a e) -> p j g a e", j=QT, g=8, a=16)[:, j],
                da[:, j * E0:(j + 1) * E0].rearrange("p (g a e) -> p g a e", g=8, a=1).broadcast_to([P, 8, 16, 8]),
                iota_a[:, :].rearrange("p (g a e) -> p g a e", g=8, a=16), ALU.is_equal)

        block = ctx.enter_context(nc.Block())

        IDENT_OK, ZEROS_OK, WCOL_OK, ROWV_OK, CONSTS_OK = 2, 5, 6, 7, 31
        BQV_OK, WQV_OK, HEAD_OK, BO_OK, WO_OK, SD_OK, SW_OK = 1, 2, 3, 4, 5, 6, 8

        @block.sync
        def _(sp):
            xd = A["x"].rearrange("t p d -> p t d")
            xv = x_all[:, :].rearrange("p (t d) -> p t d", d=P)
            sp.dma_start(xv[:, 0:8, :], xd[:, 0:8, :]).then_inc(sem("x_first"), 16)
            sp.dma_start(wcol[:, :], A["L0_xattn_w_sim"].rearrange("(c p) -> p c", p=P),
                         allow_slow_non_contiguous=True).then_inc(sem("x_first"), 16)

            def ctx_tile(t, u, r):
                after(sp, sem("hqT_done"), t - RA)
                sp.dma_start(ctx_in[u], A["ctx_1024"][t:t + 1, :, :].rearrange("t p d -> p (t d)") if isinstance(t, int)
                             else A["ctx_1024"][bass.ds(t, 1), :, :].rearrange("t p d -> p (t d)")
                             ).then_inc(sem(f"ctx_in{u}"), 16)

            def rows_out(t, u, r):
                after(sp, sem("xn1_done"), t)
                sp.dma_start(rows_dram[at(t), 0:P], xn1[u]).then_inc(sem(f"rows_out{u}"), 16)

            def rest(t, u, r):
                if isinstance(t, int) and t == 0:
                    for name, o, n in (("L0_xattn_b_qv", BQV, 128), ("L0_ffn_e_bias", EB, 64), ("L1_xattn_bo", BO, 128),
                                       ("L1_ffn_router_bias", RB, 8), ("L0_xattn_b_sim", BSIM, 1), ("g_xattn", GX, 2),
                                       ("g_ffn", GF, 2)):
                        sp.dma_start(rowin[0:1, o:o + n], A[name].rearrange("(a d) -> a d", a=1)).then_inc(sem("rows_in"), 16)
                elif isinstance(t, int) and t == 1:
                    for name, dst_ in (("L1_xattn_bq", bq), ("L1_xattn_bk", bk), ("L1_xattn_bv", bv)):
                        sp.dma_start(dst_[:, :], A[name].rearrange("(p c) -> p c", c=1)).then_inc(sem("cols_in"), 16)
                    sp.dma_start(wqv[:, :].rearrange("p (c n) -> p c n", c=4),
                                 A["L0_xattn_W_qv"].rearrange("(c p) n -> p c n", p=P)).then_inc(sem("wqv_in"), 16)
                elif isinstance(t, int) and t == 3:
                    sp.dma_start(xv[:, 8:NT, :], xd[:, 8:NT, :]).then_inc(sem("x_rest"), 16)

            pipeline(sp, NT, RA, [(0, ctx_tile), (0, rest), (5, rows_out)])

            sp.wait_ge(sem("pool_setup"), ZEROS_OK)
            for acc in acc_dram:
                av = acc.rearrange("(p r) d -> p (r d)", p=P)
                for k in range(3):
                    sp.dma_start(av[:, k * 1408:(k + 1) * 1408], zeros[:, :]).then_inc(sem("acc_zero"), 16)
            sp.dma_start(sw1[:, :], A["L1_ffn_sw1"]).then_inc(sem("w_late"), 16)
            sp.dma_start(sw3[:, :], A["L1_ffn_sw3"]).then_inc(sem("w_late"), 16)
            sp.dma_start(sw2[:, :].rearrange("p (c n) -> p c n", c=2),
                         A["L1_ffn_sw2"].rearrange("(c p) n -> p c n", p=P)).then_inc(sem("w_late"), 16)
            sp.dma_start(ew1[:, :].rearrange("p (e n) -> p e n", e=E1),
                         A["L1_ffn_ew1"].rearrange("e p n -> p e n")).then_inc(sem("w_late"), 16)
            sp.dma_start(ew2[:, :].rearrange("p (e n) -> p e n", e=E1),
                         A["L1_ffn_ew2"].rearrange("e p n -> p e n")).then_inc(sem("w_late"), 16)

            sp.wait_ge(sem("lg_done"), NT)
            for u in range(RA):
                sp.wait_ge(sem(f"rows_out{u}"), 16 * (NT // RA))

            sp.wait_ge(sem("wr_done"), 1)
            sp.dma_start(rows_dram[:, P:ROW].rearrange("(t p) e -> p t e", p=P),
                         wr.rearrange("p (t e) -> p t e", e=E0)).then_inc(sem("wr_out"), 16)

            def expert_weights(t, u, r):
                after(sp, sem("w2T_psum"), t - 2)
                for w, dst_ in (("L0_ffn_w1", w1n), ("L0_ffn_w3", w3n)):
                    src = A[w].rearrange("e f d -> (e f) d")
                    sp.dma_start(dst_[u], src[at(t), :]).then_inc(sem(f"w_in{u}"), 16)
                src = A["L0_ffn_w2"]
                e2 = src[2 * t:2 * t + 2] if isinstance(t, int) else src[bass.ds(t * 2, 2)]
                sp.dma_start(w2n[u].rearrange("p (e f) -> p e f", e=2),
                             e2.rearrange("e d f -> d e f")).then_inc(sem(f"w_in{u}"), 16)
            pipeline(sp, NPAIR, 2, [(0, expert_weights)])

            sp.wait_ge(sem("acc_done0"), 16 * NPAIR)
            sp.wait_ge(sem("acc_done1"), 16 * NPAIR)

            def sums_in(t, u, r):
                after(sp, sem("x2a"), t - 2)
                sp.dma_start(a0[u], acc_dram[0][at(t), :]).then_inc(sem(f"sums_in{u}"), 16)
                sp.dma_start(a1[u], acc_dram[1][at(t), :]).then_inc(sem(f"sums_in{u}"), 16)
            pipeline(sp, NT, 2, [(0, sums_in)])

            ov = out.rearrange("(q t) p d -> q p t d", t=QT)
            with sp.Fori(0, NQ) as q:
                sp.wait_ge(sem("y_added"), 1 + ((q * E1 + E1) * QT))
                sp.dma_start(ov[bass.ds(q, 1)].rearrange("q p t d -> p (q t) d"),
                             x_all[:, bass.ds(q * 512, 512)].rearrange("p (t d) -> p t d", d=P)
                             ).then_inc(sem("out_done"), 16)
            sp.wait_ge(sem("out_done"), 16 * NQ)

        @block.gpsimd
        def _(pool):
            k = [0]

            def link(ins):
                k[0] += 1
                ins.then_inc(sem("pool_setup"), 1)
                pool.wait_ge(sem("pool_setup"), k[0])

            start(pool, "pool")
            link(pool.memset(ident[:, :], 0.0))
            link(pool.affine_select(out=ident[:, :], in_=ident[:, :], compare_op=ALU.not_equal, fill=1.0, base=0,
                               pattern=[[-1, P]], channel_multiplier=1))
            assert k[0] == IDENT_OK
            link(pool.memset(ones[:, :], 1.0))
            link(pool.memset(half_pow[:, :], -0.5))
            link(pool.memset(zeros[:, :], 0.0))
            assert k[0] == ZEROS_OK
            pool.wait_ge(sem("x_first"), 32)
            link(pool.tensor_scalar(w2b[:, :], ones[:, :], wcol[:, 1:2], None, ALU.mult))
            assert k[0] == WCOL_OK

            def later_constants(part):
                if part == 0:
                    pool.wait_ge(sem("cols_in"), 16 * 3)
                    link(pool.tensor_scalar(bv_rep[:, :], ones[:, :], bv[:, 0:1], None, ALU.mult))
                    link(pool.memset(ones_bf[:, :], 1.0))
                    link(pool.memset(tri_bf[:, :], 1.0))
                    link(pool.affine_select(out=tri_bf[:, :], in_=tri_bf[:, :], compare_op=ALU.is_gt, fill=0.0, base=0,
                                            pattern=[[1, P]], channel_multiplier=-1))
                elif part == 1:
                    link(pool.iota(ipart[:, 0:1], pattern=[[1, 1]], base=0, channel_multiplier=1))
                    link(pool.tensor_copy(pcol[:, :], ipart[:, 0:1]))
                    link(pool.tensor_scalar(dump_row[:, :], pcol[:, :], 1.0, float(NT * P), ALU.mult, ALU.add))
                elif part == 2:
                    link(pool.iota(itile[:, :], pattern=[[P, NT]], base=-HALF, channel_multiplier=1))
                    link(pool.tensor_copy(tok_no[:, :], itile[:, :]))
                    link(pool.iota(imod8[:, :], pattern=[[-1, 8]], base=8, channel_multiplier=1))
                    link(pool.iota(ihead[:, :], pattern=[[-8, 4]], base=32, channel_multiplier=1))
                elif part == 3:
                    link(pool.iota(iota_a[:, :], pattern=[[0, 8], [1, 16], [0, 8]], base=0, channel_multiplier=0,
                                   allow_small_or_imprecise_dtypes=True))
                elif part == 4:
                    link(pool.iota(iota_b[:, :], pattern=[[1, 8], [0, E0]], base=0, channel_multiplier=0,
                                   allow_small_or_imprecise_dtypes=True))
                    link(pool.memset(same8[:, :], 1.0))
                elif part == 5:
                    sv = same8[:, :].rearrange("p (a b) -> p a b", b=8)
                    link(pool.affine_select(out=sv, in_=sv, compare_op=ALU.is_ge, fill=0.0, base=0,
                                            pattern=[[-8, 16], [0, 8]], channel_multiplier=1))
                    link(pool.affine_select(out=sv, in_=sv, compare_op=ALU.is_ge, fill=0.0, base=7,
                                            pattern=[[8, 16], [0, 8]], channel_multiplier=-1))
                elif part == 6:
                    link(pool.memset(group_m[:, :], 1.0))
                    link(pool.affine_select(out=group_m[:, :], in_=group_m[:, :], compare_op=ALU.is_ge, fill=0.0,
                                            base=0, pattern=[[-32, 4]], channel_multiplier=1))
                    link(pool.affine_select(out=group_m[:, :], in_=group_m[:, :], compare_op=ALU.is_ge, fill=0.0,
                                            base=31, pattern=[[32, 4]], channel_multiplier=-1))
                    link(pool.memset(vmask[:, :], 0.0))
                elif part == 7:
                    for h in range(4):
                        vh = vmask[:, h * P:(h + 1) * P].rearrange("p (g h d) -> p g h d", g=4, h=4)
                        link(pool.affine_select(out=vh, in_=vh, compare_op=ALU.not_equal, fill=1.0, base=-h,
                                                pattern=[[0, 4], [1, 4], [0, HD]], channel_multiplier=0))
                    assert k[0] == CONSTS_OK, k[0]

            def a_pow(t, u, r):
                after(pool, sem("ve_done"), t, 3)
                pool.tensor_tensor(rstd[u], ve[u], half_pow[:, 0:1], ALU.pow).then_inc(sem("rstd_done"), 1)

            def a_gmax(t, u, r):
                pool.wait_ge(sem("max_steps"), t * 3 + 2)
                hold(pool, sem("pool_passed"))
                pool.partition_all_reduce(gmax[u], msim[u], P, bass.bass_isa.ReduceOp.max).then_inc(sem("gmax_done"), 1)

            def a_bias(t, u, r):
                after(pool, sem("x1_done"), t - RA)
                if isinstance(t, int) and t == 0:
                    pool.wait_ge(sem("scaled"), BQV_OK)
                pool.tensor_tensor(xb[u], x_all[:, at(t)], bqv_row[:, :], ALU.add).then_inc(sem("xb_done"), 1)

            def a_pow1(t, u, r):
                after(pool, sem("ve1_done"), t, 3)
                pool.tensor_tensor(rstd1[u], ve1[u], half_pow[:, 0:1], ALU.pow).then_inc(sem("rstd1_done"), 1)

            def a_keep(t, u, r):
                after(pool, sem("xn1T_done"), t)
                pool.tensor_copy(xT_all[:, at(t)], xn1T[u]).then_inc(sem("xT_kept"), 1)

            def a_constants(t, u, r):
                if isinstance(t, int) and t == 0:
                    pool.wait_ge(sem("rows_in"), 16 * 7)
                    link(pool.partition_broadcast(rowv[:, 0:BV], rowin[0:1, 0:BV]))
                    assert k[0] == ROWV_OK
                elif isinstance(t, int) and t >= 2:
                    later_constants(t - 2)

            def a_running(t, u, r):
                if isinstance(t, int) and t == 0:
                    pool.memset(s_bf[:, 0:E0], 0.0).then_inc(sem("s_done"), 1)
                after(pool, sem("m_done"), r)
                after(pool, sem("s_done"), t)
                pool.tensor_tensor(s_bf[:, at(t + 1, E0)], s_bf[:, at(t, E0)], m_bf[:, at(t, E0)], ALU.add
                                   ).then_inc(sem("s_done"), 1)

            def a_chosen(q):
                after(pool, sem("m_done"), q)
                cols = at(q, QT * E0)
                pool.tensor_tensor(wr[:, cols], sc[:, cols], m_bf[:, cols], ALU.mult).then_inc(sem("chosen_done"), 1)

            pipeline(pool, NT, RA, [
                (2, a_gmax), (5, a_pow1), (6, a_keep), (0, a_pow), (13, once_a_turn(a_chosen)),
                (0, a_constants), (3, a_bias), (15, a_running),
            ])
            pool.wait_ge(sem("rsum_done"), 1)
            v3 = lambda b, n: b.rearrange("p (t e) -> p t e", e=n)
            pool.tensor_tensor(v3(wr, E0), v3(wr, E0), rsum.rearrange("p (t a) -> p t a", a=1).broadcast_to([P, NT, E0]),
                               ALU.mult).then_inc(sem("wr_done"), 1)

            for u in range(RA):
                pool.wait_ge(sem(f"rows_out{u}"), 16 * (NT // RA))
            pool.wait_ge(sem("lg_done"), NT)
            pool.wait_ge(sem("xn1T_psum"), NT)
            pool.wait_ge(sem("out_psum"), NT)
            for u in range(2):
                pool.memset(w2T[u], 0.0).then_inc(sem("w2T_zero"), 1)

            pool.wait_ge(sem("acc_zero"), 16 * 6)
            pool.wait_ge(sem("wr_out"), 16)
            pool.wait_ge(sem("idx_done"), 2)

            def gather(t, u, r):
                after(pool, sem("gi_done"), t)
                after(pool, sem("ye_done"), t - RE)
                for j in range(2):
                    hold(pool, sem("pool_passed"))
                    pool.indirect_dma_start(out=xe[u][:, j * ROW:(j + 1) * ROW], out_offset=None, in_=rows_dram,
                                            in_offset=bass.IndirectOffsetOnAxis(ap=gi[u][:, j:j + 1], axis=0)
                                            ).then_inc(sem(f"xe_in{u}"), 16)

            def scatter(t, u, r):
                after(pool, sem("ye_done"), t)
                for j in range(2):
                    after(pool, sem(f"acc_done{j}"), t - 1, 16)
                    hold(pool, sem("pool_passed"))
                    pool.indirect_dma_start(out=acc_dram[j], out_offset=bass.IndirectOffsetOnAxis(ap=si[u][:, j:j + 1], axis=0),
                                            in_=ye[u][:, j * P:(j + 1) * P], in_offset=None, compute_op=ALU.add,
                                            bounds_check=NROWS - 1, oob_is_err=True).then_inc(sem(f"acc_done{j}"), 16)

            pipeline(pool, NPAIR, RE, [(4, scatter), (0, gather)])

            pool.wait_ge(sem("v_done"), NT)
            pool.wait_ge(sem("shx_done"), NQ)

            def c_sum(t, u, r):
                after(pool, sem(f"sums_in{u % 2}"), r * 2 + u // 2, 32)
                after(pool, sem("x2_done"), t - 2)
                pool.tensor_tensor(x2[u], a0[u], a1[u], ALU.add).then_inc(sem("x2a"), 1)
                after(pool, sem("x2a"), t)
                pool.tensor_tensor(x_all[:, at(t)], x2[u], x_all[:, at(t)], ALU.add).then_inc(sem("x2_done"), 1)

            def c_pow(t, u, r):
                after(pool, sem("cve_done"), t, 3)
                pool.tensor_tensor(crs[u], cve[u], half_pow[:, 0:1], ALU.pow).then_inc(sem("crs_done"), 1)

            def c_k(t, u, r):
                after(pool, sem("s_psum"), t - 2, 4)
                pool.tensor_tensor(kbd[u].rearrange("p (h k) -> p h k", h=4),
                                   kT_all[:, at(t)].rearrange("p (a k) -> p a k", a=1).broadcast_to([P, 4, P]),
                                   head_m[:, :].rearrange("p (h a) -> p h a", a=1).broadcast_to([P, 4, P]),
                                   ALU.mult).then_inc(sem("kbd_done"), 1)

            def c_qm(t, u, r):
                after(pool, sem("q_done"), t)
                after(pool, sem("s_psum"), t - 2, 4)
                pool.tensor_tensor(qm[u].rearrange("p (g q) -> p g q", g=4),
                                   qs[u].rearrange("p (a q) -> p a q", a=1).broadcast_to([P, 4, P]),
                                   group_m[:, :].rearrange("p (g a) -> p g a", a=1).broadcast_to([P, 4, P]),
                                   ALU.mult).then_inc(sem("qm_done"), 1)

            def c_v(t, u, r):
                after(pool, sem("pv_psum"), t - 2)
                pool.tensor_tensor(vbd[u].rearrange("p (h k) -> p h k", h=4),
                                   v_all[:, at(t)].rearrange("p (a k) -> p a k", a=1).broadcast_to([P, 4, P]),
                                   vmask[:, :].rearrange("p (h k) -> p h k", h=4),
                                   ALU.mult).then_inc(sem("vbd_done"), 1)

            def c_row(t, u, r):
                after(pool, sem("srec_done"), t)
                after(pool, sem("rec_psum"), t - 2)
                pool.tensor_tensor(srow[u].rearrange("p (h d) -> p h d", d=HD),
                                   srec[u].rearrange("p (h a) -> p h a", a=1).broadcast_to([P, HEADS, HD]),
                                   ones[:, :].rearrange("p (h d) -> p h d", d=HD), ALU.mult).then_inc(sem("srow_done"), 1)

            def c_bias(t, u, r):
                after(pool, sem("x3_done"), t - 2)
                pool.tensor_tensor(x2b[u], x_all[:, at(t)], bo_row[:, :], ALU.add).then_inc(sem("x2b_done"), 1)

            def d_pow(t, u, r):
                after(pool, sem("dve_done"), t, 3)
                pool.tensor_tensor(drs[u], dve_[u], half_pow[:, 0:1], ALU.pow).then_inc(sem("drs_done"), 1)

            pipeline(pool, NT, RC, [(4, c_row), (0, c_sum), (1, c_k), (0, c_pow), (3, c_v), (5, d_pow), (1, c_qm),
                                    (4, c_bias)])

        @block.tensor
        def _(pe):
            def T(dst_, src, n=P):
                return pe.transpose(dst_, src, ident[0:n, 0:n])

            start(pe, "pe")
            pe.wait_ge(sem("pool_setup"), IDENT_OK)
            def a_T(t, u, r):
                after(pe, sem("xn_done"), t)
                after(pe, sem(f"ctx_in{u}"), r, 16)
                after(pe, sem("eT_done"), t - 1, 2)
                b = bank[0]
                T(b[:, 0:P], xn[u])
                T(b[:, P:2 * P], ctx_in[u]).then_inc(sem("T_psum"), 1)

            def a_S(t, u, r):
                after(pe, sem("eT_done"), t, 2)
                after(pe, sem("pr_done"), t - 1)
                b = bank[1]
                pe.matmul(b[:, 0:P], w2b[:, :], cT[u], start=True, stop=False)
                after(pe, sem("cw_done"), t)
                pe.matmul(b[:, 0:P], eT[u], cw[u], start=False, stop=True).then_inc(sem("sim_psum"), 1)

            def a_PT(t, u, r):
                after(pe, sem("prn_done"), t)
                after(pe, sem("pT_done"), t - 1)
                T(bank[2][:, 0:P], prn[u]).then_inc(sem("pT_psum"), 1)

            def a_HC(t, u, r):
                after(pe, sem("eb_done"), t)
                after(pe, sem("hc_steps"), t - 1, 3)
                b = bank[4]
                pe.matmul(b[:, 0:P], xn[u], eb[u], start=True, stop=True)
                pe.matmul(b[:, P:2 * P], ones[:, :], eb[u], start=True, stop=True).then_inc(sem("hc_psum"), 1)

            def a_HQ(t, u, r):
                after(pe, sem("pT_done"), t)
                after(pe, sem("hq_done"), t - 1)
                pe.matmul(bank[3][:, 0:P], ctx_in[u], pT[u], start=True, stop=True).then_inc(sem("hqT_done"), 1)

            def a_OUT(t, u, r):
                after(pe, sem("x1_done"), t - 1)
                b = bank[5][:, 0:P]
                pe.matmul(b, eT[u], wqv[:, 0:P], start=True, stop=False)
                after(pe, sem("hq_done"), t)
                pe.matmul(b, hq[u], wqv[:, P:2 * P], start=False, stop=False)
                after(pe, sem("hc_steps"), t, 3)
                pe.matmul(b, ecT[u], wqv[:, 3 * P:4 * P], start=False, stop=False)
                after(pe, sem("ehT_done"), t)
                pe.matmul(b, ehT[u], wqv[:, 2 * P:3 * P], start=False, stop=True).then_inc(sem("out_psum"), 1)

            def a_XT(t, u, r):
                after(pe, sem("xn1_done"), t)
                after(pe, sem("lg_done"), t - 1)
                T(bank[6][:, 0:P], xn1[u]).then_inc(sem("xn1T_psum"), 1)

            def a_LG(t, u, r):
                after(pe, sem("xn1T_done"), t)
                pe.matmul(bank[6][:, P:2 * P], xn1T[u], wT[:, GATE * P:(GATE + 1) * P], start=True, stop=True
                          ).then_inc(sem("lg_psum"), 1)

            def a_KV(t, u, r):
                after(pe, sem("v_done"), t - 1)
                b = bank[7]
                pe.matmul(b[:, 0:P], wT[:, WK * P:(WK + 1) * P], cT[u], start=True, stop=True)
                pe.matmul(b[:, P:2 * P], cT[u], wT[:, WV * P:(WV + 1) * P], start=True, stop=True
                          ).then_inc(sem("kv_psum"), 1)

            def a_weights(t, u, r):
                if not (isinstance(t, int) and t == 0):
                    return
                pe.wait_ge(sem("wnat_in"), 16 * 9)
                for k in range(8):
                    n = E0 if k == GATE else P
                    m = T(bank[4 + k // 4][:, (k % 4) * P:(k % 4) * P + n], wnat[0:n, k * P:(k + 1) * P], n)
                    if k % 4 == 3:
                        m.then_inc(sem("wT_psum"), 1)
                T(bank[6][:, 0:E1], rw_nat[0:E1, :], E1).then_inc(sem("wT_psum"), 1)
                pe.wait_ge(sem("wT_done"), 4)
                pe.wait_ge(sem("pool_setup"), WCOL_OK)
                pe.wait_ge(sem("scaled"), WQV_OK)

            pipeline(pe, NT, RA, [(2, a_S), (3, a_PT), (1, a_T), (1, a_weights), (4, a_OUT), (6, a_XT), (3, a_HC),
                                  (3, a_HQ), (2, a_KV), (6, a_LG)])

            pe.wait_ge(sem("hc_steps"), 3 * NT)
            pe.wait_ge(sem("pool_setup"), CONSTS_OK)
            pe.matmul(bank[4][:, 0:P], bv_rep[:, :], wT[:, WO * P:(WO + 1) * P], start=True, stop=True
                      ).then_inc(sem("bvo_psum"), 1)

            pe.wait_ge(sem("xT_kept"), NT)
            pe.wait_ge(sem("eT_done"), 2 * NT)
            pe.wait_ge(sem("pr_done"), NT)
            pe.wait_ge(sem("pT_done"), NT)

            pe.wait_ge(sem("pool_setup"), CONSTS_OK)
            pe.wait_ge(sem("lg_done"), NT)
            pe.wait_ge(sem("xn1T_done"), NT)
            pe.wait_ge(sem("x1_done"), NT)
            pe.wait_ge(sem("pool_setup"), ZEROS_OK)
            pe.matmul(bank[6][:, :], zeros[:, 0:P], zeros[:, 0:512], start=True, stop=False, skip_group_check=True)
            hb = hot_v.rearrange("p (j b e) -> p j b e", j=QT, e=E0)
            ha = hot_a.rearrange("p (j g x) -> p j g x", j=QT, g=8)
            pe.sem_inc(sem("lists_psum"), QT)

            def positions(q):
                pe.wait_ge(sem("s_done"), q * QT + (QT + 1))
                pe.wait_ge(sem("key_done"), 1 + q)
                cols = slice(0, QT * E0) if isinstance(q, int) else bass.ds(q * (QT * E0), QT * E0)
                pe.matmul(bank[5][:, 0:QT * E0], tri_bf[:, :], m_bf[:, cols], start=True, stop=False)
                pe.matmul(bank[5][:, 0:QT * E0], ones_bf[:, :], s_bf[:, cols], start=False, stop=True
                          ).then_inc(sem("pos_psum"), 1)

            def lists(q, j):
                pe.wait_ge(sem("hot_a_done"), q * QT + (j + 1))
                pe.wait_ge(sem("hot_v_done"), q * QT + (j + 1))
                for g in range(8):
                    m = pe.matmul(bank[6][:, g * 64:(g + 1) * 64], ha[:, j, g, :], hb[:, j, :, 8 * g:8 * g + 8],
                                  start=False, stop=False, skip_group_check=True)
                m.then_inc(sem("lists_psum"), 1)
            positions(0)
            with pe.Fori(0, NQ - 1) as q:
                lists(q, 0)
                positions(q + 1)
                for j in range(1, QT):
                    lists(q, j)
            for j in range(QT):
                lists(NQ - 1, j)
            pe.wait_ge(sem("s_done"), NT + 1)
            pe.wait_ge(sem("key_done"), 1 + (NQ))
            pe.matmul(bank[5][:, 0:E0], ones_bf[:, :], s_bf[:, NT * E0:(NT + 1) * E0], start=True, stop=True
                      ).then_inc(sem("cnt_psum"), 1)
            pe.wait_ge(sem("tbl_done"), 1)
            pe.wait_ge(sem("hq_done"), NT)
            pe.matmul(bank[3][:, :], same8[:, :], tbl[2][:, :], start=True, stop=True).then_inc(sem("slot_psum"), 1)

            pe.wait_ge(sem("idx_done"), 2)

            def b_W(t, u, r):
                after(pe, sem(f"w_in{u % 2}"), r * 2 + u // 2, 48)
                after(pe, sem("w13T_done"), t - 1)
                T(bank[0][:, 0:P], w1n[u])
                T(bank[0][:, P:2 * P], w3n[u]).then_inc(sem("w13T_psum"), 1)
                after(pe, sem("w2T_done"), t - 1, 2)
                T(bank[1][:, 0:P], w2n[u]).then_inc(sem("w2T_psum"), 1)

            def b_X(t, u, r):
                after(pe, sem(f"xe_in{u}"), r, 32)
                after(pe, sem("xeT_done"), t - 1)
                T(bank[2][:, 0:P], xe[u][:, 0:P])
                T(bank[2][:, P:2 * P], xe[u][:, ROW:ROW + P]).then_inc(sem("xeT_psum"), 1)

            def b_H(t, u, r):
                after(pe, sem("xeT_done"), t)
                after(pe, sem("w13T_done"), t)
                after(pe, sem("hh_done"), t - 1)
                for j in range(2):
                    m = pe.matmul(bank[3][:, j * P:(j + 1) * P], xeT[u][:, j * P:(j + 1) * P],
                                  w13T[u][:, j * P:(j + 1) * P], start=True, stop=True)
                m.then_inc(sem("h_psum"), 1)

            def b_HT(t, u, r):
                after(pe, sem("hh_done"), t)
                after(pe, sem("hhT_done"), t - 1)
                T(bank[4][:, 0:P], hh[u]).then_inc(sem("hhT_psum"), 1)

            def b_Y(t, u, r):
                after(pe, sem("hhT_done"), t)
                after(pe, sem("w2T_done"), t, 2)
                after(pe, sem("ye_done"), t - 1)
                pe.matmul(bank[5][:, 0:2 * P], hhT[u], w2T[u], start=True, stop=True).then_inc(sem("y_psum"), 1)

            pe.wait_ge(sem("scaled"), SD_OK)
            def sh_up(q):
                xq = at(q, QT * P)
                after(pe, sem("shx_done"), q - 1)
                pe.matmul(bank[6][:, :], wT[:, SG * P:(SG + 1) * P], xT_all[:, xq], start=True, stop=True)
                pe.matmul(bank[7][:, :], wT[:, SU * P:(SU + 1) * P], xT_all[:, xq], start=True, stop=True
                          ).then_inc(sem("sh_psum"), 1)

            def sh_down(q):
                after(pe, sem("shh_done"), q)
                for j in range(QT):
                    m = pe.matmul(bank[6][:, j * P:(j + 1) * P], sh_h[:, j * P:(j + 1) * P],
                                  wT[:, SD * P:(SD + 1) * P], start=True, stop=True)
                m.then_inc(sem("shy_psum"), 1)

            pipeline(pe, NPAIR, RE, [(1, b_W), (2, b_X), (3, b_HT), (2, b_H), (3, b_Y),
                                      (0, once_a_turn(sh_up)), (2, once_a_turn(sh_down))])

            pe.wait_ge(sem("ye_done"), NPAIR)
            pe.wait_ge(sem("w2T_done"), 2 * NPAIR)

            def c_XT(t, u, r):
                after(pe, sem("cxn_done"), t)
                after(pe, sem("dlog_done"), t - 6)
                T(bank[0][:, 0:P], cxn[u]).then_inc(sem("cxT_psum"), 1)

            def c_Q(t, u, r):
                after(pe, sem("cxT_done"), t)
                pe.matmul(bank[0][:, P:2 * P], wT[:, WQ * P:(WQ + 1) * P], cxT[u], start=True, stop=True
                          ).then_inc(sem("q_psum"), 1)

            def d_T(t, u, r):
                after(pe, sem("dxn_done"), t)
                after(pe, sem("dlog_done"), t - 1)
                after(pe, sem("q_done"), min(t + 5, NT - 1) if isinstance(t, int) else t + 5)
                T(bank[0][:, 2 * P:3 * P], dxn[u]).then_inc(sem("dxT_psum"), 1)

            def d_R(t, u, r):
                after(pe, sem("dxT_done"), t)
                pe.matmul(bank[0][:, 3 * P:4 * P], dxT[u], rwT[:, :], start=True, stop=True
                          ).then_inc(sem("dlog_psum"), 1)

            def c_S(t, u, g):
                if g == 0:
                    after(pe, sem("qm_done"), t)
                    after(pe, sem("kbd_done"), t)
                if not isinstance(t, int):
                    pe.wait_ge(sem("pexp_done"), t * 4 + (g - 3))
                elif t >= 1:
                    pe.wait_ge(sem("pexp_done"), 4 * t + g - 3)
                pe.matmul(bank[S_BANK[g]][:, :], qm[u][:, g * P:(g + 1) * P], kbd[u], start=True, stop=True
                          ).then_inc(sem("s_psum"), 1)

            def c_PT(t, u, g):
                pe.wait_ge(sem("pexp_done"), t * 4 + (g + 1))
                done = sem("ppT_even" if g % 2 == 0 else "ppT_odd")
                if not isinstance(t, int):
                    pe.wait_ge(done, t * 2 + g // 2)
                elif 2 * t + g // 2 > 0:
                    pe.wait_ge(done, 2 * t + g // 2)
                for h in range(4):
                    m = T(bank[4 + g % 2][:, h * P:(h + 1) * P], pexp[g][:, h * P:(h + 1) * P])
                m.then_inc(sem("ppT_psum"), 1)

            def c_PV(t, u, half):
                if half == 0:
                    after(pe, sem("ppT_even"), t, 2)
                    after(pe, sem("ppT_odd"), t, 2)
                    after(pe, sem("vbd_done"), t)
                    after(pe, sem("x3_done"), t - 1)
                for h in (2 * half, 2 * half + 1):
                    for g in range(4):
                        m = pe.matmul(bank[7][32 * g:32 * g + 32, 0:P], vbd[u][:, h * P + 32 * g:h * P + 32 * g + 32],
                                      ppT[u][:, (g * 4 + h) * P:(g * 4 + h + 1) * P],
                                      start=(h == 0), stop=(h == 3), skip_group_check=True)
                if half == 1:
                    m.then_inc(sem("pv_psum"), 1)

            def c_RT(t, u, r):
                after(pe, sem("srow_done"), t)
                T(bank[7][:, P:2 * P], srow[u]).then_inc(sem("rec_psum"), 1)

            def c_OUT(t, u, r):
                after(pe, sem("oT_done"), t)
                pe.matmul(bank[7][:, 2 * P:3 * P], oT[u], wT[:, WO * P:(WO + 1) * P], start=True, stop=True
                          ).then_inc(sem("c_out_psum"), 1)

            pe.wait_ge(sem("scaled"), WO_OK)
            of = lambda step, g: lambda t, u, r: step(t, u, g)
            pipeline(pe, NT, RC, [
                (3, of(c_PT, 0)), (2, of(c_S, 0)), (7, d_R), (4, of(c_PV, 0)),
                (3, of(c_PT, 1)), (2, of(c_S, 1)), (1, c_XT), (4, of(c_PV, 1)), (4, c_RT),
                (3, of(c_PT, 2)), (2, of(c_S, 2)), (1, c_Q), (3, of(c_PT, 3)), (4, c_OUT), (2, of(c_S, 3)),
                (6, d_T),
            ])

            pe.wait_ge(sem("pexp_done"), 4 * NT)
            pe.wait_ge(sem("ppT_even"), 2 * NT)
            pe.wait_ge(sem("ppT_odd"), 2 * NT)
            pe.wait_ge(sem("x3_done"), NT)
            pe.wait_ge(sem("w_late"), 16 * 5)
            pe.wait_ge(sem("scaled"), SW_OK)
            pe.wait_ge(sem("xT2_kept"), NT)
            pe.wait_ge(sem("dlog_done"), NT)
            def quad(q):
                return xT_all[:, q * 512:(q + 1) * 512] if isinstance(q, int) else xT_all[:, bass.ds(q * 512, 512)]

            def shared_up(q, c):
                if c == 0:
                    pe.wait_ge(sem("fx_done"), 1 + q)
                pe.wait_ge(sem("fh_done"), 1 + q * 2)
                pe.matmul(bank[2 - 2 * c][:, :], sw1[:, c * P:(c + 1) * P], quad(q), start=True, stop=True)
                pe.matmul(bank[3 - 2 * c][:, :], sw3[:, c * P:(c + 1) * P], quad(q), start=True, stop=True
                          ).then_inc(sem("f_psum"), 1)

            def shared_down(q):
                pe.wait_ge(sem("fh_done"), 1 + (q * 2 + 2))
                for j in range(QT):
                    for c in range(2):
                        m = pe.matmul(bank[2][:, j * P:(j + 1) * P], fh[c][:, j * P:(j + 1) * P],
                                      sw2[:, c * P:(c + 1) * P], start=(c == 0), stop=(c == 1))
                m.then_inc(sem("fy_psum"), 1)

            def up(q, e):
                pe.wait_ge(sem("eh_done"), 1 + (q * E1 + (e - 1) if e >= 1 else q * E1))
                pe.matmul(bank[5 + e % 2][:, :], ew1[:, e * P:(e + 1) * P], quad(q), start=True, stop=True
                          ).then_inc(sem("eh_psum"), 1)

            def down(q, e):
                pe.wait_ge(sem("eh_done"), 1 + (q * E1 + (e + 1)))
                if e >= 1:
                    pe.wait_ge(sem("y_added"), 1 + ((q * E1 + (e - 1)) * QT))
                else:
                    pe.wait_ge(sem("y_added"), 1 + (q * (E1 * QT)))
                for j in range(QT):
                    m = pe.matmul(bank[4 if e % 2 else 7][:, j * P:(j + 1) * P], eh[e % 2][:, j * P:(j + 1) * P],
                                  ew2[:, e * P:(e + 1) * P], start=True, stop=True)
                m.then_inc(sem("ey_psum"), 1)

            def routed(q, more):
                up(q, 0)
                up(q, 1)
                shared_down(q)
                for e in range(2, E1):
                    down(q, e - 2)
                    up(q, e)
                if more:
                    shared_up(q + 1, 0)
                down(q, E1 - 2)
                if more:
                    shared_up(q + 1, 1)
                down(q, E1 - 1)
            shared_up(0, 0)
            shared_up(0, 1)
            with pe.Fori(0, NQ - 1) as q:
                routed(q, True)
            routed(NQ - 1, False)

        @block.scalar
        def _(act):
            start(act, "act")
            wn = wnat[:, :].rearrange("p (k d) -> p k d", d=P)
            act.dma_start(wn[0:E0, GATE, :], A["L0_ffn_gate_weight"]).then_inc(sem("wnat_in"), 16)
            for name, k in (("L0_ffn_shared_gate", SG), ("L0_ffn_shared_up", SU), ("L0_ffn_shared_down", SD),
                            ("L1_xattn_Wq", WQ), ("L1_xattn_Wk", WK), ("L1_xattn_Wv", WV), ("L1_xattn_Wo", WO)):
                act.dma_start(wn[:, k, :], A[name]).then_inc(sem("wnat_in"), 16)
            act.dma_start(rw_nat[0:E1, :], A["L1_ffn_router_w"]).then_inc(sem("wnat_in"), 16)
            def a_weights(t, u, r):
                if not (isinstance(t, int) and t == 0):
                    return
                act.wait_ge(sem("pool_setup"), ROWV_OK)
                act.activation(th[:, :], rowv[:, GX:GX + 4], ACT.Tanh).then_inc(sem("th_done"), 1)
                act.wait_ge(sem("wT_zero"), 1)
                act.wait_ge(sem("wT_psum"), 3)
                act.activation(wT[:, 0:E0], bank[4][:, 0:E0], ACT.Copy).then_inc(sem("wT_done"), 1)
                act.activation(wT[:, P:4 * P], bank[4][:, P:4 * P], ACT.Copy).then_inc(sem("wT_done"), 1)
                act.activation(wT[:, 4 * P:8 * P], bank[5][:, :], ACT.Copy).then_inc(sem("wT_done"), 1)
                act.activation(rwT[:, 0:E1], bank[6][:, 0:E1], ACT.Copy).then_inc(sem("wT_done"), 1)

            def a_E(t, u, r):
                after(act, sem("T_psum"), t)
                if isinstance(t, int) and t == 0:
                    act.wait_ge(sem("x_first"), 32)
                after(act, sem("out_psum"), t - RA)
                after(act, sem("kv_psum"), t - RA)
                act.activation(cw[u], bank[0][:, P:2 * P], ACT.Identity, bias=wcol[:, 0:1], scale=wcol[:, 2:3]
                               ).then_inc(sem("cw_done"), 1)
                act.activation(cT[u], bank[0][:, P:2 * P], ACT.Copy).then_inc(sem("eT_done"), 1)
                act.activation(eT[u], bank[0][:, 0:P], ACT.Copy).then_inc(sem("eT_done"), 1)

            def a_exp(t, u, r):
                after(act, sem("max_steps"), t, 3)
                after(act, sem("prn_done"), t - RA)
                act.activation(pr[u], bank[1][:, 0:P], ACT.Exp, bias=nb[u], accum_out=ssum[u]
                               ).then_inc(sem("pr_done"), 1)

            def a_eb(t, u, r):
                after(act, sem("ngmax_done"), t)
                after(act, sem("hc_psum"), t - RA)
                act.activation(eb[u], msim[u].broadcast_to([P, P]), ACT.Exp, bias=ngmax[u]).then_inc(sem("eb_done"), 1)

            def a_prn(t, u, r):
                after(act, sem("rs_done"), t)
                after(act, sem("pT_psum"), t - RA)
                act.activation(prn[u], pr[u], ACT.Copy, scale=rs[u]).then_inc(sem("prn_done"), 1)

            def a_pT(t, u, r):
                after(act, sem("pT_psum"), t)
                after(act, sem("hqT_done"), t - RA)
                act.activation(pT[u], bank[2][:, 0:P], ACT.Copy).then_inc(sem("pT_done"), 1)

            def a_hq(t, u, r):
                after(act, sem("hqT_done"), t)
                after(act, sem("out_psum"), t - RA)
                act.activation(hq[u], bank[3][:, 0:P], ACT.Copy).then_inc(sem("hq_done"), 1)

            def a_x1T(t, u, r):
                after(act, sem("xn1T_psum"), t)
                after(act, sem("lg_psum"), t - RA)
                after(act, sem("xT_kept"), t - RA)
                act.activation(xn1T[u], bank[6][:, 0:P], ACT.Copy).then_inc(sem("xn1T_done"), 1)

            def a_lg(t, u, r):
                after(act, sem("lg_psum"), t)
                act.activation(logits[:, at(t, E0)], bank[6][:, P:P + E0], ACT.Copy).then_inc(sem("lg_done"), 1)

            def a_sc(q):
                after(act, sem("lg_done"), q, QT)
                act.activation(sc[:, at(q, QT * E0)], logits[:, at(q, QT * E0)], ACT.Sigmoid).then_inc(sem("sc_done"), 1)

            def a_kv(t, u, r):
                after(act, sem("kv_psum"), t)
                if isinstance(t, int) and t == 0:
                    act.wait_ge(sem("cols_in"), 16 * 3)
                act.activation(kT_all[:, at(t)], bank[7][:, 0:P], ACT.Identity, bias=bk[:, 0:1])
                act.activation(v_all[:, at(t)], bank[7][:, P:2 * P], ACT.Copy).then_inc(sem("v_done"), 1)

            pipeline(act, NT, RA, [
                (3, a_eb), (3, a_pT), (2, a_exp), (6, a_x1T), (1, a_E), (1, a_weights), (3, a_hq), (2, a_prn),
                (2, a_kv), (7, once_a_turn(a_sc)), (6, a_lg),
            ])

            for u in range(RA):
                act.wait_ge(sem(f"rows_out{u}"), 16 * (NT // RA))

            hvx, hbx = hot_v.rearrange("p (j x) -> p j x", j=QT), hot_b.rearrange("p (j x) -> p j x", j=QT)
            act.wait_ge(sem("pool_setup"), CONSTS_OK)
            with act.Fori(0, NQ) as q:
                for j in range(QT):
                    act.wait_ge(sem("hot_b_done"), q * QT + (j + 1))
                    act.wait_ge(sem("lists_psum"), q * QT + (j + 1))
                    act.activation(hvx[:, j], hbx[:, j], ACT.Copy, scale=tok_no[:, bass.ds(q * QT + j, 1)]
                                   ).then_inc(sem("hot_v_done"), 1)

            def b_w13(t, u, r):
                after(act, sem("w13T_psum"), t)
                after(act, sem("h_psum"), t - 2)
                act.activation(w13T[u].rearrange("p (e k f) -> p k e f", e=2, k=2),
                               bank[0][:, 0:2 * P].rearrange("p (k e f) -> p k e f", k=2, e=2), ACT.Copy
                               ).then_inc(sem("w13T_done"), 1)

            def b_xeT(t, u, r):
                after(act, sem("xeT_psum"), t)
                after(act, sem("h_psum"), t - 2)
                act.activation(xeT[u], bank[2][:, 0:2 * P], ACT.Copy).then_inc(sem("xeT_done"), 1)

            def b_silu(t, u, r):
                after(act, sem("h_psum"), t)
                after(act, sem("hh_done"), t - 2)
                act.activation(sil[u].rearrange("p (e f) -> p e f", e=2),
                               bank[3][:, 0:2 * P].rearrange("p (e k f) -> p e k f", e=2, k=2)[:, :, 0, :], ACT.Silu
                               ).then_inc(sem("sil_done"), 1)

            def b_hhT(t, u, r):
                after(act, sem("hhT_psum"), t)
                after(act, sem("y_psum"), t - 2)
                act.activation(hhT[u], bank[4][:, 0:P], ACT.Copy).then_inc(sem("hhT_done"), 1)

            def sh_silu(q):
                after(act, sem("sh_psum"), q)
                after(act, sem("shh_done"), q - 1)
                act.activation(sh_s, bank[6][:, :], ACT.Silu).then_inc(sem("shs_done"), 1)

            pipeline(act, NPAIR, RE, [
                (1, b_w13), (2, b_xeT), (1, once_a_turn(sh_silu)), (3, b_hhT), (2, b_silu),
            ])

            def c_xT(t, u, r):
                after(act, sem("cxT_psum"), t)
                after(act, sem("q_psum"), t - 2)
                act.activation(cxT[u], bank[0][:, 0:P], ACT.Copy).then_inc(sem("cxT_done"), 1)

            def c_exp(t, u, g):
                act.wait_ge(sem("nmax_done"), t * 4 + (g + 1))
                if not isinstance(t, int) or t >= 1:
                    act.wait_ge(sem("ppT_psum"), (t - 1) * 4 + (g + 1))
                after(act, sem("srec_done"), t - 2)
                for h in range(4):
                    c = g * 4 + h
                    m = act.activation(pexp[g][:, h * P:(h + 1) * P], bank[S_BANK[g]][:, h * P:(h + 1) * P], ACT.Exp,
                                       bias=nmax[u][:, c:c + 1], scale=float(HD) ** -0.5, accum_out=ssum_[u][:, c:c + 1])
                m.then_inc(sem("pexp_done"), 1)

            def c_ppT(t, u, g):
                act.wait_ge(sem("ppT_psum"), t * 4 + (g + 1))
                after(act, sem("pv_psum"), t - 2)
                act.activation(ppT[u][:, g * 512:(g + 1) * 512], bank[4][:, :], ACT.Copy).then_inc(sem("ppT_even"), 1)

            def d_t(t, u, r):
                after(act, sem("dxT_psum"), t)
                after(act, sem("dlog_psum"), t - RC)
                after(act, sem("xT2_kept"), t - RC)
                act.activation(dxT[u], bank[0][:, 2 * P:3 * P], ACT.Copy).then_inc(sem("dxT_done"), 1)

            def d_l(t, u, r):
                after(act, sem("dlog_psum"), t)
                act.activation(dlog[:, at(t, E1)], bank[0][:, 3 * P:3 * P + E1], ACT.Copy).then_inc(sem("dlog_done"), 1)

            of = lambda step, g: lambda t, u, r: step(t, u, g)
            pipeline(act, NT, RC, [
                (3, of(c_exp, 0)), (7, d_t), (3, of(c_exp, 1)), (7, d_l), (3, of(c_ppT, 0)), (3, of(c_exp, 2)),
                (1, c_xT), (3, of(c_exp, 3)), (3, of(c_ppT, 2)),
            ])
            act.wait_ge(sem("dlog_done"), NT)
            act.activation(dsc, dlog, ACT.Sigmoid).then_inc(sem("dsc_done"), 1)
            with act.Fori(0, NQ) as q:
                for c in range(2):
                    act.wait_ge(sem("f_psum"), q * 2 + (c + 1))
                    act.wait_ge(sem("fh_done"), 1 + q * 2)
                    act.activation(fg[c], bank[2 - 2 * c][:, :], ACT.Silu).then_inc(sem("fg_done"), 1)
                for e in range(E1):
                    act.wait_ge(sem("eh_psum"), q * E1 + (e + 1))
                    act.wait_ge(sem("ey_psum"), 1 + (q * E1 + (e - 1) if e >= 1 else q * E1))
                    act.activation(eh[e % 2], bank[5 + e % 2][:, :], ACT.Gelu).then_inc(sem("eh_done"), 1)

        @block.vector
        def _(dve):
            k = [0]

            def link(ins):
                k[0] += 1
                ins.then_inc(sem("dve_setup"), 1)
                dve.wait_ge(sem("dve_setup"), k[0])

            start(dve, "dve")
            dve.memset(rwT[:, :], 0.0)
            dve.memset(wT[:, 0:P], 0.0).then_inc(sem("wT_zero"), 1)
            def norm_steps(src, s_, m_, v_, stats, first=None):
                def sums(t, u, r):
                    if first:
                        first(t, u, r)
                    hold(dve, sem("dve_passed"))
                    dve.bn_stats(s_[u], src[:, at(t)]).then_inc(sem(stats), 1)

                def moments(t, u, r):
                    dve.wait_ge(sem(stats), t * 3 + 1)
                    hold(dve, sem("dve_passed"))
                    dve.bn_aggr(m_[u], s_[u]).then_inc(sem(stats), 1)

                def variance(t, u, r):
                    dve.wait_ge(sem(stats), t * 3 + 2)
                    dve.tensor_scalar(v_[u], m_[u][:, 1:2], EPS, None, ALU.add).then_inc(sem(stats), 1)
                return sums, moments, variance

            def x_there(t, u, r):
                if isinstance(t, int) and t in (0, 7):
                    dve.wait_ge(sem("x_first" if t == 0 else "x_rest"), 32 if t == 0 else 16)

            a_sums, a_moments, a_var = norm_steps(x_all, st, mv, ve, "ve_done", x_there)

            def a_xn(t, u, r):
                after(dve, sem("rstd_done"), t)
                after(dve, sem("hc_psum"), t - RA)
                dve.tensor_scalar(xn[u], x_all[:, at(t)], mv[u][:, 0:1], rstd[u], ALU.subtract, ALU.mult
                                  ).then_inc(sem("xn_done"), 1)

            def a_scaled(t, u, r):
                if not (isinstance(t, int) and t == 0):
                    return
                dve.wait_ge(sem("th_done"), 1)
                dve.tensor_scalar(bqv_row[:, :], rowv[:, BQV:BQV + P], th[:, 0:1], None, ALU.mult
                                  ).then_inc(sem("scaled"), 1)
                dve.wait_ge(sem("wqv_in"), 16)
                dve.tensor_scalar(wqv[:, :], wqv[:, :], th[:, 0:1], None, ALU.mult).then_inc(sem("scaled"), 1)

            def a_max(t, u, r):
                if isinstance(t, int) and t == 0:
                    dve.wait_ge(sem("pool_setup"), ROWV_OK)
                after(dve, sem("sim_psum"), t)
                dve.tensor_reduce(mraw[u], bank[1][:, 0:P], AX.X, ALU.max).then_inc(sem("max_steps"), 1)

            def a_msim(t, u, r):
                dve.wait_ge(sem("max_steps"), t * 3 + 1)
                dve.tensor_scalar(msim[u], mraw[u], rowv[:, BSIM:BSIM + 1], None, ALU.add).then_inc(sem("max_steps"), 1)

            def a_nb(t, u, r):
                dve.wait_ge(sem("max_steps"), t * 3 + 1)
                dve.tensor_scalar(nb[u], mraw[u], -1.0, None, ALU.mult).then_inc(sem("max_steps"), 1)

            def a_rs(t, u, r):
                after(dve, sem("pr_done"), t)
                dve.reciprocal(rs[u], ssum[u]).then_inc(sem("rs_done"), 1)

            def a_ng(t, u, r):
                after(dve, sem("gmax_done"), t)
                dve.tensor_scalar(ngmax[u], gmax[u], -1.0, None, ALU.mult).then_inc(sem("ngmax_done"), 1)

            def a_hcr(t, u, r):
                after(dve, sem("hc_psum"), t)
                dve.reciprocal(hcr[u], bank[4][:, P:P + 1]).then_inc(sem("hc_steps"), 1)

            def a_hc(t, u, r):
                dve.wait_ge(sem("hc_steps"), t * 3 + 1)
                dve.tensor_scalar(hc[u], bank[4][:, 0:1], hcr[u], None, ALU.mult).then_inc(sem("hc_steps"), 1)

            def a_ec(t, u, r):
                dve.wait_ge(sem("hc_steps"), t * 3 + 2)
                after(dve, sem("out_psum"), t - RA)
                dve.tensor_scalar(ecT[u], eT[u], hc[u], None, ALU.mult).then_inc(sem("hc_steps"), 1)

            def a_eh(t, u, r):
                after(dve, sem("hq_done"), t)
                dve.tensor_tensor(ehT[u], eT[u], hq[u], ALU.mult).then_inc(sem("ehT_done"), 1)

            def a_x1(t, u, r):
                after(dve, sem("out_psum"), t)
                after(dve, sem("xb_done"), t)
                dve.tensor_tensor(x_all[:, at(t)], bank[5][:, 0:P], xb[u], ALU.add).then_inc(sem("x1_done"), 1)

            def x1_there(t, u, r):
                after(dve, sem("x1_done"), t)

            b_sums, b_moments, b_var = norm_steps(x_all, st1, mv1, ve1, "ve1_done", x1_there)

            def a_xn1(t, u, r):
                after(dve, sem("rstd1_done"), t)
                after(dve, sem("xn1T_psum"), t - RA)
                after(dve, sem(f"rows_out{u}"), r - 1, 16)
                dve.tensor_scalar(xn1[u], x_all[:, at(t)], mv1[u][:, 0:1], rstd1[u], ALU.subtract, ALU.mult
                                  ).then_inc(sem("xn1_done"), 1)

            v3 = lambda b, n: b.rearrange("p (t e) -> p t e", e=n)
            gsxv, g8v, g8xv, glv, gmv = v3(gsx, 12), v3(g8, 8), v3(g8x, 8), v3(gleft, 12), v3(gmask, 8)
            tmv, k8v, klv = v3(tmp, E0), v3(k8, 8), v3(kleft, E0)
            NG = QT * G0
            hi4, lo4 = t1[:, 0:4 * NG].rearrange("p (n k) -> p n k", k=4), t2[:, 0:4 * NG].rearrange("p (n k) -> p n k", k=4)
            hi2, mi2, lo2, se2 = (b[:, 4 * NG + c * 2 * NG:4 * NG + (c + 1) * 2 * NG].rearrange("p (n k) -> p n k", k=2)
                                  for b in (t1, t2) for c in range(2))
            q3 = t3[:, 0:4 * NG].rearrange("p (c n a) -> p c n a", c=4, a=1)

            def choose(part):
                def step(q):
                    cols = at(q, QT * E0)

                    def needs(n):
                        dve.wait_ge(sem("choice"), q * 19 + n)
                    if part == 1:
                        after(dve, sem("sc_done"), q)
                        after(dve, sem("m_done"), q - 1)
                        ins = dve.tensor_tensor(v3(sfc[:, cols], E0), v3(sc[:, cols], E0),
                                                rowv[:, EB:EB + E0].rearrange("p (a e) -> p a e", a=1
                                                                              ).broadcast_to([P, QT, E0]), ALU.add)
                    sv_ = sfc[:, cols].rearrange("p (n k) -> p n k", k=8)
                    if part == 2:
                        needs(1)
                        ins = dve.tensor_tensor(hi4, sv_[:, :, 0:4], sv_[:, :, 4:8], ALU.max)
                    if part == 3:
                        needs(1)
                        ins = dve.tensor_tensor(lo4, sv_[:, :, 0:4], sv_[:, :, 4:8], ALU.min)
                    if part == 4:
                        needs(2)
                        ins = dve.tensor_tensor(hi2, hi4[:, :, 0:2], hi4[:, :, 2:4], ALU.max)
                    if part == 5:
                        needs(2)
                        ins = dve.tensor_tensor(mi2, hi4[:, :, 0:2], hi4[:, :, 2:4], ALU.min)
                    if part == 6:
                        needs(3)
                        ins = dve.tensor_tensor(lo2, lo4[:, :, 0:2], lo4[:, :, 2:4], ALU.max)
                    if part == 7:
                        needs(4)
                        ins = dve.tensor_tensor(q3[:, 0], hi2[:, :, 0:1], hi2[:, :, 1:2], ALU.max)
                    if part == 8:
                        needs(6)
                        ins = dve.tensor_tensor(se2, mi2, lo2, ALU.max)
                    if part == 9:
                        needs(4)
                        ins = dve.tensor_tensor(q3[:, 1], hi2[:, :, 0:1], hi2[:, :, 1:2], ALU.min)
                    if part == 10:
                        needs(8)
                        ins = dve.tensor_tensor(q3[:, 2], se2[:, :, 0:1], se2[:, :, 1:2], ALU.max)
                    if part == 11:
                        needs(10)
                        ins = dve.tensor_tensor(q3[:, 3], q3[:, 1], q3[:, 2], ALU.max)
                    if part == 12:
                        needs(11)
                        ins = dve.tensor_tensor(gsxv[:, :, 0:8], q3[:, 0].rearrange("p (t g) a -> p t (g a)", g=G0),
                                                q3[:, 3].rearrange("p (t g) a -> p t (g a)", g=G0), ALU.add)
                    if part == 13:
                        needs(12)
                        hold(dve, sem("dve_passed"))
                        for j in range(QT):
                            ins = dve.max(g8v[:, j], gsxv[:, j, 0:8])
                    if part == 14:
                        needs(13)
                        ins = dve.tensor_copy(g8xv[:, :, 0:4], g8v[:, :, 0:4])
                    if part == 15:
                        needs(14)
                        hold(dve, sem("dve_passed"))
                        for j in range(QT):
                            ins = dve.match_replace(out=glv[:, j], in_to_replace=g8xv[:, j], in_values=gsxv[:, j],
                                                    imm_value=GONE)
                    if part == 16:
                        needs(15)
                        ins = dve.tensor_scalar(gmv, glv[:, :, 0:8], GONE / 2, None, ALU.is_lt)
                    if part == 17:
                        needs(16)
                        ins = dve.tensor_tensor(tmp.rearrange("p (n k) -> p n k", k=8), sv_,
                                                gmask.rearrange("p (n a) -> p n a", a=1).broadcast_to([P, NG, 8]),
                                                ALU.mult)
                    if part == 18:
                        needs(17)
                        hold(dve, sem("dve_passed"))
                        for j in range(QT):
                            ins = dve.max(k8v[:, j], tmv[:, j])
                    if part == 19:
                        needs(18)
                        hold(dve, sem("dve_passed"))
                        for j in range(QT):
                            ins = dve.match_replace(out=klv[:, j], in_to_replace=k8v[:, j], in_values=tmv[:, j],
                                                    imm_value=GONE)
                    if part == 20:
                        needs(19)
                        dve.tensor_scalar(m_bf[:, cols], kleft, GONE / 2, None, ALU.is_lt).then_inc(sem("m_done"), 1)
                    else:
                        ins.then_inc(sem("choice"), 1)
                return once_a_turn(step)

            def choices(k):
                return [(8, choose(k)), (9, choose(5 + k)), (10, choose(10 + k)), (11, choose(15 + k))]

            dve.memset(gsx, BIG)
            link(dve.memset(g8x, BIG))
            pipeline(dve, NT, RA, [
                (3, a_ng), (1, a_xn), (1, a_scaled), (5, a_x1), *choices(1), (2, a_max), (5, b_sums),
                (2, a_msim), (5, b_moments), (2, a_nb), *choices(2), (5, b_var), (0, a_sums), *choices(3),
                (0, a_moments), (3, a_hcr), (2, a_rs), (0, a_var), *choices(4), (3, a_hc), *choices(5),
                (3, a_ec), (3, a_eh), (5, a_xn1),
            ])

            dve.wait_ge(sem("pool_setup"), CONSTS_OK)
            link(dve.tensor_scalar(imod8[:, :], imod8[:, :], 7, None, ALU.bitwise_and))
            link(dve.tensor_scalar(mod8[:, :], imod8[:, :], 0, None, ALU.is_equal))
            link(dve.tensor_scalar(ihead[:, :], ihead[:, :], 3, 3, ALU.logical_shift_right, ALU.bitwise_and))
            dve.tensor_scalar(head_m[:, :], ihead[:, :], 0, None, ALU.is_equal).then_inc(sem("scaled"), 1)

            dve.wait_ge(sem("m_done"), NQ)
            dve.wait_ge(sem("chosen_done"), NQ)
            link(dve.tensor_reduce(rsum, v3(wr, E0), AX.X, ALU.add))
            link(dve.tensor_scalar(rsum, rsum, 1e-20, None, ALU.add))
            link(dve.reciprocal(rsum, rsum))
            dve.tensor_scalar(rsum, rsum, ROUTE_SCALE, th[:, 2:3], ALU.mult, ALU.mult).then_inc(sem("rsum_done"), 1)

            def keys(q):
                dve.wait_ge(sem("pos_psum"), q + 1)
                dve.scalar_tensor_tensor(out=key, in0=m_bf[:, at(q, QT * E0)], scalar=-8192.0,
                                         in1=bank[5][:, 0:QT * E0], op0=ALU.mult, op1=ALU.add
                                         ).then_inc(sem("key_done"), 1)

            def digits(q):
                dve.wait_ge(sem("key_done"), 1 + (q + 1))
                dve.tensor_scalar(db_i, key, 7, None, ALU.bitwise_and).then_inc(sem("digits"), 1)
                dve.tensor_scalar(da_i, key, 3, None, ALU.arith_shift_right).then_inc(sem("digits"), 1)

            def digits_as_halves(q):
                after(dve, sem("hot_b_done"), q - 1, QT)
                after(dve, sem("hot_a_done"), q - 1, QT)
                dve.wait_ge(sem("digits"), q * 4 + 1)
                dve.tensor_copy(db, db_i).then_inc(sem("digits"), 1)
                dve.wait_ge(sem("digits"), q * 4 + 2)
                dve.tensor_scalar(da, da_i, 1024.0, None, ALU.add).then_inc(sem("digits"), 1)

            def one_hots(q, j):
                if j == 0:
                    dve.wait_ge(sem("digits"), q * 4 + 3)
                dve.wait_ge(sem("lists_psum"), q * QT + (j + 1))
                one_hot_b(dve, j).then_inc(sem("hot_b_done"), 1)
                if j == 0:
                    dve.wait_ge(sem("digits"), q * 4 + 4)
                one_hot_a(dve, j).then_inc(sem("hot_a_done"), 1)

            keys(0)
            digits(0)
            digits_as_halves(0)
            with dve.Fori(0, NQ - 1) as q:
                one_hots(q, 0)
                one_hots(q, 1)
                one_hots(q, 2)
                keys(q + 1)
                one_hots(q, 3)
                digits(q + 1)
                digits_as_halves(q + 1)
            for j in range(QT):
                one_hots(NQ - 1, j)
            dve.wait_ge(sem("lists_psum"), QT + NT)
            dve.tensor_tensor(tbl[2][:, :].rearrange("p (x e) -> p x e", e=8),
                              bank[6][:, :].rearrange("p (x e) -> p x e", e=8),
                              mod8[:, :].rearrange("p (a e) -> p a e", a=1).broadcast_to([P, 64, 8]), ALU.mult
                              ).then_inc(sem("tbl_done"), 1)
            dve.wait_ge(sem("cnt_psum"), 1)
            link(dve.tensor_copy(cnt[:, :], bank[5][:, 0:E0]))
            link(dve.tensor_scalar(filled[:, :], cnt[:, :], pcol[:, 0:1], None, ALU.is_gt))
            dve.wait_ge(sem("bvo_psum"), 1)
            link(dve.tensor_tensor(bo_row[:, :], bank[4][:, 0:P], rowv[:, BO:BO + P], ALU.add))
            dve.tensor_scalar(bo_row[:, :], bo_row[:, :], th[:, 1:2], None, ALU.mult).then_inc(sem("scaled"), 1)
            dve.tensor_scalar(wT[:, WO * P:(WO + 1) * P], wT[:, WO * P:(WO + 1) * P], th[:, 1:2], None, ALU.mult
                              ).then_inc(sem("scaled"), 1)
            dve.tensor_scalar(wT[:, SD * P:(SD + 1) * P], wT[:, SD * P:(SD + 1) * P], th[:, 2:3], None, ALU.mult
                              ).then_inc(sem("scaled"), 1)
            dve.wait_ge(sem("slot_psum"), 1)
            link(dve.tensor_tensor(tbl[0][:, :].rearrange("p (g b e) -> p g b e", g=8, b=8),
                                   bank[3][:, :].rearrange("p (g b e) -> p g b e", g=8, b=8),
                                   mod8[:, :].rearrange("p (a b c) -> p a b c", a=1, c=1).broadcast_to([P, 8, 8, 8]),
                                   ALU.mult))
            link(dve.tensor_reduce(slot_tok[:, :].rearrange("p (g e) -> p g e", g=8),
                                   tbl[0][:, :].rearrange("p (g b e) -> p g e b", g=8, b=8), AX.X, ALU.add))
            link(dve.tensor_scalar(slot_tok[:, :], slot_tok[:, :], float(HALF), None, ALU.add))
            dve.tensor_copy(gidx[:, :], slot_tok[:, :]).then_inc(sem("idx_done"), 1)
            link(dve.tensor_scalar(slot_row[:, :], slot_tok[:, :], dump_row[:, 0:1], None, ALU.subtract))
            link(dve.tensor_tensor(slot_row[:, :], slot_row[:, :], filled[:, :], ALU.mult))
            link(dve.tensor_scalar(slot_row[:, :], slot_row[:, :], dump_row[:, 0:1], None, ALU.add))
            dve.tensor_copy(sidx[:, :], slot_row[:, :]).then_inc(sem("idx_done"), 1)

            def b_w2(t, u, r):
                if isinstance(t, int) and t < 2:
                    dve.wait_ge(sem("w2T_zero"), 2)
                after(dve, sem("w2T_psum"), t)
                after(dve, sem("y_psum"), t - 2)
                dve.tensor_copy(w2T[u][0:F0, 0:P], bank[1][0:F0, 0:P]).then_inc(sem("w2T_done"), 1)
                dve.tensor_copy(w2T[u][F0:P, P:2 * P], bank[1][F0:P, 0:P]).then_inc(sem("w2T_done"), 1)

            def b_hh(t, u, r):
                after(dve, sem("sil_done"), t)
                after(dve, sem("hhT_psum"), t - 2)
                dve.tensor_tensor(hh[u].rearrange("p (e f) -> p e f", e=2),
                                  bank[3][:, 0:2 * P].rearrange("p (e k f) -> p e k f", e=2, k=2)[:, :, 1, :],
                                  sil[u].rearrange("p (e f) -> p e f", e=2), ALU.mult).then_inc(sem("hh_done"), 1)

            def b_gi(t, u, r):
                after(dve, sem(f"xe_in{u}"), r - 1, 32)
                dve.tensor_copy(gi[u], gidx[:, at(t, 2)]).then_inc(sem("gi_done"), 1)

            def b_y(t, u, r):
                after(dve, sem("y_psum"), t)
                for j in range(2):
                    after(dve, sem(f"acc_done{j}"), t - RE, 16)
                dve.tensor_copy(si[u], sidx[:, at(t, 2)])
                for j in range(2):
                    e = 2 * t + j if isinstance(t, int) else t * 2 + j
                    col = j * ROW + P + e
                    w = xe[u][:, col:col + 1] if isinstance(t, int) else xe[u][:, bass.ds(col, 1)]
                    m = dve.tensor_scalar(ye[u][:, j * P:(j + 1) * P], bank[5][:, j * P:(j + 1) * P], w, None, ALU.mult)
                m.then_inc(sem("ye_done"), 1)
            dve.wait_ge(sem("idx_done"), 2)

            def sh_product(q):
                after(dve, sem("shs_done"), q)
                after(dve, sem("shy_psum"), q - 1)
                dve.tensor_tensor(sh_h, bank[7][:, :], sh_s, ALU.mult).then_inc(sem("shh_done"), 1)

            def sh_add(q):
                after(dve, sem("shy_psum"), q)
                xq = x_all[:, at(q, QT * P)]
                dve.tensor_tensor(xq, bank[6][:, :], xq, ALU.add).then_inc(sem("shx_done"), 1)

            pipeline(dve, NPAIR, RE, [
                (0, b_gi), (1, b_w2), (3, b_y), (1, once_a_turn(sh_product)), (3, once_a_turn(sh_add)),
                (2, b_hh),
            ])

            dve.wait_ge(sem("w_late"), 16 * 5)
            dve.tensor_scalar(sw2[:, :], sw2[:, :], th[:, 3:4], None, ALU.mult).then_inc(sem("scaled"), 1)
            dve.tensor_scalar(ew2[:, :], ew2[:, :], th[:, 3:4], None, ALU.mult).then_inc(sem("scaled"), 1)

            dve.wait_ge(sem("scaled"), HEAD_OK)

            def x2_there(t, u, r):
                after(dve, sem("x2_done"), t)

            c_sums, c_moments, c_var = norm_steps(x_all, cst, cmv, cve, "cve_done", x2_there)

            def c_xn(t, u, r):
                after(dve, sem("crs_done"), t)
                after(dve, sem("cxT_psum"), t - 2)
                dve.tensor_scalar(cxn[u], x_all[:, at(t)], cmv[u][:, 0:1], crs[u], ALU.subtract, ALU.mult
                                  ).then_inc(sem("cxn_done"), 1)

            def c_max(t, u, g):
                dve.wait_ge(sem("s_psum"), t * 4 + (g + 1))
                dve.tensor_reduce(smax[u][:, g * 4:g * 4 + 4], bank[S_BANK[g]][:, :].rearrange("p (h k) -> p h k", h=4),
                                  AX.X, ALU.max).then_inc(sem("smax_done"), 1)

            def c_nmax(t, u, g):
                dve.wait_ge(sem("smax_done"), t * 4 + (g + 1))
                after(dve, sem("pexp_done"), t - 2, 4)
                dve.tensor_scalar(nmax[u][:, g * 4:g * 4 + 4], smax[u][:, g * 4:g * 4 + 4], -float(HD) ** -0.5, None,
                                  ALU.mult).then_inc(sem("nmax_done"), 1)

            def c_q(t, u, r):
                after(dve, sem("q_psum"), t)
                after(dve, sem("qm_done"), t - 2)
                dve.tensor_scalar(qs[u], bank[0][:, P:2 * P], bq[:, 0:1], None, ALU.add).then_inc(sem("q_done"), 1)

            def c_ppT(t, u, g):
                dve.wait_ge(sem("ppT_psum"), t * 4 + (g + 1))
                after(dve, sem("pv_psum"), t - 2)
                dve.tensor_copy(ppT[u][:, g * 512:(g + 1) * 512], bank[5][:, :]).then_inc(sem("ppT_odd"), 1)

            def c_rec(t, u, r):
                after(dve, sem("pexp_done"), t, 4)
                after(dve, sem("srow_done"), t - 2)
                dve.reciprocal(srec[u], ssum_[u]).then_inc(sem("srec_done"), 1)

            def c_o(t, u, r):
                after(dve, sem("pv_psum"), t)
                after(dve, sem("rec_psum"), t)
                after(dve, sem("c_out_psum"), t - 2)
                dve.tensor_copy(srT[u], bank[7][:, P:2 * P]).then_inc(sem("srT_done"), 1)
                after(dve, sem("srT_done"), t)
                dve.tensor_tensor(oT[u], bank[7][:, 0:P], srT[u], ALU.mult).then_inc(sem("oT_done"), 1)

            def c_x3(t, u, r):
                after(dve, sem("c_out_psum"), t)
                after(dve, sem("x2b_done"), t)
                dve.tensor_tensor(x_all[:, at(t)], bank[7][:, 2 * P:3 * P], x2b[u], ALU.add).then_inc(sem("x3_done"), 1)

            def x3_there(t, u, r):
                after(dve, sem("x3_done"), t)

            d_sums, d_moments, d_var = norm_steps(x_all, dst, dmv, dve_, "dve_done", x3_there)

            def d_xn(t, u, r):
                after(dve, sem("drs_done"), t)
                after(dve, sem("dxT_psum"), t - RC)
                dve.tensor_scalar(dxn[u], x_all[:, at(t)], dmv[u][:, 0:1], drs[u], ALU.subtract, ALU.mult
                                  ).then_inc(sem("dxn_done"), 1)

            def d_keep(t, u, r):
                after(dve, sem("dxT_done"), t)
                dve.tensor_copy(xT_all[:, at(t)], dxT[u]).then_inc(sem("xT2_kept"), 1)

            of = lambda step, g: lambda t, u, r: step(t, u, g)
            pipeline(dve, NT, RC, [
                (4, c_rec), (5, c_x3), (6, d_xn), (1, c_xn), (2, of(c_max, 0)), (5, d_sums), (0, c_sums),
                (5, d_moments), (0, c_moments), (2, of(c_max, 1)), (5, d_var), (2, of(c_nmax, 0)), (0, c_var),
                (3, of(c_ppT, 1)), (4, c_o), (2, of(c_nmax, 1)), (2, of(c_max, 2)), (1, c_q), (7, d_keep),
                (3, of(c_ppT, 3)), (2, of(c_nmax, 2)), (2, of(c_max, 3)), (2, of(c_nmax, 3)),
            ])


            def gates(q, part):
                cols, tiles, n = at(q, QT * E1), at(q, QT), [0]
                first = (1, 3, 5, 7, 9, 11, 13, 16)[part]

                def step(ins):
                    ins.then_inc(sem("gates"), 1)
                    n[0] += 1
                    dve.wait_ge(sem("gates"), q * 15 + (first - 1 + n[0]))

                row = lambda b: b[:, tiles].rearrange("p (t a) -> p t a", a=1).broadcast_to([P, QT, E1])
                selv, s8v_, s8xv, slv = v3(selx, 14), v3(s8, 8), v3(s8x, 8), v3(sleft, 14)
                if part == 0:
                    step(dve.tensor_tensor(selv[:, :, 0:8], v3(dsc[:, cols], E1),
                                           rowv[:, RB:RB + E1].rearrange("p (a e) -> p a e", a=1
                                                                         ).broadcast_to([P, QT, E1]), ALU.add))
                    hold(dve, sem("dve_passed"))
                    for j in range(QT):
                        m = dve.max(s8v_[:, j], selv[:, j, 0:8])
                    step(m)
                elif part == 1:
                    step(dve.tensor_copy(s8xv[:, :, 0:2], s8v_[:, :, 0:2]))
                    hold(dve, sem("dve_passed"))
                    for j in range(QT):
                        m = dve.match_replace(out=slv[:, j], in_to_replace=s8xv[:, j], in_values=selv[:, j],
                                              imm_value=GONE)
                    step(m)
                elif part == 2:
                    step(dve.tensor_scalar(v3(dmask[:, cols], E1), slv[:, :, 0:8], GONE / 2, None, ALU.is_lt))
                    step(dve.tensor_tensor(dgat[:, cols], dsc[:, cols], dmask[:, cols], ALU.mult))
                elif part == 3:
                    step(dve.tensor_reduce(dden[:, tiles], v3(dgat[:, cols], E1), AX.X, ALU.add))
                    step(dve.tensor_scalar(dok[:, tiles], dden[:, tiles], 1e-9, None, ALU.is_gt))
                elif part == 4:
                    step(dve.tensor_scalar(dno[:, tiles], dok[:, tiles], -0.5, 0.5, ALU.mult, ALU.add))
                    step(dve.tensor_scalar(dden[:, tiles], dden[:, tiles], 1e-9, None, ALU.add))
                elif part == 5:
                    step(dve.reciprocal(dden[:, tiles], dden[:, tiles]))
                    step(dve.tensor_tensor(dden[:, tiles], dden[:, tiles], dok[:, tiles], ALU.mult))
                elif part == 6:
                    step(dve.tensor_tensor(v3(dgat[:, cols], E1), v3(dgat[:, cols], E1), row(dden), ALU.mult))
                    step(dve.tensor_tensor(v3(dalt[:, cols], E1), v3(dmask[:, cols], E1), row(dno), ALU.mult))
                    step(dve.tensor_tensor(dgat[:, cols], dgat[:, cols], dalt[:, cols], ALU.add))

            def gated(q, c):
                dve.wait_ge(sem("fg_done"), q * 2 + (c + 1))
                dve.wait_ge(sem("fy_psum"), 1 + q)
                dve.tensor_tensor(fh[c], bank[3 - 2 * c][:, :], fg[c], ALU.mult).then_inc(sem("fh_done"), 1)

            def add_expert(q, e):
                dve.wait_ge(sem("ey_psum"), 1 + (q * E1 + (e + 1)))
                dve.wait_ge(sem("y_added"), 1 + ((q * E1 + e) * QT))
                for j in range(QT):
                    xt = x_all[:, at(q * QT + j)]
                    g = (q * QT + j) * E1 + e
                    dve.scalar_tensor_tensor(out=xt, in0=bank[4 if e % 2 else 7][:, j * P:(j + 1) * P],
                                             scalar=dgat[:, g:g + 1] if isinstance(q, int) else dgat[:, bass.ds(g, 1)],
                                             in1=xt, op0=ALU.mult, op1=ALU.add).then_inc(sem("y_added"), 1)

            def add_quad(q, more):
                dve.wait_ge(sem("fy_psum"), 1 + (q + 1))
                xq = x_all[:, at(q, QT * P)]
                dve.tensor_tensor(xq, bank[2][:, :], xq, ALU.add).then_inc(sem("fx_done"), 1)
                dve.wait_ge(sem("fx_done"), 1 + (q + 1))
                for e in range(E1 - 1):
                    add_expert(q, e)
                    if more:
                        gates(q + 1, e)
                if more:
                    gated(q + 1, 0)
                    gated(q + 1, 1)
                add_expert(q, E1 - 1)
            link(dve.memset(selx, BIG))
            link(dve.memset(s8x, BIG))
            dve.wait_ge(sem("dsc_done"), 1)
            gates(0, 0)
            gates(0, 1)
            gates(0, 2)
            gated(0, 0)
            gates(0, 3)
            gated(0, 1)
            for part in (4, 5, 6):
                gates(0, part)
            with dve.Fori(0, NQ - 1) as q:
                add_quad(q, True)
            add_quad(NQ - 1, False)


_INS = ['x', 'ctx_1024', 'g_xattn', 'g_ffn', 'L0_xattn_w_sim', 'L0_xattn_b_sim', 'L0_xattn_W_qv', 'L0_xattn_b_qv',
        'L0_ffn_gate_weight', 'L0_ffn_e_bias', 'L0_ffn_w1', 'L0_ffn_w2', 'L0_ffn_w3', 'L0_ffn_shared_gate',
        'L0_ffn_shared_up', 'L0_ffn_shared_down', 'L1_xattn_Wq', 'L1_xattn_bq', 'L1_xattn_Wk', 'L1_xattn_bk',
        'L1_xattn_Wv', 'L1_xattn_bv', 'L1_xattn_Wo', 'L1_xattn_bo', 'L1_ffn_router_w', 'L1_ffn_router_bias',
        'L1_ffn_sw1', 'L1_ffn_sw3', 'L1_ffn_sw2', 'L1_ffn_ew1', 'L1_ffn_ew2']


def kernel(**inputs):
    import numpy as _np
    import concourse.bacc as _bacc
    from concourse import mybir as _mybir
    from concourse.bass_utils import run_bass_kernel_spmd as _run

    nc = _bacc.Bacc("TRN2", target_bir_lowering=False, num_devices=1)
    arrays, aps = {}, {}
    for name in _INS:
        a = _np.ascontiguousarray(inputs[name])
        arrays[f"in_{name}"] = a
        aps[name] = nc.dram_tensor(f"in_{name}", a.shape, _mybir.dt.from_np(a.dtype), kind="ExternalInput").ap()
    out = nc.dram_tensor("out_0", (NT, P, P), _mybir.dt.float32, kind="ExternalOutput").ap()
    build(nc, aps, out)
    r = _run(nc, [arrays], core_ids=[0])
    return r.results[0]["out_0"]
```
